# Optimizing a Trainium2 kernel written in Bass

```python
import numpy as np
import jax
import jax.numpy as jnp

def _softmax(x, axis=-1):
    return jax.nn.softmax(x, axis=axis)

def _gelu(x):
    return jax.nn.gelu(x, approximate=True)

def _silu(x):
    return jax.nn.silu(x)

def _sigmoid(x):
    return jax.nn.sigmoid(x)

def _layernorm(x, axis=-1, eps=1e-05):
    m = jnp.mean(x, axis=axis, keepdims=True)
    v = jnp.var(x, axis=axis, keepdims=True)
    return (x - m) / jnp.sqrt(v + eps)

def _scatter_add(tgt, idx, src, axis=0):
    return tgt.at[idx].add(src)

def _segment_sum(src, seg, n):
    return jax.ops.segment_sum(src, seg, n)
kernel_name = 'mk_prb_d4_jaxref_r8_535726'

def setup_inputs(seed: int=0):
    np.random.seed(seed)
    _w = jnp.asarray

    def _L0_attn_setup():
        import jax, jax.numpy as jnp
        import numpy as np
        D_MODEL = 256
        N_HEADS = 16
        HEAD_DIM = D_MODEL // N_HEADS
        BATCH = 2
        SEQ = 256

        def apply_rope(x):
            b, h, t, d = x.shape
            half = d // 2
            pos = jnp.arange(t, dtype=x.dtype)[:, None]
            inv_freq = 1.0 / 10000.0 ** (jnp.arange(half, dtype=x.dtype) / half)
            angles = pos * inv_freq[None, :]
            sin = jnp.sin(angles)[None, None]
            cos = jnp.cos(angles)[None, None]
            x1, x2 = (x[..., :half], x[..., half:])
            return jnp.concatenate([x1 * cos - x2 * sin, x1 * sin + x2 * cos], axis=-1)
        key = jax.random.key(seed)
        ks = jax.random.split(key, 5)
        scale = 1.0 / np.sqrt(D_MODEL)
        x = jax.random.normal(ks[0], (BATCH, SEQ, D_MODEL), dtype=jnp.float32)
        Wq = jax.random.normal(ks[1], (D_MODEL, D_MODEL), dtype=jnp.float32) * scale
        Wk = jax.random.normal(ks[2], (D_MODEL, D_MODEL), dtype=jnp.float32) * scale
        Wv = jax.random.normal(ks[3], (D_MODEL, D_MODEL), dtype=jnp.float32) * scale
        Wo = jax.random.normal(ks[4], (D_MODEL, D_MODEL), dtype=jnp.float32) * scale
        return {'x': x, 'Wq': Wq, 'Wk': Wk, 'Wv': Wv, 'Wo': Wo}
    _L0_attn_in = _L0_attn_setup()

    def _L0_ffn_setup():
        import jax, jax.numpy as jnp
        import numpy as np
        HIDDEN = 256
        INTER = 1024
        BATCH, LOCAL_SEQ = (2, 512)
        key = jax.random.key(seed)
        k1, k2, k3 = jax.random.split(key, 3)
        h_shard = jax.random.normal(k1, (BATCH, LOCAL_SEQ, HIDDEN), dtype=jnp.float32)
        w_gate_up = jax.random.normal(k2, (2 * INTER, HIDDEN), dtype=jnp.float32) * 0.02
        w_down = jax.random.normal(k3, (HIDDEN, INTER), dtype=jnp.float32) * 0.02
        return {'h_shard': h_shard, 'w_gate_up': w_gate_up, 'w_down': w_down}
    _L0_ffn_in = _L0_ffn_setup()

    def _L1_attn_setup():
        import jax, jax.numpy as jnp
        import numpy as np
        B, S, HID = (1, 256, 256)
        H, HKV, D = (16, 4, 128)
        BS, NSEL = (64, 16)
        THETA = 10000.0

        def _rope(x, cos, sin):
            c = cos[None, :, None, :]
            s_ = sin[None, :, None, :]
            x1, x2 = jnp.split(x, 2, axis=-1)
            return x * c + jnp.concatenate([-x2, x1], axis=-1) * s_
        key = jax.random.key(seed)
        ks = jax.random.split(key, 8)
        w = lambda k, shape, fan: jax.random.normal(k, shape, jnp.float32) * fan ** (-0.5)
        return {'hidden_states': jax.random.normal(ks[0], (B, S, HID), jnp.float32), 'Wq': w(ks[1], (H * D, HID), HID), 'Wk': w(ks[2], (HKV * D, HID), HID), 'Wv': w(ks[3], (HKV * D, HID), HID), 'Wo': w(ks[4], (HID, H * D), H * D), 'Wkc': w(ks[5], (D // 4, D), D), 'Wgslc': w(ks[6], (H, HID), HID), 'Wgswa': w(ks[7], (H, HID), HID)}
    _L1_attn_in = _L1_attn_setup()

    def _L1_ffn_setup():
        import jax, jax.numpy as jnp
        import numpy as np
        DIM_IN = 256
        DIM_HIDDEN = 1024
        key = jax.random.key(seed)
        k_x, k_g, k_u, k_d = jax.random.split(key, 4)
        s_in = 1.0 / np.sqrt(DIM_IN)
        s_hid = 1.0 / np.sqrt(DIM_HIDDEN)
        x = jax.random.normal(k_x, (4, 256, DIM_IN), dtype=jnp.float32)
        w_gate = jax.random.uniform(k_g, (DIM_HIDDEN, DIM_IN), jnp.float32, -s_in, s_in)
        w_up = jax.random.uniform(k_u, (DIM_HIDDEN, DIM_IN), jnp.float32, -s_in, s_in)
        w_down = jax.random.uniform(k_d, (DIM_IN, DIM_HIDDEN), jnp.float32, -s_hid, s_hid)
        return {'x': x, 'w_gate': w_gate, 'w_up': w_up, 'w_down': w_down}
    _L1_ffn_in = _L1_ffn_setup()

    def _L2_attn_setup():
        import jax, jax.numpy as jnp
        from jax import lax
        import numpy as np
        B, L, D_MODEL = (1, 128, 256)
        H, P, G, S = (32, 64, 8, 32)
        D_SSM = H * P
        CONV_DIM = D_SSM + 2 * G * S
        PROJ_DIM = 2 * D_SSM + 2 * G * S + H
        K = 4
        EPS = 1e-05

        def _forward(hidden_states, W_in, b_in, conv_w, conv_b, A_log, D_param, dt_bias, norm_w, W_out, b_out, mup_vector):
            Bb, Ll, _ = hidden_states.shape
            zxbcdt = (hidden_states @ W_in + b_in) * mup_vector
            z = zxbcdt[..., :D_SSM]
            xBC = zxbcdt[..., D_SSM:D_SSM + CONV_DIM]
            dt = zxbcdt[..., D_SSM + CONV_DIM:]
            xBC_t = jnp.transpose(xBC, (0, 2, 1))
            conv = lax.conv_general_dilated(xBC_t, conv_w[:, None, :], (1,), [(K - 1, 0)], dimension_numbers=('NCH', 'OIH', 'NCH'), feature_group_count=CONV_DIM)
            xBC = jnp.transpose(jax.nn.silu(conv + conv_b[None, :, None]), (0, 2, 1))
            x = xBC[..., :D_SSM].reshape(Bb, Ll, H, P)
            Bm = xBC[..., D_SSM:D_SSM + G * S].reshape(Bb, Ll, G, S)
            Cm = xBC[..., D_SSM + G * S:].reshape(Bb, Ll, G, S)
            rep = H // G
            Bh = jnp.repeat(Bm, rep, axis=2)
            Ch = jnp.repeat(Cm, rep, axis=2)
            dt = jax.nn.softplus(dt + dt_bias)
            a = jnp.exp(dt * -jnp.exp(A_log))
            db = dt[..., None, None] * x[..., None] * Bh[:, :, :, None, :]

            def combine(e1, e2):
                a1, s1 = e1
                a2, s2 = e2
                return (a1 * a2, a2[..., None, None] * s1 + s2)
            states = lax.associative_scan(combine, (a, db), axis=1)[1]
            y = jnp.einsum('blhps,blhs->blhp', states, Ch) + D_param[None, None, :, None] * x
            y = y.reshape(Bb, Ll, D_SSM) * jax.nn.silu(z)
            yg = y.reshape(Bb, Ll, G, D_SSM // G)
            var = jnp.mean(yg * yg, axis=-1, keepdims=True)
            y = (yg * lax.rsqrt(var + EPS)).reshape(Bb, Ll, D_SSM) * norm_w
            return y @ W_out + b_out
        key = jax.random.key(seed)
        ks = jax.random.split(key, 12)
        mults = np.array([0.9, 1.1, 0.8, 1.2, 1.0], dtype=np.float32)
        mv = np.ones(PROJ_DIM, dtype=np.float32)
        mv[:D_SSM] *= mults[0]
        mv[D_SSM:2 * D_SSM] *= mults[1]
        mv[2 * D_SSM:2 * D_SSM + G * S] *= mults[2]
        mv[2 * D_SSM + G * S:2 * D_SSM + 2 * G * S] *= mults[3]
        mv[2 * D_SSM + 2 * G * S:] *= mults[4]
        return {'hidden_states': jax.random.normal(ks[0], (B, L, D_MODEL), jnp.float32), 'W_in': jax.random.normal(ks[1], (D_MODEL, PROJ_DIM), jnp.float32) * 0.02, 'b_in': jax.random.normal(ks[2], (PROJ_DIM,), jnp.float32) * 0.01, 'conv_w': jax.random.normal(ks[3], (CONV_DIM, K), jnp.float32) * 0.2, 'conv_b': jax.random.normal(ks[4], (CONV_DIM,), jnp.float32) * 0.01, 'A_log': jnp.log(jax.random.uniform(ks[5], (H,), jnp.float32, 1.0, 16.0)), 'D_param': jax.random.normal(ks[6], (H,), jnp.float32) * 0.5 + 1.0, 'dt_bias': jax.random.normal(ks[7], (H,), jnp.float32) * 0.5, 'norm_w': jnp.ones((D_SSM,), jnp.float32) + 0.01 * jax.random.normal(ks[8], (D_SSM,), jnp.float32), 'W_out': jax.random.normal(ks[9], (D_SSM, D_MODEL), jnp.float32) * 0.02, 'b_out': jnp.zeros((D_MODEL,), jnp.float32), 'mup_vector': jnp.asarray(mv)}
    _L2_attn_in = _L2_attn_setup()

    def _L2_ffn_setup():
        import jax, jax.numpy as jnp
        import numpy as np
        EPS = 1e-08

        def _quantize(w):
            gamma = jnp.mean(jnp.abs(w))
            return jnp.clip(jnp.round(w / (gamma + EPS)), -1.0, 1.0)

        def _bitlinear(x, w):
            return jnp.matmul(x, _quantize(w).T)
        key = jax.random.key(seed)
        k1, k2, k3, k4 = jax.random.split(key, 4)
        d, h = (256, 704)
        x = jax.random.normal(k1, (4, 256, d), dtype=jnp.float32)
        w1 = jax.random.normal(k2, (h, d), dtype=jnp.float32)
        w2 = jax.random.normal(k3, (h, d), dtype=jnp.float32)
        w3 = jax.random.normal(k4, (d, h), dtype=jnp.float32)
        return {'x': x, 'w1': w1, 'w2': w2, 'w3': w3}
    _L2_ffn_in = _L2_ffn_setup()

    def _L3_attn_setup():
        import jax, jax.numpy as jnp
        import numpy as np
        H = 256
        Q_RANK = 32
        SCALE = float(np.sqrt(Q_RANK))
        key = jax.random.key(seed)
        k_x, k_s, k_a, k_o, k_b = jax.random.split(key, 5)
        B, L = (4, 512)
        x = jax.random.normal(k_x, (B, L, H), dtype=jnp.float32)
        Ws = jax.random.normal(k_s, (H, Q_RANK), dtype=jnp.float32) / np.sqrt(H)
        Wa = jax.random.normal(k_a, (H, Q_RANK), dtype=jnp.float32) / np.sqrt(H)
        Wo = jax.random.normal(k_o, (H, H), dtype=jnp.float32) / np.sqrt(H)
        bo = jax.random.normal(k_b, (H,), dtype=jnp.float32) * 0.01
        return {'x': x, 'Ws': Ws, 'Wa': Wa, 'Wo': Wo, 'bo': bo}
    _L3_attn_in = _L3_attn_setup()

    def _L3_ffn_setup():
        import jax, jax.numpy as jnp
        import numpy as np
        NUM_EXPERTS = 16
        TOP_K = 2
        HIDDEN = 256
        D_FF = 512
        BATCH, SEQ = (4, 256)

        def _moe_forward(hidden, router_w, W1, W2):
            B, S, D = hidden.shape
            x = hidden.reshape(-1, D)
            T = x.shape[0]
            logits = x @ router_w
            top_vals, top_ids = jax.lax.top_k(logits, TOP_K)
            probs = jax.nn.softmax(top_vals, axis=-1)
            combine = jnp.zeros((T, NUM_EXPERTS), dtype=x.dtype)
            combine = combine.at[jnp.arange(T)[:, None], top_ids].add(probs)
            out = jnp.zeros_like(x)
            for e in range(NUM_EXPERTS):
                h = jax.nn.silu(x @ W1[e]) @ W2[e]
                out = out + combine[:, e:e + 1] * h
            return out.reshape(B, S, D)
        key = jax.random.key(seed)
        k_h, k_r, k_w1, k_w2 = jax.random.split(key, 4)
        hidden = jax.random.normal(k_h, (BATCH, SEQ, HIDDEN), dtype=jnp.float32)
        router_w = jax.random.normal(k_r, (HIDDEN, NUM_EXPERTS), dtype=jnp.float32) * HIDDEN ** (-0.5)
        W1 = jax.random.normal(k_w1, (NUM_EXPERTS, HIDDEN, D_FF), dtype=jnp.float32) * HIDDEN ** (-0.5)
        W2 = jax.random.normal(k_w2, (NUM_EXPERTS, D_FF, HIDDEN), dtype=jnp.float32) * D_FF ** (-0.5)
        return {'hidden': hidden, 'router_w': router_w, 'W1': W1, 'W2': W2}
    _L3_ffn_in = _L3_ffn_setup()
    _d = {'L0_attn_x': _L0_attn_in['x'], 'L0_attn_Wq': _L0_attn_in['Wq'], 'L0_attn_Wk': _L0_attn_in['Wk'], 'L0_attn_Wv': _L0_attn_in['Wv'], 'L0_attn_Wo': _L0_attn_in['Wo'], 'L0_ffn_w_gate_up': _L0_ffn_in['w_gate_up'], 'L0_ffn_w_down': _L0_ffn_in['w_down'], 'L1_attn_Wq': _L1_attn_in['Wq'], 'L1_attn_Wk': _L1_attn_in['Wk'], 'L1_attn_Wv': _L1_attn_in['Wv'], 'L1_attn_Wo': _L1_attn_in['Wo'], 'L1_attn_Wkc': _L1_attn_in['Wkc'], 'L1_attn_Wgslc': _L1_attn_in['Wgslc'], 'L1_attn_Wgswa': _L1_attn_in['Wgswa'], 'L1_ffn_w_gate': _L1_ffn_in['w_gate'], 'L1_ffn_w_up': _L1_ffn_in['w_up'], 'L1_ffn_w_down': _L1_ffn_in['w_down'], 'L2_attn_W_in': _L2_attn_in['W_in'], 'L2_attn_b_in': _L2_attn_in['b_in'], 'L2_attn_conv_w': _L2_attn_in['conv_w'], 'L2_attn_conv_b': _L2_attn_in['conv_b'], 'L2_attn_A_log': _L2_attn_in['A_log'], 'L2_attn_D_param': _L2_attn_in['D_param'], 'L2_attn_dt_bias': _L2_attn_in['dt_bias'], 'L2_attn_norm_w': _L2_attn_in['norm_w'], 'L2_attn_W_out': _L2_attn_in['W_out'], 'L2_attn_b_out': _L2_attn_in['b_out'], 'L2_attn_mup_vector': _L2_attn_in['mup_vector'], 'L2_ffn_w1': _L2_ffn_in['w1'], 'L2_ffn_w2': _L2_ffn_in['w2'], 'L2_ffn_w3': _L2_ffn_in['w3'], 'L3_attn_Ws': _L3_attn_in['Ws'], 'L3_attn_Wa': _L3_attn_in['Wa'], 'L3_attn_Wo': _L3_attn_in['Wo'], 'L3_attn_bo': _L3_attn_in['bo'], 'L3_ffn_router_w': _L3_ffn_in['router_w'], 'L3_ffn_W1': _L3_ffn_in['W1'], 'L3_ffn_W2': _L3_ffn_in['W2']}
    _x0 = _d['L0_attn_x']
    _d['L0_attn_x'] = jax.random.normal(jax.random.fold_in(jax.random.key(seed), 1), (2, 1024, 256), dtype=_x0.dtype)
    del _x0
    return _d

def reference(L0_attn_x, L0_attn_Wq, L0_attn_Wk, L0_attn_Wv, L0_attn_Wo, L0_ffn_w_gate_up, L0_ffn_w_down, L1_attn_Wq, L1_attn_Wk, L1_attn_Wv, L1_attn_Wo, L1_attn_Wkc, L1_attn_Wgslc, L1_attn_Wgswa, L1_ffn_w_gate, L1_ffn_w_up, L1_ffn_w_down, L2_attn_W_in, L2_attn_b_in, L2_attn_conv_w, L2_attn_conv_b, L2_attn_A_log, L2_attn_D_param, L2_attn_dt_bias, L2_attn_norm_w, L2_attn_W_out, L2_attn_b_out, L2_attn_mup_vector, L2_ffn_w1, L2_ffn_w2, L2_ffn_w3, L3_attn_Ws, L3_attn_Wa, L3_attn_Wo, L3_attn_bo, L3_ffn_router_w, L3_ffn_W1, L3_ffn_W2):

    def _L0_attn_ref(x, Wq, Wk, Wv, Wo):
        import jax, jax.numpy as jnp
        import numpy as np
        D_MODEL = 256
        N_HEADS = 16
        HEAD_DIM = D_MODEL // N_HEADS
        BATCH = 2
        SEQ = 256

        def apply_rope(x):
            b, h, t, d = x.shape
            half = d // 2
            pos = jnp.arange(t, dtype=x.dtype)[:, None]
            inv_freq = 1.0 / 10000.0 ** (jnp.arange(half, dtype=x.dtype) / half)
            angles = pos * inv_freq[None, :]
            sin = jnp.sin(angles)[None, None]
            cos = jnp.cos(angles)[None, None]
            x1, x2 = (x[..., :half], x[..., half:])
            return jnp.concatenate([x1 * cos - x2 * sin, x1 * sin + x2 * cos], axis=-1)
        b, t, _ = x.shape

        def proj(W):
            y = jnp.einsum('btd,ed->bte', x, W)
            return y.reshape(b, t, N_HEADS, HEAD_DIM).transpose(0, 2, 1, 3)
        q = apply_rope(proj(Wq))
        k = apply_rope(proj(Wk))
        v = proj(Wv)
        scores = jnp.einsum('bhqd,bhkd->bhqk', q, k) / np.sqrt(HEAD_DIM)
        causal = jnp.tril(jnp.ones((t, t), dtype=bool))
        scores = jnp.where(causal[None, None], scores, -jnp.inf)
        attn = jax.nn.softmax(scores, axis=-1)
        out = jnp.einsum('bhqk,bhkd->bhqd', attn, v)
        out = out.transpose(0, 2, 1, 3).reshape(b, t, D_MODEL)
        return jnp.einsum('btd,ed->bte', out, Wo)

    def _L0_ffn_ref(h_shard, w_gate_up, w_down):
        import jax, jax.numpy as jnp
        import numpy as np
        HIDDEN = 256
        INTER = 1024
        BATCH, LOCAL_SEQ = (2, 512)
        batch, local_seq, hidden = h_shard.shape
        gate_up = jnp.einsum('bsh,oh->bso', h_shard, w_gate_up)
        gate, up = jnp.split(gate_up, 2, axis=-1)
        h = jax.nn.silu(gate) * up
        out = jnp.einsum('bsi,hi->bsh', h, w_down)
        return out

    def _L1_attn_ref(hidden_states, Wq, Wk, Wv, Wo, Wkc, Wgslc, Wgswa):
        import jax, jax.numpy as jnp
        import numpy as np
        B, S, HID = (1, 256, 256)
        H, HKV, D = (16, 4, 128)
        BS, NSEL = (64, 16)
        THETA = 10000.0

        def _rope(x, cos, sin):
            c = cos[None, :, None, :]
            s_ = sin[None, :, None, :]
            x1, x2 = jnp.split(x, 2, axis=-1)
            return x * c + jnp.concatenate([-x2, x1], axis=-1) * s_
        b, sl, _ = hidden_states.shape
        g_slc = jax.nn.sigmoid(hidden_states @ Wgslc.T)
        g_swa = jax.nn.sigmoid(hidden_states @ Wgswa.T)
        q = (hidden_states @ Wq.T).reshape(b, sl, H, D)
        k = (hidden_states @ Wk.T).reshape(b, sl, HKV, D)
        v = (hidden_states @ Wv.T).reshape(b, sl, HKV, D)
        inv_freq = 1.0 / THETA ** (jnp.arange(0, D, 2, dtype=jnp.float32) / D)
        t = jnp.arange(sl, dtype=jnp.float32)
        freqs = jnp.outer(t, inv_freq)
        emb = jnp.concatenate([freqs, freqs], axis=-1)
        cos, sin = (jnp.cos(emb), jnp.sin(emb))
        q = _rope(q, cos, sin)
        k = _rope(k, cos, sin)
        q = q.transpose(0, 2, 1, 3)
        k = jnp.repeat(k.transpose(0, 2, 1, 3), H // HKV, axis=1)
        v = jnp.repeat(v.transpose(0, 2, 1, 3), H // HKV, axis=1)
        nb = (sl + BS - 1) // BS
        kc = k @ Wkc.T
        pad = nb * BS - sl
        kc = jnp.pad(kc, ((0, 0), (0, 0), (0, pad), (0, 0)))
        kbm = kc.reshape(b, H, nb, BS, D // 4).mean(axis=3)
        qc = q @ Wkc.T
        bscores = jnp.einsum('bhsd,bhnd->bhsn', qc, kbm) / jnp.sqrt(jnp.float32(D // 4))
        pos_blk = jnp.arange(sl) // BS
        cmask = jnp.arange(nb)[None, :] <= pos_blk[:, None]
        bscores = jnp.where(cmask[None, None], bscores, -jnp.inf)
        topk = min(NSEL, nb)
        _, idx = jax.lax.top_k(bscores, topk)
        block_indices = jnp.sort(idx, axis=-1)
        scale = 1.0 / jnp.sqrt(jnp.float32(D))
        scores = jnp.einsum('bhsd,bhtd->bhst', q, k) * scale
        causal = jnp.tril(jnp.ones((sl, sl), bool))
        scores = jnp.where(causal[None, None], scores, -jnp.inf)
        attn = jnp.einsum('bhst,bhtd->bhsd', jax.nn.softmax(scores, axis=-1), v)
        g = (g_slc + g_swa).transpose(0, 2, 1)[..., None]
        out = (g * attn).transpose(0, 2, 1, 3).reshape(b, sl, H * D)
        return out @ Wo.T

    def _L1_ffn_ref(x, w_gate, w_up, w_down):
        import jax, jax.numpy as jnp
        import numpy as np
        DIM_IN = 256
        DIM_HIDDEN = 1024
        gate = jnp.einsum('bsd,hd->bsh', x, w_gate)
        up = jnp.einsum('bsd,hd->bsh', x, w_up)
        gated = jax.nn.silu(gate) * up
        return jnp.einsum('bsh,dh->bsd', gated, w_down)

    def _L2_attn_ref(hidden_states, W_in, b_in, conv_w, conv_b, A_log, D_param, dt_bias, norm_w, W_out, b_out, mup_vector):
        import jax, jax.numpy as jnp
        from jax import lax
        import numpy as np
        B, L, D_MODEL = (1, 128, 256)
        H, P, G, S = (32, 64, 8, 32)
        D_SSM = H * P
        CONV_DIM = D_SSM + 2 * G * S
        PROJ_DIM = 2 * D_SSM + 2 * G * S + H
        K = 4
        EPS = 1e-05

        def _forward(hidden_states, W_in, b_in, conv_w, conv_b, A_log, D_param, dt_bias, norm_w, W_out, b_out, mup_vector):
            Bb, Ll, _ = hidden_states.shape
            zxbcdt = (hidden_states @ W_in + b_in) * mup_vector
            z = zxbcdt[..., :D_SSM]
            xBC = zxbcdt[..., D_SSM:D_SSM + CONV_DIM]
            dt = zxbcdt[..., D_SSM + CONV_DIM:]
            xBC_t = jnp.transpose(xBC, (0, 2, 1))
            conv = lax.conv_general_dilated(xBC_t, conv_w[:, None, :], (1,), [(K - 1, 0)], dimension_numbers=('NCH', 'OIH', 'NCH'), feature_group_count=CONV_DIM)
            xBC = jnp.transpose(jax.nn.silu(conv + conv_b[None, :, None]), (0, 2, 1))
            x = xBC[..., :D_SSM].reshape(Bb, Ll, H, P)
            Bm = xBC[..., D_SSM:D_SSM + G * S].reshape(Bb, Ll, G, S)
            Cm = xBC[..., D_SSM + G * S:].reshape(Bb, Ll, G, S)
            rep = H // G
            Bh = jnp.repeat(Bm, rep, axis=2)
            Ch = jnp.repeat(Cm, rep, axis=2)
            dt = jax.nn.softplus(dt + dt_bias)
            a = jnp.exp(dt * -jnp.exp(A_log))
            db = dt[..., None, None] * x[..., None] * Bh[:, :, :, None, :]

            def combine(e1, e2):
                a1, s1 = e1
                a2, s2 = e2
                return (a1 * a2, a2[..., None, None] * s1 + s2)
            states = lax.associative_scan(combine, (a, db), axis=1)[1]
            y = jnp.einsum('blhps,blhs->blhp', states, Ch) + D_param[None, None, :, None] * x
            y = y.reshape(Bb, Ll, D_SSM) * jax.nn.silu(z)
            yg = y.reshape(Bb, Ll, G, D_SSM // G)
            var = jnp.mean(yg * yg, axis=-1, keepdims=True)
            y = (yg * lax.rsqrt(var + EPS)).reshape(Bb, Ll, D_SSM) * norm_w
            return y @ W_out + b_out
        return _forward(hidden_states, W_in, b_in, conv_w, conv_b, A_log, D_param, dt_bias, norm_w, W_out, b_out, mup_vector)

    def _L2_ffn_ref(x, w1, w2, w3):
        import jax, jax.numpy as jnp
        import numpy as np
        EPS = 1e-08

        def _quantize(w):
            gamma = jnp.mean(jnp.abs(w))
            return jnp.clip(jnp.round(w / (gamma + EPS)), -1.0, 1.0)

        def _bitlinear(x, w):
            return jnp.matmul(x, _quantize(w).T)
        x1 = _bitlinear(x, w1)
        x2 = _bitlinear(x, w2)
        hidden = jax.nn.sigmoid(x1) * x2
        return _bitlinear(hidden, w3)

    def _L3_attn_ref(x, Ws, Wa, Wo, bo):
        import jax, jax.numpy as jnp
        import numpy as np
        H = 256
        Q_RANK = 32
        SCALE = float(np.sqrt(Q_RANK))
        B, L, _ = x.shape
        state = jnp.einsum('blh,hr->blr', x, Ws)
        action = jnp.einsum('blh,hr->blr', x, Wa)
        q_values = jnp.einsum('bir,bjr->bij', state, action) / SCALE
        causal = jnp.tril(jnp.ones((L, L), dtype=bool))
        q_values = jnp.where(causal, q_values, -jnp.inf)
        weights = jax.nn.softmax(q_values, axis=-1)
        out = jnp.einsum('bij,bjh->bih', weights, x)
        return jnp.einsum('bih,ho->bio', out, Wo.T) + bo

    def _L3_ffn_ref(hidden, router_w, W1, W2):
        import jax, jax.numpy as jnp
        import numpy as np
        NUM_EXPERTS = 16
        TOP_K = 2
        HIDDEN = 256
        D_FF = 512
        BATCH, SEQ = (4, 256)

        def _moe_forward(hidden, router_w, W1, W2):
            B, S, D = hidden.shape
            x = hidden.reshape(-1, D)
            T = x.shape[0]
            logits = x @ router_w
            top_vals, top_ids = jax.lax.top_k(logits, TOP_K)
            probs = jax.nn.softmax(top_vals, axis=-1)
            combine = jnp.zeros((T, NUM_EXPERTS), dtype=x.dtype)
            combine = combine.at[jnp.arange(T)[:, None], top_ids].add(probs)
            out = jnp.zeros_like(x)
            for e in range(NUM_EXPERTS):
                h = jax.nn.silu(x @ W1[e]) @ W2[e]
                out = out + combine[:, e:e + 1] * h
            return out.reshape(B, S, D)
        return _moe_forward(hidden, router_w, W1, W2)
    x = L0_attn_x
    xn = _layernorm(x, axis=-1)
    x = x + _L0_attn_ref(xn, L0_attn_Wq, L0_attn_Wk, L0_attn_Wv, L0_attn_Wo) + _L0_ffn_ref(xn, L0_ffn_w_gate_up, L0_ffn_w_down)
    xn = _layernorm(x, axis=-1)
    x = x + _L1_attn_ref(xn, L1_attn_Wq, L1_attn_Wk, L1_attn_Wv, L1_attn_Wo, L1_attn_Wkc, L1_attn_Wgslc, L1_attn_Wgswa) + _L1_ffn_ref(xn, L1_ffn_w_gate, L1_ffn_w_up, L1_ffn_w_down)
    xn = _layernorm(x, axis=-1)
    x = x + _L2_attn_ref(xn, L2_attn_W_in, L2_attn_b_in, L2_attn_conv_w, L2_attn_conv_b, L2_attn_A_log, L2_attn_D_param, L2_attn_dt_bias, L2_attn_norm_w, L2_attn_W_out, L2_attn_b_out, L2_attn_mup_vector) + _L2_ffn_ref(xn, L2_ffn_w1, L2_ffn_w2, L2_ffn_w3)
    xn = _layernorm(x, axis=-1)
    x = x + _L3_attn_ref(xn, L3_attn_Ws, L3_attn_Wa, L3_attn_Wo, L3_attn_bo) + _L3_ffn_ref(xn, L3_ffn_router_w, L3_ffn_W1, L3_ffn_W2)
    return x

_drawn_inputs = setup_inputs


def setup_inputs(seed=0):
    import zlib

    import numpy as np

    out = dict(_drawn_inputs(seed))
    spreads = {'L2_attn_b_out': (0.0, 0.8)}
    factors = {'L2_attn_W_in': 8.0,
     'L2_attn_b_in': 8.0,
     'L2_attn_conv_w': 8.0,
     'L2_attn_conv_b': 8.0,
     'L2_attn_A_log': 8.0,
     'L2_attn_D_param': 8.0,
     'L2_attn_dt_bias': 8.0,
     'L2_attn_norm_w': 8.0,
     'L2_attn_W_out': 8.0,
     'L2_attn_mup_vector': 8.0,
     'L3_attn_Ws': 8.0,
     'L3_attn_Wa': 8.0,
     'L3_attn_Wo': 8.0,
     'L3_attn_bo': 8.0,
     'L3_ffn_router_w': 8.0,
     'L3_ffn_W1': 8.0,
     'L3_ffn_W2': 8.0}
    for name, (base, spread) in spreads.items():
        noise = np.random.default_rng([zlib.crc32(name.encode()), seed]).standard_normal(out[name].shape)
        drawn = base * np.exp(spread * noise) if base else spread * noise
        out[name] = jnp.asarray(drawn.astype(out[name].dtype))
    for name, factor in factors.items():
        out[name] = (out[name] * factor).astype(out[name].dtype)
    return out
```

```python
import numpy as np
from contextlib import ExitStack
import concourse.bass as bass
from concourse import mybir

F32 = mybir.dt.float32
U32 = mybir.dt.uint32
ALU = mybir.AluOpType
ACT = mybir.ActivationFunctionType
AX = mybir.AxisListType

T = 2048
NT = 16
D = 256
NEG = -1.0e30

X0, XNT0, CONST0, WA0, WF0, WK0, EX0, END = 0, 4096, 8192, 9216, 22528, 28672, 52000, 53200


class Lane:

    def __init__(self, name, sem):
        self.name, self.sem, self.count, self.seen, self.queue = name, sem, 0, {}, []

    def wait(self, tokens):
        for sem, value in tokens:
            if value > self.seen.get(id(sem), 0):
                self.seen[id(sem)] = value
                self.queue.append(lambda e, s=sem, v=value: e.wait_ge(s, v))

    def __call__(self, f, *tokens, mark=True):
        self.wait(flat(tokens))
        if not mark:
            self.queue.append(f)
            return None
        self.count += 1
        self.queue.append(lambda e, s=self.sem: f(e).then_inc(s, 1))
        return (self.sem, self.count)

    def last(self):
        return (self.sem, self.count)


def flat(tokens):
    for t in tokens:
        if t is None:
            continue
        if isinstance(t, list):
            yield from flat(t)
        else:
            yield t


class Ring:

    def __init__(self, bufs):
        self.bufs, self.free, self.at = bufs, [[] for _ in bufs], -1

    def take(self):
        self.at = (self.at + 1) % len(self.bufs)
        return self.at, self.bufs[self.at], self.free[self.at]

    def done(self, i, *tokens):
        self.free[i] = list(flat(tokens))


class K:
    def __init__(self, nc, ctx, ins, outs):
        self.nc, self.ins, self.outs = nc, ins, outs
        self.A = ctx.enter_context(nc.sbuf_tensor("arena", [128, END], F32))
        self.PS = ctx.enter_context(nc.psum_tensor("ps", [128, 8, 512], F32))
        mk = lambda n: ctx.enter_context(nc.semaphore(n))
        self.pe = Lane("pe", mk("s_pe"))
        self.act = Lane("act", mk("s_act"))
        self.dve = Lane("dve", mk("s_dve"))
        self.pool = Lane("pool", mk("s_pool"))
        self.sp = Lane("sp", mk("s_sp"))
        self.mk = mk
        self.dsem = {}

    def sb(self, at, *shape):
        n = int(np.prod(shape))
        assert at + n <= END
        v = self.A[:, at:at + n]
        if len(shape) == 2:
            v = v.rearrange("p (a b) -> p a b", a=shape[0])
        elif len(shape) == 3:
            v = v.rearrange("p (a b c) -> p a b c", a=shape[0], b=shape[1])
        return v

    def dma(self, name, out, in_, *tokens, lane=None):
        if name not in self.dsem:
            self.dsem[name] = [self.mk("d_" + name), 0]
        s = self.dsem[name]
        s[1] += 16
        (lane or self.sp)(lambda e, sem=s[0]: e.dma_start(out, in_).then_inc(sem, 16), *tokens, mark=False)
        return (s[0], s[1])

    def barrier(self):
        lanes = [self.pe, self.act, self.dve, self.pool]
        marks = [l.last() for l in lanes]
        for l in lanes + [self.sp]:
            l.wait(marks)

    def consts(self):
        pool, dve = self.pool, self.dve
        self.ident = self.sb(CONST0, 128)
        self.mask = self.sb(CONST0 + 128, 128)
        self.ones = self.sb(CONST0 + 256, 128)
        self.eps = self.sb(CONST0 + 384, 1)
        self.eps8 = self.sb(CONST0 + 385, 1)
        self.zero1 = self.sb(CONST0 + 386, 1)
        self.misc = CONST0 + 400
        t0 = pool(lambda e: e.memset(self.ident, 0.0))
        t1 = pool(lambda e: e.memset(self.mask, 0.0))
        pool(lambda e: e.memset(self.ones, 1.0))
        pool(lambda e: e.memset(self.eps, 1e-5))
        pool(lambda e: e.memset(self.zero1, 0.0))
        pool(lambda e: e.affine_select(out=self.ident, in_=self.ident, compare_op=ALU.not_equal, fill=1.0,
                                       base=0, pattern=[[-1, 128]], channel_multiplier=1), t0)
        t = pool(lambda e: e.affine_select(out=self.mask, in_=self.mask, compare_op=ALU.is_ge, fill=NEG,
                                           base=0, pattern=[[-1, 128]], channel_multiplier=1), t1)
        for l in (self.pe, self.act, self.dve):
            l.wait([t])

    def norm(self, X, XNT, XN=None):
        pe, act, dve = self.pe, self.act, self.dve
        st = self.sb(WK0, 16, 6)
        mv = self.sb(WK0 + 96, 16, 2)
        sd = self.sb(WK0 + 128, 16)
        tmp = Ring([self.sb(WK0 + 256 + 256 * i, 256) for i in range(4)])
        ps = Ring([self.PS[:, i, :] for i in range(8)])
        for i in range(NT):
            t = dve(lambda e, i=i: e.bn_stats(st[:, i, :], X[:, i, :]))
            t = dve(lambda e, i=i: e.bn_aggr(mv[:, i, :], st[:, i, :]), t)
        t = act(lambda e: e.activation(sd, mv[:, :, 1], ACT.Sqrt, bias=self.eps), t)
        trs = dve(lambda e: e.reciprocal(sd, sd), t)
        tl = []
        tm = self.dve.last()
        for i0 in range(0, NT, 4):
            pend = []
            (b0, p0, f0), (b1, p1, f1) = ps.take(), ps.take()
            for i in range(i0, i0 + 4):
                if XN is None:
                    k, xn, fr = tmp.take()
                else:
                    xn, fr = XN[:, i, :], []
                t = dve(lambda e, i=i, xn=xn: e.tensor_scalar(xn, X[:, i, :], mv[:, i, 0:1], sd[:, i:i + 1],
                                                              ALU.subtract, ALU.mult), trs, tm, fr)
                for c, (p, f) in enumerate(((p0, f0), (p1, f1))):
                    t2 = pe(lambda e, p=p, xn=xn, c=c, j=i - i0: e.transpose(
                        p[:, j * 128:j * 128 + 128], xn[:, c * 128:c * 128 + 128], self.ident), t, f)
                if XN is None:
                    tmp.done(k, t2)
            a = act(lambda e, p=p0, i0=i0: e.activation(XNT[:, 0, i0 * 128:i0 * 128 + 512], p, ACT.Copy), t2)
            b = dve(lambda e, p=p1, i0=i0: e.tensor_copy(XNT[:, 1, i0 * 128:i0 * 128 + 512], p), t2)
            ps.done(b0, a)
            ps.done(b1, b)
            tl += [a, b]
        return tl

    def proj(self, ps, lhsT, rhs, n, nk, *tokens):
        for k in range(nk):
            t = self.pe(lambda e, k=k, a=lhsT(k), b=rhs(k): e.matmul(ps, a, b, start=(k == 0), stop=(k == nk - 1)),
                        *tokens, mark=(k == nk - 1))
        return t

    def project_add(self, X, first, n, ring, lhsT, rhs, nk, *tokens):
        for i in range(0, n, 2):
            pi, p, pf = ring.take()
            for j in range(2):
                t = self.proj(p[:, j * 256:j * 256 + 256], lambda k: lhsT(i + j, k), rhs, 256, nk, pf, *tokens)
            x = X[:, first + i:first + i + 2, :]
            t2 = self.dve(lambda e, p=p, x=x: e.tensor_tensor(x, x, p.rearrange("p (a b) -> p a b", a=2), ALU.add), t)
            ring.done(pi, t2)
        return t

    def ffn(self, X, XNT, nf, wg, wu, wd, rows, gate, work, tw, out_scale=None):
        pe, act, dve = self.pe, self.act, self.dve
        g_r = Ring([self.PS[:, i, :] for i in (0, 1)])
        u_r = Ring([self.PS[:, i, :] for i in (2, 3)])
        d_r = Ring([self.PS[:, i, :] for i in (4, 5, 6, 7)])
        tmp = Ring([self.sb(work + 512 * i, 512) for i in range(3)])
        H = Ring([self.sb(work + 1536 + 512 * nf * i, nf, 512) for i in range(2)])

        def up(tt):
            hi, h, hf = H.take()
            done = []
            tok = slice(tt * 512, tt * 512 + 512)
            for f in range(nf):
                r = rows(f)
                gi, g, gf = g_r.take()
                ui, u, uf = u_r.take()
                tg = self.proj(g[:r, :], lambda k: wg(k, f), lambda k: XNT[:, k, tok], 512, 2, gf, tw)
                tu = self.proj(u[:r, :], lambda k: wu(k, f), lambda k: XNT[:, k, tok], 512, 2, uf, tw)
                ti, s, sf = tmp.take()
                ta = act(lambda e, s=s, g=g, r=r: e.activation(s[:r, :], g[:r, :], gate), tg, sf)
                g_r.done(gi, ta)
                td = dve(lambda e, s=s, u=u, r=r, f=f: e.tensor_tensor(h[:r, f, :], s[:r, :], u[:r, :], ALU.mult),
                         ta, tu, hf)
                u_r.done(ui, td)
                tmp.done(ti, td)
            return tt, hi, h, td

        def down(tt, hi, h, th):
            t = self.project_add(X, tt * 4, 4, d_r, lambda i, k: h[:rows(k), k, i * 128:i * 128 + 128],
                                 lambda k: wd(k)[:rows(k), :], nf, th, tw)
            H.done(hi, t)

        prev = None
        for tt in range(4):
            cur = up(tt)
            if prev:
                down(*prev)
            prev = cur
        down(*prev)

    def attend(self, units, nh, work, score, scale, pscale, pv, rings, npt=4, after=None):
        pe, act, dve, pool = self.pe, self.act, self.dve, self.pool
        s_r, t_r = rings
        PB = [self.sb(work + nh * 1024 * i, nh, 1024) for i in range(2)]
        PTr = Ring([self.sb(work + nh * 2048 + 128 * nh * i, nh * 128) for i in range(npt)])
        small = self.misc
        pfree = [[], []]
        evac = [0]

        def scores(n, u, h):
            qt = u[-1]
            nk = 128 * (qt + 1)
            q, k, tk = score(u, h)
            si, s, sf = s_r.take()
            for c in range(0, nk, 512):
                w = min(512, nk - c)
                t = pe(lambda e, c=c, w=w: e.matmul(s[:, c:c + w], q, k(c, c + w), start=True, stop=True), sf, tk,
                       mark=(c + 512 >= nk))
            if after:
                after(u, h, t)
            t = dve(lambda e: e.tensor_tensor(s[:, nk - 128:nk], s[:, nk - 128:nk], self.mask, ALU.add), t)
            st = self.sb(small + (n % 2) * 32, 4, 8)
            t = dve(lambda e: e.tensor_reduce(st[:, 0, h:h + 1], s[:, :nk], AX.X, ALU.max, negate=True), t,
                    pfree[n % 2])
            if scale != 1.0:
                t = dve(lambda e: e.tensor_scalar(st[:, 0, h:h + 1], st[:, 0, h:h + 1], scale, None, ALU.mult), t)
            P = PB[n % 2]
            t = act(lambda e: e.activation(P[:, h, :nk], s[:, :nk], ACT.Exp, bias=st[:, 0, h:h + 1], scale=scale,
                                           accum_out=st[:, 1, h:h + 1]), t, pfree[n % 2])
            s_r.done(si, t)
            if pscale is not None:
                t = dve(lambda e: e.reciprocal(st[:, 2, h:h + 1], st[:, 1, h:h + 1]), t)
                g = pscale(u, h)
                t = dve(lambda e: e.tensor_tensor(st[:, 3, h:h + 1], st[:, 2, h:h + 1], g, ALU.mult), t)
                t = pool(lambda e: e.tensor_scalar(P[:, h, :nk], P[:, h, :nk], st[:, 3, h:h + 1], 1.0, ALU.mult,
                                                   ALU.mult), t)
            return t

        def blocks(n, u, tp):
            qt = u[-1]
            P = PB[n % 2]
            pts = {}

            def tr(j):
                ti, tp_, tf = t_r.take()
                for h in range(nh):
                    t = pe(lambda e, h=h: e.transpose(tp_[:, h * 128:h * 128 + 128], P[:, h, j * 128:j * 128 + 128],
                                                      self.ident), tp[h], tf, mark=(h == nh - 1))
                pi, PT, pf = PTr.take()
                evac[0] += 1
                w = nh * 128
                if evac[0] % 2:
                    t2 = act(lambda e: e.activation(PT, tp_[:, :w], ACT.Copy), t, pf)
                else:
                    t2 = dve(lambda e: e.tensor_copy(PT, tp_[:, :w]), t, pf)
                t_r.done(ti, t2)
                pts[j] = (pi, PT, t2)
                if j == qt:
                    pfree[n % 2] = [t]

            def mul(j):
                pi, PT, t2 = pts[j]
                t = pv(u, j, PT, t2)
                PTr.done(pi, t)

            steps = [lambda j=j: tr(j) for j in range(qt + 1)]
            out = [steps[0]]
            for j in range(qt + 1):
                if j + 1 <= qt:
                    out.append(steps[j + 1])
                out.append(lambda j=j: mul(j))
            return out

        pending = []
        for n, u in enumerate(units):
            tp = []
            for h in range(nh):
                tp.append(scores(n, u, h))
                share = -(-len(pending) // (nh - h))
                for _ in range(share):
                    pending.pop(0)()
            pending = blocks(n, u, tp)
        while pending:
            pending.pop(0)()

    def layer0(self, X, XNT):
        pe, act, dve, pool = self.pe, self.act, self.dve, self.pool
        I = self.ins
        Wq, Wa, Wb = (self.sb(WA0 + 1024 * i, 2, 512) for i in range(3))
        Wv = self.sb(WA0 + 3072, 2, 256)
        Wo = self.sb(WA0 + 4096, 4, 256)
        Tq, Tc, Ts = (self.sb(WA0 + 5120 + 1024 * i, 1024) for i in range(3))
        tmp = Ring([self.sb(WA0 + 8192 + 512 * i, 512) for i in range(2)])
        Wgu = self.sb(WF0, 2, 2048)
        Wd = self.sb(WF0 + 4096, 8, 256)
        tw = [self.dma("w_a", Wq, I["l0_wq"]), self.dma("w_a", Wa, I["l0_wa"]), self.dma("w_a", Wb, I["l0_wb"]),
              self.dma("w_a", Wv, I["l0_wv"]), self.dma("w_a", Wo, I["l0_wo"]), self.dma("w_a", Tq, I["l0_tq"]),
              self.dma("w_a", Tc, I["l0_tc"]), self.dma("w_a", Ts, I["l0_ts"])][-1:]
        tf = [self.dma("w_f", Wgu, I["l0_wgu"]), self.dma("w_f", Wd, I["l0_wd"])][-1:]
        self.norm(X, XNT)
        self.barrier()
        qk = Ring([self.sb(WK0 + 2048 * i, 2, 1024) for i in range(2)])
        V = self.sb(WK0 + 4096, 8, 16, 32)
        aT = self.sb(WK0 + 8192, 4, 1024)
        work = WK0 + 12288
        s_r = Ring([self.PS[:, 2 * i:2 * i + 2, :].rearrange("p a b -> p (a b)") for i in range(2)])
        t_r = Ring([self.PS[:, i, :] for i in (4, 5)])
        o_r = Ring([self.PS[:, i, :] for i in (6, 7)])
        nrm = Ring([self.sb(WA0 + 9216 + 256 * i, 2, 128) for i in range(2)])
        t_one = pool(lambda e: e.memset(V[:, :, :, 16:32], 1.0))
        state = {}

        def make_qk(b, ht):
            qi, QK, qf = qk.take()
            done = []
            for tt in range(2):
                tok = slice(b * 1024 + tt * 512, b * 1024 + tt * 512 + 512)
                o = slice(tt * 512, tt * 512 + 512)
                W = slice(ht * 128, ht * 128 + 128)
                si, s, sf = s_r.take()
                t = self.proj(s[:, 0:512], lambda k: Wq[:, k, W], lambda k: XNT[:, k, tok], 512, 2, sf, tw)
                t = dve(lambda e, s=s, o=o: e.tensor_tensor(QK[:, 0, o], s[:, 0:512], Tq[:, o], ALU.mult), t, qf)
                s_r.done(si, t)
                si, s, sf = s_r.take()
                ta = self.proj(s[:, 0:512], lambda k: Wa[:, k, W], lambda k: XNT[:, k, tok], 512, 2, sf, tw)
                tb = self.proj(s[:, 512:1024], lambda k: Wb[:, k, W], lambda k: XNT[:, k, tok], 512, 2, sf, tw)
                ti, tm, tf_ = tmp.take()
                t1 = dve(lambda e, s=s, o=o: e.tensor_tensor(QK[:, 1, o], s[:, 0:512], Tc[:, o], ALU.mult), ta, qf)
                t2 = dve(lambda e, s=s, o=o, tm=tm: e.tensor_tensor(tm, s[:, 512:1024], Ts[:, o], ALU.mult), tb, tf_)
                t3 = pool(lambda e, o=o, tm=tm: e.tensor_tensor(QK[:, 1, o], QK[:, 1, o], tm, ALU.add), t1, t2)
                s_r.done(si, t2)
                tmp.done(ti, t3)
                done += [t, t3]
            state[(b, ht)] = (qi, QK, done)

        def make_v(b):
            for i in range(8):
                oi, o, of = o_r.take()
                tok = slice(b * 1024 + i * 128, b * 1024 + i * 128 + 128)
                t = self.proj(o[:, 0:256], lambda k: XNT[:, k, tok], lambda k: Wv[:, k, :], 256, 2, of, tw)
                t = act(lambda e, o=o, i=i: e.activation(V[:, i, :, 0:16],
                        o[:, 0:256].rearrange("p (h d) -> p h d", h=16), ACT.Copy), t, state.get("vfree"))
                o_r.done(oi, t)
            state["v"] = t

        cur = {}

        def score(u, h):
            b, ht, qt = u
            if (b, ht) not in state:
                make_qk(b, ht)
            qi, QK, done = state[(b, ht)]
            r = slice(32 * h, 32 * h + 32)
            return QK[r, 0, qt * 128:qt * 128 + 128], lambda c0, c1: QK[r, 1, c0:c1], done

        def pv(u, j, PT, t2):
            b, ht, qt = u
            if j == 0:
                cur["o"] = o_r.take()
            oi, o, of = cur["o"]
            for h in range(4):
                t = pe(lambda e, h=h: e.matmul(o[32 * h:32 * h + 32, 0:128], V[:, j, ht * 4 + h, :],
                                               PT[:, h * 128:h * 128 + 128], start=(j == 0), stop=(j == qt)),
                       t2, of, state["v"], t_one, mark=(h == 3))
            if j == qt:
                ni, nb, nf = nrm.take()
                m = [16 + i % 16 for i in range(32)]
                ta = dve(lambda e: e.stream_shuffle(nb[:, 0, :], o[:, 0:128], m), t, nf)
                tb = dve(lambda e: e.reciprocal(nb[:, 1, :], nb[:, 0, :]), ta)
                tc = dve(lambda e: e.tensor_tensor(aT[:, ht, qt * 128:qt * 128 + 128], o[:, 0:128], nb[:, 1, :],
                                                   ALU.mult), tb, state.get("afree"))
                nrm.done(ni, tc)
                o_r.done(oi, tc)
                state["a"] = tc
                if qt == 7:
                    qk.done(state[(b, ht)][0], t)
                if qt == 7 and ht == 3:
                    state["vfree"] = t
                    out_proj(b)
            return t

        def out_proj(b):
            t = self.project_add(X, b * 8, 8, o_r, lambda i, k: aT[:, k, i * 128:i * 128 + 128],
                                 lambda k: Wo[:, k, :], 4, state["a"])
            state["afree"] = t
            if b == 0:
                make_v(1)

        make_v(0)
        units = [(b, ht, qt) for b in range(2) for ht in range(4) for qt in range(8)]
        self.attend(units, 4, work, score, 1.0, None, pv, (s_r, t_r))
        self.barrier()
        self.ffn(X, XNT, 8, lambda k, f: Wgu[:, k, f * 128:f * 128 + 128],
                 lambda k, f: Wgu[:, k, 1024 + f * 128:1024 + f * 128 + 128], lambda k: Wd[:, k, :],
                 lambda f: 128, ACT.Silu, WK0, tf)
        self.barrier()

    def layer1(self, X, XNT):
        pe, act, dve, pool = self.pe, self.act, self.dve, self.pool
        I = self.ins
        Wq = self.sb(WA0, 2, 2048)
        Wk, Wv = self.sb(WA0 + 4096, 2, 512), self.sb(WA0 + 5120, 2, 512)
        Wo = self.sb(WA0 + 6144, 16, 256)
        Tc, Ts = self.sb(WA0 + 10240, 1024), self.sb(WA0 + 11264, 1024)
        Wg = self.sb(WA0 + 12288, 2, 32)
        tmp = Ring([self.sb(EX0 + 512 * i, 512) for i in range(2)])
        Wgu = self.sb(WF0, 2, 2048)
        Wd = self.sb(WF0 + 4096, 8, 256)
        for dst, src in ((Wq, "l1_wq"), (Wk, "l1_wk"), (Wv, "l1_wv"), (Wo, "l1_wo"), (Tc, "l1_tc"), (Ts, "l1_ts"),
                         (Wg, "l1_wg")):
            tw = self.dma("w_a", dst, I[src])
        self.dma("w_f", Wgu, I["l1_wgu"])
        tf = self.dma("w_f", Wd, I["l1_wd"])
        self.norm(X, XNT)
        self.barrier()
        Q = self.sb(WK0, 4, 1024)
        Kt = self.sb(WK0 + 4096, 1024)
        V = self.sb(WK0 + 5120, 8, 512)
        aT = self.sb(WK0 + 9216, 4, 1024)
        G = self.sb(WK0 + 13312, 16, 16)
        work = WK0 + 13568
        s_r = Ring([self.PS[:, 2 * i:2 * i + 2, :].rearrange("p a b -> p (a b)") for i in range(2)])
        t_r = Ring([self.PS[:, i, :] for i in (4, 5)])
        o_r = Ring([self.PS[:, i, :] for i in (6, 7)])
        state, cur = {}, {}
        sg = self.sb(work, 16, 32)
        for i in range(NT):
            oi, o, of = o_r.take()
            t = self.proj(o[:, 0:32], lambda k: XNT[:, k, i * 128:i * 128 + 128], lambda k: Wg[:, k, :], 32, 2, of, tw)
            t = act(lambda e, o=o, i=i: e.activation(sg[:, i, :], o[:, 0:32], ACT.Sigmoid), t)
            o_r.done(oi, t)
        tg = dve(lambda e: e.tensor_tensor(G, sg[:, :, 0:16], sg[:, :, 16:32], ALU.add), t)
        state["sg"] = tg
        act.wait([tg])

        def rotate(W, dst, b, tt, *free):
            tok = slice(b * 1024 + tt * 512, b * 1024 + tt * 512 + 512)
            o = slice(tt * 512, tt * 512 + 512)
            si, s, sf = s_r.take()
            t = self.proj(s[:, 0:512], W, lambda k: XNT[:, k, tok], 512, 2, sf, tw)
            ti, tm, tf_ = tmp.take()
            t1 = dve(lambda e: e.tensor_tensor(dst[:, o], s[:, 0:512], Tc[:, o], ALU.mult), t, *free)
            dve(lambda e: e.tensor_tensor(tm[0:64, :], s[64:128, 0:512], Ts[64:128, o], ALU.mult), t, tf_)
            t2 = dve(lambda e: e.tensor_tensor(tm[64:128, :], s[0:64, 0:512], Ts[0:64, o], ALU.mult), t, tf_)
            t3 = pool(lambda e: e.tensor_tensor(dst[:, o], dst[:, o], tm, ALU.add), t1, t2)
            s_r.done(si, t2)
            tmp.done(ti, t3)
            return t3

        def make_qk(b, g):
            free = state.get("qfree")
            done = []
            for tt in range(2):
                done.append(rotate(lambda k: Wk[:, k, g * 128:g * 128 + 128], Kt, b, tt, free))
                for h in range(4):
                    c = (g * 4 + h) * 128
                    done.append(rotate(lambda k: Wq[:, k, c:c + 128], Q[:, h, :], b, tt, free))
            state[(b, g)] = done

        def make_v(b):
            for i in range(8):
                oi, o, of = o_r.take()
                tok = slice(b * 1024 + i * 128, b * 1024 + i * 128 + 128)
                t = self.proj(o, lambda k: XNT[:, k, tok], lambda k: Wv[:, k, :], 512, 2, of, tw)
                t = act(lambda e, o=o, i=i: e.activation(V[:, i, :], o, ACT.Copy), t, state.get("vfree"))
                o_r.done(oi, t)
            state["v"] = t

        def score(u, h):
            b, g, qt = u
            if (b, g) not in state:
                make_qk(b, g)
            return Q[:, h, qt * 128:qt * 128 + 128], lambda c0, c1: Kt[:, c0:c1], state[(b, g)]

        def after_score(u, h, t):
            if u[-1] == 7 and h == 3:
                state["qfree"] = t

        def pv(u, j, PT, t2):
            b, g, qt = u
            if j == 0:
                cur["o"] = o_r.take()
            oi, o, of = cur["o"]
            t = pe(lambda e: e.matmul(o, V[:, j, g * 128:g * 128 + 128], PT, start=(j == 0), stop=(j == qt)),
                   t2, of, state["v"])
            if j == qt:
                dst = aT[:, :, qt * 128:qt * 128 + 128]
                ta = act(lambda e: e.activation(dst, o.rearrange("p (h q) -> p h q", h=4), ACT.Copy), t,
                         state.get("afree"))
                o_r.done(oi, ta)
                state["a"] = ta
                if qt == 7:
                    if g == 3:
                        state["vfree"] = t
                    out_proj(b, g)
            return t

        def out_proj(b, g):
            t = self.project_add(X, b * 8, 8, o_r, lambda i, k: aT[:, k, i * 128:i * 128 + 128],
                                 lambda k: Wo[:, g * 4 + k, :], 4, state["a"])
            state["afree"] = t
            if (b, g) == (0, 3):
                make_v(1)

        make_v(0)
        units = [(b, g, qt) for b in range(2) for g in range(4) for qt in range(8)]
        self.attend(units, 4, work, score, float(np.float32(1.0) / np.sqrt(np.float32(128.0))),
                    lambda u, h: G[:, u[0] * 8 + u[2], u[1] * 4 + h:u[1] * 4 + h + 1], pv, (s_r, t_r), 3, after_score)
        self.barrier()
        self.ffn(X, XNT, 8, lambda k, f: Wgu[:, k, f * 128:f * 128 + 128],
                 lambda k, f: Wgu[:, k, 1024 + f * 128:1024 + f * 128 + 128], lambda k: Wd[:, k, :],
                 lambda f: 128, ACT.Silu, WK0, tf)
        self.barrier()

    def layer2(self, X, XNT):
        pe, act, dve, pool = self.pe, self.act, self.dve, self.pool
        I = self.ins
        Win = self.sb(WA0, 2, 4640)
        Wout = self.sb(WA0 + 9280, 16, 256)
        W12 = self.sb(WA0 + 13376, 2, 1408)
        W3 = self.sb(WA0 + 16192, 6, 256)
        Crep = self.sb(WA0 + 17728, 1024)
        sel = Ring([self.sb(WA0 + 18752 + 128 * i, 128) for i in range(2)])
        ident4 = self.sb(EX0, 512)
        dt = self.sb(EX0 + 512, 16, 32)
        vec = self.sb(self.misc, 204)
        mup, bin_, cw, cb, Dv, nw = (vec[:, 0:36], vec[:, 36:72], vec[:, 72:152], vec[:, 152:172], vec[:, 172:188],
                                     vec[:, 188:204])
        bm = self.sb(self.misc + 204, 36)
        dv = self.sb(self.misc + 240, 4, 32)
        bout = self.sb(WK0 + 20000, 256)
        for dst, src in ((Win, "l2_win"), (Wout, "l2_wout"), (vec, "l2_vec"), (dv, "l2_dt"), (bout, "l2_bout")):
            tw = self.dma("w_a", dst, I[src])
        self.dma("w_f", W12, I["l2_w12"])
        tf = self.dma("w_f", W3, I["l2_w3"])
        self.norm(X, XNT)
        for i in range(4):
            pool(lambda e, i=i: e.tensor_copy(ident4[:, i * 128:i * 128 + 128], self.ident))
        for i in range(NT):
            tx = pool(lambda e, i=i: e.tensor_tensor(X[:, i, :], X[:, i, :], bout, ALU.add), tw, dve.last())
        tbm = dve(lambda e: e.tensor_tensor(bm, bin_, mup, ALU.mult), tw)
        self.barrier()
        BC = self.sb(WK0, 4, 1024)
        BT = self.sb(WK0 + 4096, 8, 256)
        RAW = self.sb(WK0 + 6144, 2, 1032)
        XC = self.sb(WK0 + 8208, 2, 1024)
        XD = self.sb(WK0 + 10256, 8, 256)
        LT = self.sb(WK0 + 12304, 4, 8, 128)
        Y = self.sb(WK0 + 16400, 2, 1024)
        CP = self.sb(WK0 + 18448, 1024)
        R = self.sb(WK0 + 19472, 2048)
        Zr = Ring([self.sb(WK0 + 21520 + 512 * i, 512) for i in range(2)])
        Bd = Ring([self.sb(WK0 + 22544 + 128 * i, 4, 32) for i in range(2)])
        Hb = Ring([self.sb(WK0 + 22800 + 256 * i, 256) for i in range(2)])
        ach = self.sb(self.misc + 368, 8)
        aR = Ring([self.PS[:, i, :] for i in (0, 1)])
        bR = Ring([self.PS[:, i, :] for i in (2, 3)])
        sR = Ring([self.PS[:, i, 0:64] for i in (4, 7)])
        yR = Ring([self.PS[:, i, :] for i in (5, 6)])

        ai, ap_, af = aR.take()
        for i in range(NT):
            t = self.proj(ap_[:, i * 32:i * 32 + 32], lambda k: XNT[:, k, i * 128:i * 128 + 128],
                          lambda k: Win[:, k, 4608:4640], 32, 2, tw)
        W = [self.sb(WK0 + 512 * i, 16, 32) for i in range(6)]
        wide = lambda r: dv[:, r:r + 1, :].broadcast_to([128, 16, 32])
        pv3 = ap_.rearrange("p (a b) -> p a b", a=16)
        t = dve(lambda e: e.tensor_tensor(W[0], pv3, wide(0), ALU.add), t)
        aR.done(ai, t)
        t = dve(lambda e: e.tensor_tensor(W[0], W[0], wide(1), ALU.mult), t)
        tv = dve(lambda e: e.tensor_tensor(W[0], W[0], wide(2), ALU.add), t)
        t = dve(lambda e: e.tensor_scalar(W[1], W[0], -1.0, None, ALU.mult), tv)
        t = dve(lambda e: e.tensor_tensor(W[1], W[0], W[1], ALU.min), t)
        te = act(lambda e: e.activation(W[2], W[1], ACT.Exp), t)
        tA = act(lambda e: e.activation(dv[:, 3, :], dv[:, 3, :], ACT.Exp), tw)
        t = dve(lambda e: e.tensor_scalar(W[3], W[2], 2.0, None, ALU.add), te)
        t = dve(lambda e: e.reciprocal(W[3], W[3]), t)
        ts = dve(lambda e: e.tensor_tensor(W[3], W[2], W[3], ALU.mult), t)
        tz = dve(lambda e: e.tensor_tensor(W[4], W[3], W[3], ALU.mult), ts)
        t = dve(lambda e: e.tensor_scalar(W[5], W[4], 2.0 / 17.0, 2.0 / 15.0, ALU.mult, ALU.add), tz)
        for n in (13, 11, 9, 7, 5, 3, 1):
            t = dve(lambda e: e.tensor_tensor(W[5], W[5], W[4], ALU.mult), t)
            t = dve(lambda e, n=n: e.tensor_scalar(W[5], W[5], 2.0 / n, None, ALU.add), t)
        t = dve(lambda e: e.tensor_tensor(W[5], W[5], W[3], ALU.mult), t)
        t2 = dve(lambda e: e.tensor_scalar(W[0], W[0], 0.0, None, ALU.max), tv)
        tdt = dve(lambda e: e.tensor_tensor(dt, W[0], W[5], ALU.add), t, t2)
        t = dve(lambda e: e.tensor_tensor(W[1], dt, wide(3), ALU.mult), tdt, tA)
        t = act(lambda e: e.activation(W[1], W[1], ACT.Exp, scale=-1.0), t)
        for j in range(4):
            bi, bp, bf = bR.take()
            for i in range(4):
                t2 = pe(lambda e, i=i, bp=bp, j=j: e.transpose(bp[0:32, i * 128:i * 128 + 128], W[1][:, j * 4 + i, :],
                                                              self.ident), t, bf)
            t3 = dve(lambda e, bp=bp, j=j: e.tensor_copy(R[0:32, j * 512:j * 512 + 512], bp[0:32, :]), t2)
            bR.done(bi, t3)
        for c in range(16):
            o = slice(c * 128, c * 128 + 128)
            t = dve(lambda e, o=o: e.tensor_tensor_scan(R[32:64, o], R[0:32, o], self.ones[0:32, :], 1.0, ALU.mult,
                                                        ALU.mult), t3)
        tR = dve(lambda e: e.memset(R[0:32, 0:2048:128], 0.0), t)
        for h in Hb.bufs:
            pool(lambda e, h=h: e.memset(h, 0.0))
        tpad = pool(lambda e: e.memset(RAW[:, :, 0:3], 0.0))
        self.barrier()

        def raw(col, tile, slot, b, *free):
            for tt in range(2):
                tok = slice(b * 1024 + tt * 512, b * 1024 + tt * 512 + 512)
                ai, p, af = aR.take()
                t = self.proj(p, lambda k: Win[:, k, col:col + 128], lambda k: XNT[:, k, tok], 512, 2, af)
                t = act(lambda e, p=p, tt=tt: e.activation(RAW[:, slot, 3 + tt * 512:3 + tt * 512 + 512], p,
                        ACT.Identity, scale=mup[:, tile:tile + 1], bias=bm[:, tile:tile + 1]), t, *free)
                aR.done(ai, t)
            return t

        def conv(slot, ct, dst, t, *free):
            t = dve(lambda e: e.tensor_scalar(dst, RAW[:, slot, 0:1024], cw[:, ct * 4:ct * 4 + 1], None, ALU.mult), t,
                    *free)
            for k in range(1, 4):
                t = dve(lambda e, k=k: e.scalar_tensor_tensor(dst, RAW[:, slot, k:k + 1024],
                        cw[:, ct * 4 + k:ct * 4 + k + 1], dst, ALU.mult, ALU.add), t)
            return t, act(lambda e: e.activation(dst, dst, ACT.Silu, bias=cb[:, ct:ct + 1]), t)

        rfree = [None, None]
        last = {}
        for b in range(2):
            tbc = []
            for n in range(4):
                s = n % 2
                t = raw(4096 + n * 128, 32 + n, s, b, rfree[s])
                rfree[s], t = conv(s, 16 + n, BC[:, n, :], t, last.get("bc"))
                tbc.append(t)
            for c in range(8):
                bi, bp, bf = bR.take()
                for n in range(2):
                    t = pe(lambda e, n=n, bp=bp, c=c: e.transpose(bp[:, n * 128:n * 128 + 128],
                           BC[:, n, c * 128:c * 128 + 128], self.ident), tbc[n], bf)
                tbt = act(lambda e, bp=bp, c=c: e.activation(BT[:, c, :], bp[:, 0:256], ACT.Copy), t, last.get("bt"))
                bR.done(bi, tbt)
            for g in range(8):
                gg, bt, ct = g % 4, g // 4, 2 + g // 4
                q = slice(32 * gg, 32 * gg + 32)
                for r in range(4):
                    tc = self.dma("crep", Crep[32 * r:32 * r + 32, :], BC[q, ct, :], tbc[ct - 0], last.get("crep"))
                tcx = []
                for s in range(2):
                    tile = 2 * g + s
                    t = raw(2048 + tile * 128, 16 + tile, s, b, rfree[s])
                    rfree[s], t = conv(s, tile, XC[:, s, :], t, last.get("xc"))
                    tcx.append(t)
                for h in range(4):
                    for c4 in range(2):
                        bi, bp, bf = bR.take()
                        hh = 4 * g + h
                        o = slice(b * 1024 + c4 * 512, b * 1024 + c4 * 512 + 512)
                        t = pe(lambda e, bp=bp, hh=hh, o=o: e.matmul(bp, self.ident[0:32, hh:hh + 1].broadcast_to(
                            [32, 128]), R[0:32, o], start=True, stop=True), bf)
                        tl = dve(lambda e, bp=bp, h=h, c4=c4: e.tensor_tensor_scan(
                            LT[:, h, c4 * 4:c4 * 4 + 4, :].rearrange("p a b -> p (a b)"), bp, ident4, 0.0, ALU.mult,
                            ALU.add), t, last.get("lt"))
                        bR.done(bi, tl)
                gi, sg, gf = sel.take()
                tsg = pool(lambda e, g=g, sg=sg: e.tensor_copy(sg[32:64, :].rearrange("p (a b) -> p a b", a=4),
                           self.ident[32:64, 32 + 4 * g:36 + 4 * g].unsqueeze(2).broadcast_to([32, 4, 32])), gf)
                for c4 in range(2):
                    bi, bp, bf = bR.take()
                    o = slice(b * 1024 + c4 * 512, b * 1024 + c4 * 512 + 512)
                    t = pe(lambda e, bp=bp, o=o, sg=sg: e.matmul(bp, sg[32:64, :], R[32:64, o], start=True, stop=True),
                           tsg, bf)
                    sel.done(gi, t)
                    dve(lambda e, bp=bp, c4=c4: e.tensor_copy(ach[:, c4 * 4:c4 * 4 + 4], bp[:, 127:512:128]), t,
                        last.get("h"))
                    tcp = dve(lambda e, bp=bp, c4=c4: e.tensor_tensor(CP[:, c4 * 512:c4 * 512 + 512],
                              Crep[:, c4 * 512:c4 * 512 + 512], bp, ALU.mult), t, tc, last.get("cp"))
                    bR.done(bi, tcp)
                last["crep"] = tcp
                txd = []
                for c in range(8):
                    bi, bp, bf = bR.take()
                    for s in range(2):
                        t = pe(lambda e, s=s, bp=bp, c=c: e.transpose(bp[:, s * 128:s * 128 + 128],
                               XC[:, s, c * 128:c * 128 + 128], self.ident), tcx[s], bf)
                    t = dve(lambda e, bp=bp, c=c, g=g, b=b: e.tensor_tensor(
                        XD[:, c, :].rearrange("p (h d) -> p h d", h=4), bp[:, 0:256].rearrange("p (h d) -> p h d", h=4),
                        dt[:, b * 8 + c, 4 * g:4 * g + 4].unsqueeze(2).broadcast_to([128, 4, 64]), ALU.mult), t,
                        last.get("xd"))
                    bR.done(bi, t)
                    txd.append(t)
                hcur = None
                tfin = []
                for c in range(8):
                    o = slice(c * 128, c * 128 + 128)
                    if c % 4 == 0:
                        yi0, y0, yf0 = yR.take()
                        yi1, y1, yf1 = yR.take()
                        ys = (y0, y1)
                    di, bd, df = Bd.take()
                    tbd = dve(lambda e, bd=bd, c=c, g=g: e.tensor_tensor(
                        bd, BT[:, c, 32 * g:32 * g + 32].unsqueeze(1).broadcast_to([128, 4, 32]),
                        LT[:, :, c, 127:128].broadcast_to([128, 4, 32]), ALU.mult), tl, tbt, df)
                    bi, bp, bf = bR.take()
                    t = pe(lambda e, bp=bp, o=o, q=q, bt=bt, ct=ct: e.matmul(bp[:, 0:128], BC[q, bt, o], BC[q, ct, o],
                           start=True, stop=True), bf, tbc)
                    tm = dve(lambda e, bp=bp, c=c: e.tensor_tensor(LT[:, :, c, :], LT[:, :, c, :],
                             bp[:, 0:128].unsqueeze(1).broadcast_to([128, 4, 128]), ALU.mult), t, tbd)
                    bR.done(bi, tm)
                    if c < 7:
                        si, sp_, sf = sR.take()
                        for h in range(4):
                            tS = pe(lambda e, h=h, sp_=sp_, bd=bd, c=c: e.matmul(sp_[32 * h:32 * h + 32, :],
                                    bd[:, h, :], XD[:, c, h * 64:h * 64 + 64], start=True, stop=True), tbd, txd[c], sf)
                        Bd.done(di, tS)
                    else:
                        Bd.done(di, tbd)
                    w = slice((c % 4) * 128, (c % 4) * 128 + 128)
                    for s in range(2):
                        if c > 0:
                            pe(lambda e, s=s, w=w, o=o, hc=hcur[0], y=ys[s]: e.matmul(y[:, w],
                               hc[:, s * 128:s * 128 + 128], CP[:, o], start=True, stop=True,
                               skip_group_check=True), hcur[1], tcp,
                               (yf0, yf1)[s], mark=False)
                        for k in range(2):
                            h = 2 * s + k
                            t = pe(lambda e, h=h, k=k, w=w, c=c, y=ys[s]: e.matmul(y[64 * k:64 * k + 64, w],
                                   XD[:, c, h * 64:h * 64 + 64], LT[:, h, c, :], start=(c == 0), stop=True,
                                   skip_group_check=True), tm, txd[c], (yf0, yf1)[s])
                    if hcur:
                        Hb.done(hcur[2], t)
                    if c < 7:
                        hi, hn, hf = Hb.take()
                        for h in range(4):
                            qq, cc = slice(32 * h, 32 * h + 32), slice(64 * h, 64 * h + 64)
                            if c == 0:
                                th = dve(lambda e, qq=qq, cc=cc, hn=hn, sp_=sp_: e.tensor_copy(hn[qq, cc], sp_[qq, :]),
                                         tS, hf)
                            else:
                                th = dve(lambda e, qq=qq, cc=cc, hn=hn, sp_=sp_, ho=hcur[0], c=c:
                                         e.scalar_tensor_tensor(hn[qq, cc], ho[qq, cc], ach[qq, c:c + 1], sp_[qq, :],
                                                                ALU.mult, ALU.add), tS, hf, hcur[1])
                        sR.done(si, th)
                        hcur = (hn, th, hi)
                    if c % 4 == 3:
                        w5 = slice((c // 4) * 512, (c // 4) * 512 + 512)
                        tok = slice(b * 1024 + (c // 4) * 512, b * 1024 + (c // 4) * 512 + 512)
                        for s in range(2):
                            tile = 2 * g + s
                            ai, p, af = aR.take()
                            tz = self.proj(p, lambda k: Win[:, k, tile * 128:tile * 128 + 128],
                                           lambda k: XNT[:, k, tok], 512, 2, af)
                            zi, z, zf = Zr.take()
                            tz = act(lambda e, z=z, p=p, tile=tile: e.activation(z, p, ACT.Silu,
                                     scale=mup[:, tile:tile + 1], bias=bm[:, tile:tile + 1]), tz, zf)
                            aR.done(ai, tz)
                            t1 = dve(lambda e, s=s, w5=w5, y=ys[s], tile=tile: e.scalar_tensor_tensor(
                                Y[:, s, w5], XC[:, s, w5], Dv[:, tile:tile + 1], y, ALU.mult, ALU.add), t,
                                last.get("y"))
                            yR.done((yi0, yi1)[s], t1)
                            t2 = dve(lambda e, s=s, w5=w5, z=z: e.tensor_tensor(Y[:, s, w5], Y[:, s, w5], z, ALU.mult),
                                     t1, tz)
                            Zr.done(zi, t2)
                            tfin.append(t2)
                last["xd"] = last["lt"] = last["cp"] = last["h"] = t
                last["xc"] = tfin[-1]
                for c2 in range(2):
                    w5 = slice(c2 * 512, c2 * 512 + 512)
                    bi, bp, bf = bR.take()
                    for s in range(2):
                        zi, z, zf = Zr.take()
                        t = act(lambda e, z=z, s=s, w5=w5: e.activation(z, Y[:, s, w5], ACT.Square), tfin, zf)
                        t = pe(lambda e, z=z, s=s, bp=bp: e.matmul(bp, self.ones, z, start=(s == 0), stop=(s == 1)), t,
                               bf)
                        Zr.done(zi, t)
                    zi, z, zf = Zr.take()
                    t = act(lambda e, z=z, bp=bp: e.activation(z, bp, ACT.Sqrt, scale=1.0 / 256.0, bias=self.eps), t,
                            zf)
                    bR.done(bi, t)
                    t = dve(lambda e, z=z: e.reciprocal(z, z), t)
                    for s in range(2):
                        ty = dve(lambda e, z=z, s=s, w5=w5, g=g: e.scalar_tensor_tensor(
                            Y[:, s, w5], Y[:, s, w5], nw[:, 2 * g + s:2 * g + s + 1], z, ALU.mult, ALU.mult), t)
                    Zr.done(zi, ty)
                t = self.project_add(X, b * 8, 8, aR, lambda i, k: Y[:, k, i * 128:i * 128 + 128],
                                     lambda k: Wout[:, 2 * g + k, :], 2, ty)
                last["y"] = t
                last["bc"] = last["bt"] = t
        self.barrier()
        st = self.sb(WK0, 8)
        tmp = self.sb(WK0 + 512, 1408)
        ps = Ring([self.PS[:, i, :] for i in (0, 1)])
        dve.wait([tf])
        tq = []
        for n, w in enumerate((W12[:, :, 0:704], W12[:, :, 704:1408], W3)):
            cols = 768 if n == 2 else 704
            axis = AX.XY
            t = dve(lambda e, n=n, w=w: e.tensor_reduce(st[:, n:n + 1], w, AX.XY, ALU.add, apply_absolute_value=True))
            pi, p, pf = ps.take()
            t = pe(lambda e, n=n, p=p: e.matmul(p[:, 0:1], self.ones, st[:, n:n + 1], start=True, stop=True), t, pf)
            t = dve(lambda e, p=p: e.tensor_scalar(st[:, 3:4], p[:, 0:1], 1.0 / 180224.0, 1e-8, ALU.mult, ALU.add), t)
            ps.done(pi, t)
            t1 = dve(lambda e: e.tensor_scalar(st[:, 4:5], st[:, 3:4], 0.5, None, ALU.mult), t)
            t2 = dve(lambda e: e.tensor_scalar(st[:, 5:6], st[:, 3:4], -0.5, None, ALU.mult), t)
            a, k = (6, 256) if n == 2 else (2, 704)
            tm = tmp[:, 0:1408] if n < 2 else self.sb(WK0 + 512, 1536)
            tm = tm.rearrange("p (a b) -> p a b", a=a)
            t = dve(lambda e, w=w, tm=tm: e.tensor_scalar(tm, w, st[:, 5:6], None, ALU.is_lt), t1, t2)
            t = dve(lambda e, w=w, tm=tm: e.scalar_tensor_tensor(w, w, st[:, 4:5], tm, ALU.is_gt, ALU.subtract), t)
        self.barrier()
        r = lambda f: 64 if f == 5 else 128
        self.ffn(X, XNT, 6, lambda k, f: W12[:, k, f * 128:f * 128 + r(f)],
                 lambda k, f: W12[:, k, 704 + f * 128:704 + f * 128 + r(f)], lambda k: W3[:, k, :],
                 r, ACT.Sigmoid, WK0, tf)
        self.barrier()

    def layer3(self, X, XNT):
        pe, act, dve, pool = self.pe, self.act, self.dve, self.pool
        I = self.ins
        Wsa = self.sb(WA0, 2, 64)
        Wo = self.sb(WA0 + 128, 2, 256)
        bo = self.sb(WA0 + 640, 256)
        Wr = self.sb(WA0 + 896, 2, 16)
        XN = self.sb(WA0 + 1024, 16, 256)
        QT, KT = self.sb(WA0 + 5120, 2048), self.sb(WA0 + 7168, 2048)
        for dst, src in ((Wsa, "l3_wsa"), (Wo, "l3_wo"), (bo, "l3_bo"), (Wr, "l3_wr")):
            tw = self.dma("w_a", dst, I[src])
        E1 = Ring([self.sb(WF0 + 2048 * i, 2, 512) for i in range(3)])
        E2 = [self.sb(WF0 + 2048 * i + 1024, 4, 256) for i in range(3)]
        te = {}

        def load(e):
            i, w1, free = E1.take()
            self.dma(f"e{i}", w1, I["l3_w1"][:, e], free)
            te[e] = (i, w1, E2[i], self.dma(f"e{i}", E2[i], I["l3_w2"][:, e], free))

        for e in range(3):
            load(e)
        self.norm(X, XNT, XN)
        for i in range(NT):
            pool(lambda e, i=i: e.tensor_tensor(X[:, i, :], X[:, i, :], bo, ALU.add), tw, dve.last())
        self.barrier()
        s_r = Ring([self.PS[:, 2 * i:2 * i + 2, :].rearrange("p a b -> p (a b)") for i in range(2)])
        t_r = Ring([self.PS[:, i, :] for i in (4, 5)])
        o_r = Ring([self.PS[:, i, :] for i in (6, 7)])
        LG = self.sb(WK0, 16, 16)
        M8 = self.sb(WK0 + 256, 16, 8)
        I8 = self.sb(WK0 + 384, 16, 8)
        IF = self.sb(WK0 + 512, 16, 2)
        PR = self.sb(WK0 + 544, 16, 2)
        io = self.sb(WK0 + 576, 16)
        C = self.sb(WK0 + 1024, 16, 16)
        C2 = self.sb(WK0 + 1280, 16, 16)
        oi, o, of = o_r.take()
        for i in range(NT):
            t = self.proj(o[:, i * 16:i * 16 + 16], lambda k: XNT[:, k, i * 128:i * 128 + 128], lambda k: Wr[:, k, :],
                          16, 2, of, tw)
        t = dve(lambda e: e.tensor_copy(LG, o[:, 0:256].rearrange("p (a b) -> p a b", a=16)), t)
        o_r.done(oi, t)
        tio = pool(lambda e: e.iota(io, pattern=[[1, 16]], base=0, channel_multiplier=0,
                                    allow_small_or_imprecise_dtypes=True))
        for i in range(NT):
            t1 = dve(lambda e, i=i: e.max(M8[:, i, :], LG[:, i, :]), t)
            t2 = dve(lambda e, i=i: e.max_index(I8[:, i, :].bitcast(U32), M8[:, i, :], LG[:, i, :]), t1)
        ti = dve(lambda e: e.tensor_copy(IF, I8[:, :, 0:2].bitcast(U32)), t2)
        t = dve(lambda e: e.tensor_tensor(PR[:, :, 1], M8[:, :, 1], M8[:, :, 0], ALU.subtract), t1)
        tx = act(lambda e: e.activation(PR[:, :, 1], PR[:, :, 1], ACT.Exp), t)
        t = dve(lambda e: e.tensor_scalar(PR[:, :, 0], PR[:, :, 1], 1.0, None, ALU.add), tx)
        t = dve(lambda e: e.reciprocal(PR[:, :, 0], PR[:, :, 0]), t)
        tp = dve(lambda e: e.tensor_tensor(PR[:, :, 1], PR[:, :, 1], PR[:, :, 0], ALU.mult), t)
        w3 = [128, 16, 16]
        iob = io.unsqueeze(1).broadcast_to(w3)
        tt_ = []
        for n, c in enumerate((C, C2)):
            t = dve(lambda e, n=n, c=c: e.tensor_tensor(c, iob, IF[:, :, n:n + 1].broadcast_to(w3), ALU.is_equal),
                    ti, tio)
            t = dve(lambda e, n=n, c=c: e.tensor_tensor(c, c, PR[:, :, n:n + 1].broadcast_to(w3), ALU.mult), t, tp)
            tt_.append(t)
        tC = dve(lambda e: e.tensor_tensor(C, C, C2, ALU.add), tt_)
        tq = []
        for tt in range(4):
            si, s, sf = s_r.take()
            k5 = slice(tt * 512, tt * 512 + 512)
            t = self.proj(s[0:64, 0:512], lambda k: Wsa[:, k, :], lambda k: XNT[:, k, k5], 512, 2, sf)
            t1 = act(lambda e, s=s, k5=k5: e.activation(QT[0:32, k5], s[0:32, 0:512], ACT.Copy), t)
            t2 = act(lambda e, s=s, k5=k5: e.activation(KT[0:32, k5], s[32:64, 0:512], ACT.Copy), t)
            s_r.done(si, t2)
            tq.append(t2)
        work = WK0 + 2048
        nb = Ring([self.sb(WK0 + 8192 + 512 * i, 512) for i in range(2)])
        cur = {}

        def score(u, h):
            b, qt = u
            o = b * 1024
            return (QT[0:32, o + qt * 128:o + qt * 128 + 128], lambda c0, c1: KT[0:32, o + c0:o + c1], tq)

        def pv(u, j, PT, t2):
            b, qt = u
            if j == 0:
                cur["o"] = o_r.take()
            oi, o, of = cur["o"]
            t = pe(lambda e: e.matmul(o[:, 0:256], PT, XN[:, b * 8 + j, :], start=(j == 0), stop=(j == qt)), t2, of)
            if j == qt:
                st = self.sb(self.misc + (qt % 2) * 32, 4, 8)
                ni, n, nf = nb.take()
                tr = dve(lambda e: e.reciprocal(st[:, 2, 0:1], st[:, 1, 0:1]), t)
                ta = dve(lambda e: e.tensor_scalar(n[:, 0:256], o[:, 0:256], st[:, 2, 0:1], None, ALU.mult), tr, nf)
                o_r.done(oi, ta)
                oi, o, of = o_r.take()
                for c in range(2):
                    tb = pe(lambda e, c=c, o=o: e.transpose(o[:, c * 128:c * 128 + 128], n[:, c * 128:c * 128 + 128],
                                                            self.ident), ta, of)
                tc = act(lambda e, o=o: e.activation(n[:, 256:512], o[:, 0:256], ACT.Copy), tb)
                o_r.done(oi, tc)
                oi, o, of = o_r.take()
                td = self.proj(o[:, 0:256], lambda k: n[:, 256 + k * 128:384 + k * 128], lambda k: Wo[:, k, :], 256, 2,
                               of, tc)
                nb.done(ni, td)
                x = X[:, b * 8 + qt, :]
                tf = dve(lambda e, o=o: e.tensor_tensor(x, x, o[:, 0:256], ALU.add), td)
                o_r.done(oi, tf)
            return t

        units = [(b, qt) for b in range(2) for qt in range(8)]
        self.attend(units, 1, work, score, float(np.float32(1.0 / np.sqrt(32))), None, pv, (s_r, t_r), 4)
        self.barrier()
        self.experts(X, XNT, C, te, load, E1)

    def experts(self, X, XNT, C, te, load, E1):
        pe, act, dve = self.pe, self.act, self.dve
        g_r = Ring([self.PS[:, i, :] for i in range(4)])
        d_r = Ring([self.PS[:, i, :] for i in range(4, 8)])
        H = Ring([self.sb(WK0 + 2048 + 2048 * i, 4, 512) for i in range(3)])

        def up(e_, tt):
            i, w1, w2, tw = te[e_]
            hi, h, hf = H.take()
            tok = slice(tt * 512, tt * 512 + 512)
            ta = []
            for f in range(4):
                gi, g, gf = g_r.take()
                t = self.proj(g, lambda k: w1[:, k, f * 128:f * 128 + 128], lambda k: XNT[:, k, tok], 512, 2, gf, tw)
                t = act(lambda e, g=g, f=f: e.activation(h[:, f, :], g, ACT.Silu), t, hf)
                g_r.done(gi, t)
                ta.append(t)
            return e_, tt, hi, h, ta

        def down(e_, tt, hi, h, ta):
            i, w1, w2, tw = te[e_]
            for j in range(0, 4, 2):
                di, d, df = d_r.take()
                for m in range(2):
                    t = self.proj(d[:, m * 256:m * 256 + 256],
                                  lambda k: h[:, k, (j + m) * 128:(j + m) * 128 + 128], lambda k: w2[:, k, :], 256, 4,
                                  df, ta)
                for m in range(2):
                    x = tt * 4 + j + m
                    t2 = dve(lambda e, d=d, m=m, x=x: e.scalar_tensor_tensor(X[:, x, :], d[:, m * 256:m * 256 + 256],
                             C[:, x, e_:e_ + 1], X[:, x, :], ALU.mult, ALU.add), t)
                d_r.done(di, t2)
            H.done(hi, t)
            if tt == 3 and e_ + 3 < 16:
                E1.done(i, t)
                load(e_ + 3)

        prev = None
        for e_ in range(16):
            for tt in range(4):
                cur = up(e_, tt)
                if prev:
                    down(*prev)
                prev = cur
        down(*prev)


def build(nc, ins, outs, first=0, layers=4):
    with ExitStack() as ctx:
        k = K(nc, ctx, ins, outs)
        block = ctx.enter_context(nc.Block())
        X = k.sb(X0, 16, 256)
        XNT = k.sb(XNT0, 2, 2048)
        tx = k.dma("x", X, ins["x"])
        k.consts()
        k.dve.wait([tx])
        for n in range(first, layers):
            (k.layer0, k.layer1, k.layer2, k.layer3)[n](X, XNT)
        k.barrier()
        to = k.dma("out", outs["out"], X)
        k.sp.wait([to])

        @block.sync
        def _(e):
            for f in k.sp.queue:
                f(e)

        @block.tensor
        def _(e):
            for f in k.pe.queue:
                f(e)

        @block.scalar
        def _(e):
            for f in k.act.queue:
                f(e)

        @block.vector
        def _(e):
            for f in k.dve.queue:
                f(e)

        @block.gpsimd
        def _(e):
            for f in k.pool.queue:
                f(e)


def kmajor(w):
    k, n = w.shape
    return np.ascontiguousarray(w.reshape(k // 128, 128, n).transpose(1, 0, 2))


def rope(n, d):
    inv = (np.float32(1.0) / np.power(np.float32(10000.0), np.arange(d // 2, dtype=np.float32) / np.float32(d // 2)))
    ang = np.arange(n, dtype=np.float32)[:, None] * inv.astype(np.float32)[None, :]
    return np.cos(ang).T.astype(np.float32), np.sin(ang).T.astype(np.float32)


def layout(i):
    a = {}
    a["x"] = np.ascontiguousarray(i["L0_attn_x"].reshape(16, 128, 256).transpose(1, 0, 2))
    h = np.arange(16)[:, None] * 16
    lo, hi = np.arange(8), np.arange(8, 16)
    iq = (h + np.concatenate([lo, hi, hi, lo])[None]).ravel()
    ia = (h + np.concatenate([lo, hi, lo, hi])[None]).ravel()
    ib = (h + np.concatenate([hi, lo, hi, lo])[None]).ravel()
    a["l0_wq"] = kmajor(i["L0_attn_Wq"].T[:, iq])
    a["l0_wa"] = kmajor(i["L0_attn_Wk"].T[:, ia])
    a["l0_wb"] = kmajor(i["L0_attn_Wk"].T[:, ib])
    a["l0_wv"] = kmajor(i["L0_attn_Wv"].T)
    wo = np.zeros((16, 32, 256), np.float32)
    wo[:, :16, :] = i["L0_attn_Wo"].T.reshape(16, 16, 256)
    a["l0_wo"] = kmajor(wo.reshape(512, 256))
    c, s = rope(1024, 16)
    q = np.float32(0.25)
    a["l0_tq"] = np.tile(np.concatenate([c, c, -s, s]) * q, (4, 1))
    a["l0_tc"] = np.tile(np.concatenate([c, c, c, c]), (4, 1))
    a["l0_ts"] = np.tile(np.concatenate([-s, s, -s, s]), (4, 1))
    a["l0_wgu"] = kmajor(i["L0_ffn_w_gate_up"].T)
    a["l0_wd"] = kmajor(i["L0_ffn_w_down"].T)
    a["l1_wq"] = kmajor(i["L1_attn_Wq"].T)
    a["l1_wk"] = kmajor(i["L1_attn_Wk"].T)
    a["l1_wv"] = kmajor(i["L1_attn_Wv"].T)
    a["l1_wo"] = kmajor(i["L1_attn_Wo"].T)
    a["l1_wg"] = kmajor(np.concatenate([i["L1_attn_Wgslc"].T, i["L1_attn_Wgswa"].T], axis=1))
    c, s = rope(1024, 128)
    a["l1_tc"] = np.concatenate([c, c])
    a["l1_ts"] = np.concatenate([s, -s])
    a["l1_wgu"] = kmajor(np.concatenate([i["L1_ffn_w_gate"].T, i["L1_ffn_w_up"].T], axis=1))
    a["l1_wd"] = kmajor(i["L1_ffn_w_down"].T)
    a["l2_win"] = kmajor(i["L2_attn_W_in"])
    a["l2_wout"] = kmajor(i["L2_attn_W_out"])
    col = lambda v, n: v.reshape(n, 128).T
    cw = i["L2_attn_conv_w"].reshape(20, 128, 4).transpose(1, 0, 2).reshape(128, 80)
    a["l2_vec"] = np.concatenate([col(i["L2_attn_mup_vector"][:4608], 36), col(i["L2_attn_b_in"][:4608], 36), cw,
                                  col(i["L2_attn_conv_b"], 20), col(np.repeat(i["L2_attn_D_param"], 64), 16),
                                  col(i["L2_attn_norm_w"], 16)], axis=1)
    a["l2_dt"] = np.broadcast_to(np.stack([i["L2_attn_b_in"][4608:], i["L2_attn_mup_vector"][4608:],
                                           i["L2_attn_dt_bias"], i["L2_attn_A_log"]])[None], (128, 4, 32))
    a["l2_bout"] = np.broadcast_to(i["L2_attn_b_out"][None], (128, 256))
    a["l2_w12"] = kmajor(np.concatenate([i["L2_ffn_w1"].T, i["L2_ffn_w2"].T], axis=1))
    w3 = np.zeros((768, 256), np.float32)
    w3[:704] = i["L2_ffn_w3"].T
    a["l2_w3"] = kmajor(w3)
    a["l3_wsa"] = kmajor(np.concatenate([i["L3_attn_Ws"], i["L3_attn_Wa"]], axis=1))
    a["l3_wo"] = kmajor(i["L3_attn_Wo"].T)
    a["l3_bo"] = np.broadcast_to(i["L3_attn_bo"][None], (128, 256))
    a["l3_wr"] = kmajor(i["L3_ffn_router_w"])
    a["l3_w1"] = i["L3_ffn_W1"].reshape(16, 2, 128, 512).transpose(2, 0, 1, 3)
    a["l3_w2"] = i["L3_ffn_W2"].reshape(16, 4, 128, 256).transpose(2, 0, 1, 3)
    return a


def kernel(**inputs):
    import concourse.bacc as bacc
    from concourse.bass_utils import run_bass_kernel_spmd as run

    arrays = layout({k: np.asarray(v) for k, v in inputs.items()})
    arrays = {k: np.ascontiguousarray(v) for k, v in arrays.items()}
    nc = bacc.Bacc("TRN2", target_bir_lowering=False, num_devices=1)
    ins = {k: nc.dram_tensor(k, v.shape, mybir.dt.from_np(v.dtype), kind="ExternalInput").ap()
           for k, v in arrays.items()}
    outs = {"out": nc.dram_tensor("out", (128, 16, 256), F32, kind="ExternalOutput").ap()}
    build(nc, ins, outs)
    r = run(nc, [arrays], core_ids=[0]).results[0]["out"]
    return np.ascontiguousarray(r.reshape(128, 16, 256).transpose(1, 0, 2)).reshape(2, 1024, 256)
```

```python
import numpy as np
from contextlib import ExitStack
import concourse.bass as bass
from concourse import mybir

F32 = mybir.dt.float32
U32 = mybir.dt.uint32
ALU = mybir.AluOpType
ACT = mybir.ActivationFunctionType
AX = mybir.AxisListType

T = 2048
NT = 16
D = 256
NEG = -1.0e30

X0, XNT0, CONST0, WA0, WF0, WK0, EX0, END = 0, 4096, 8192, 9216, 22528, 28672, 52000, 53200


class Lane:

    def __init__(self, name, sem):
        self.name, self.sem, self.count, self.seen, self.queue = name, sem, 0, {}, []

    def wait(self, tokens):
        for sem, value in tokens:
            if value > self.seen.get(id(sem), 0):
                self.seen[id(sem)] = value
                self.queue.append(lambda e, s=sem, v=value: e.wait_ge(s, v))

    def __call__(self, f, *tokens, mark=True):
        self.wait(flat(tokens))
        if not mark:
            self.queue.append(f)
            return None
        self.count += 1
        self.queue.append(lambda e, s=self.sem: f(e).then_inc(s, 1))
        return (self.sem, self.count)

    def last(self):
        return (self.sem, self.count)


def flat(tokens):
    for t in tokens:
        if t is None:
            continue
        if isinstance(t, list):
            yield from flat(t)
        else:
            yield t


class Ring:

    def __init__(self, bufs):
        self.bufs, self.free, self.at = bufs, [[] for _ in bufs], -1

    def take(self):
        self.at = (self.at + 1) % len(self.bufs)
        return self.at, self.bufs[self.at], self.free[self.at]

    def done(self, i, *tokens):
        self.free[i] = list(flat(tokens))


class Banks:

    def __init__(self, view, n):
        self.view, self.n, self.free, self.at = view, n, [[] for _ in range(n)], 0

    def take(self, two=True):
        w = 2 if two else 1
        self.at += self.at % w
        i = self.at % self.n
        self.at = i + w
        at = slice(i, i + w)
        return at, self.view[:, i * 512:(i + w) * 512], [self.free[j] for j in range(i, i + w)]

    def done(self, at, *tokens):
        for j in range(at.start, at.stop):
            self.free[j] = list(flat(tokens))


class K:
    def __init__(self, nc, ctx, ins, outs):
        self.nc, self.ins, self.outs = nc, ins, outs
        self.A = ctx.enter_context(nc.sbuf_tensor("arena", [128, END], F32))
        self.PS = ctx.enter_context(nc.psum_tensor("ps", [128, 8, 512], F32))
        mk = lambda n: ctx.enter_context(nc.semaphore(n))
        self.pe = Lane("pe", mk("s_pe"))
        self.act = Lane("act", mk("s_act"))
        self.dve = Lane("dve", mk("s_dve"))
        self.pool = Lane("pool", mk("s_pool"))
        self.sp = Lane("sp", mk("s_sp"))
        self.mk = mk
        self.dsem = {}
        self.later = []

    def sb(self, at, *shape):
        n = int(np.prod(shape))
        assert at + n <= END
        v = self.A[:, at:at + n]
        if len(shape) == 2:
            v = v.rearrange("p (a b) -> p a b", a=shape[0])
        elif len(shape) == 3:
            v = v.rearrange("p (a b c) -> p a b c", a=shape[0], b=shape[1])
        return v

    def dma(self, name, out, in_, *tokens, lane=None):
        if name not in self.dsem:
            self.dsem[name] = [self.mk("d_" + name), 0]
        s = self.dsem[name]
        s[1] += 16
        (lane or self.sp)(lambda e, sem=s[0]: e.dma_start(out, in_).then_inc(sem, 16), *tokens, mark=False)
        return (s[0], s[1])

    def barrier(self):
        lanes = [self.pe, self.act, self.dve, self.pool]
        marks = [l.last() for l in lanes]
        for l in lanes + [self.sp]:
            l.wait(marks)

    def consts(self):
        pool, dve = self.pool, self.dve
        self.ident = self.sb(CONST0, 128)
        self.mask = self.sb(CONST0 + 128, 128)
        self.ones = self.sb(CONST0 + 256, 128)
        self.eps = self.sb(CONST0 + 384, 1)
        self.eps8 = self.sb(CONST0 + 385, 1)
        self.zero1 = self.sb(CONST0 + 386, 1)
        self.misc = CONST0 + 400
        t0 = pool(lambda e: e.memset(self.ident, 0.0))
        t1 = pool(lambda e: e.memset(self.mask, 0.0))
        pool(lambda e: e.memset(self.ones, 1.0))
        pool(lambda e: e.memset(self.eps, 1e-5))
        pool(lambda e: e.memset(self.zero1, 0.0))
        pool(lambda e: e.affine_select(out=self.ident, in_=self.ident, compare_op=ALU.not_equal, fill=1.0,
                                       base=0, pattern=[[-1, 128]], channel_multiplier=1), t0)
        t = pool(lambda e: e.affine_select(out=self.mask, in_=self.mask, compare_op=ALU.is_ge, fill=NEG,
                                           base=0, pattern=[[-1, 128]], channel_multiplier=1), t1)
        for l in (self.pe, self.act, self.dve, self.pool):
            l.wait([t])

    def norm(self, X, XNT, XN=None):
        pe, act, dve = self.pe, self.act, self.dve
        st = self.sb(WK0, 16, 6)
        mv = self.sb(WK0 + 96, 16, 2)
        sd = self.sb(WK0 + 128, 16)
        tmp = Ring([self.sb(WK0 + 256 + 256 * i, 256) for i in range(4)])
        ps = Ring([self.PS[:, i, :] for i in range(8)])
        for i in range(NT):
            t = dve(lambda e, i=i: e.bn_stats(st[:, i, :], X[:, i, :]))
            t = dve(lambda e, i=i: e.bn_aggr(mv[:, i, :], st[:, i, :]), t)
        t = act(lambda e: e.activation(sd, mv[:, :, 1], ACT.Sqrt, bias=self.eps), t)
        trs = dve(lambda e: e.reciprocal(sd, sd), t)
        tl = []
        tm = self.dve.last()
        for i0 in range(0, NT, 4):
            pend = []
            (b0, p0, f0), (b1, p1, f1) = ps.take(), ps.take()
            for i in range(i0, i0 + 4):
                if XN is None:
                    k, xn, fr = tmp.take()
                else:
                    xn, fr = XN[:, i, :], []
                t = dve(lambda e, i=i, xn=xn: e.tensor_scalar(xn, X[:, i, :], mv[:, i, 0:1], sd[:, i:i + 1],
                                                              ALU.subtract, ALU.mult), trs, tm, fr)
                for c, (p, f) in enumerate(((p0, f0), (p1, f1))):
                    t2 = pe(lambda e, p=p, xn=xn, c=c, j=i - i0: e.transpose(
                        p[:, j * 128:j * 128 + 128], xn[:, c * 128:c * 128 + 128], self.ident), t, f)
                if XN is None:
                    tmp.done(k, t2)
            a = act(lambda e, p=p0, i0=i0: e.activation(XNT[:, 0, i0 * 128:i0 * 128 + 512], p, ACT.Copy), t2)
            b = dve(lambda e, p=p1, i0=i0: e.tensor_copy(XNT[:, 1, i0 * 128:i0 * 128 + 512], p), t2)
            ps.done(b0, a)
            ps.done(b1, b)
            tl += [a, b]
        return tl

    def flush(self):
        for f in self.later:
            f()
        self.later = []

    def proj(self, ps, lhsT, rhs, n, nk, *tokens):
        for k in range(nk):
            t = self.pe(lambda e, k=k, a=lhsT(k), b=rhs(k): e.matmul(ps, a, b, start=(k == 0), stop=(k == nk - 1)),
                        *tokens, mark=(k == nk - 1))
        return t

    def project_add(self, X, first, n, ring, lhsT, rhs, nk, *tokens):
        for i in range(0, n, 2):
            pi, p, pf = ring.take()
            for j in range(2):
                t = self.proj(p[:, j * 256:j * 256 + 256], lambda k: lhsT(i + j, k), rhs, 256, nk, pf, *tokens)
            x = X[:, first + i:first + i + 2, :]
            t2 = self.dve(lambda e, p=p, x=x: e.tensor_tensor(x, x, p.rearrange("p (a b) -> p a b", a=2), ALU.add), t)
            ring.done(pi, t2)
        return t

    def ffn(self, X, XNT, nf, wg, wu, wd, rows, gate, work, tw, out_scale=None):
        pe, act, dve = self.pe, self.act, self.dve
        g_r = Ring([self.PS[:, i, :] for i in (0, 1)])
        u_r = Ring([self.PS[:, i, :] for i in (2, 3)])
        d_r = Ring([self.PS[:, i, :] for i in (4, 5, 6, 7)])
        tmp = Ring([self.sb(work + 512 * i, 512) for i in range(3)])
        H = Ring([self.sb(work + 1536 + 512 * nf * i, nf, 512) for i in range(2)])

        def up(tt):
            hi, h, hf = H.take()
            done = []
            tok = slice(tt * 512, tt * 512 + 512)
            for f in range(nf):
                r = rows(f)
                gi, g, gf = g_r.take()
                ui, u, uf = u_r.take()
                tg = self.proj(g[:r, :], lambda k: wg(k, f), lambda k: XNT[:, k, tok], 512, 2, gf, tw)
                tu = self.proj(u[:r, :], lambda k: wu(k, f), lambda k: XNT[:, k, tok], 512, 2, uf, tw)
                ti, s, sf = tmp.take()
                ta = act(lambda e, s=s, g=g, r=r: e.activation(s[:r, :], g[:r, :], gate), tg, sf)
                g_r.done(gi, ta)
                td = dve(lambda e, s=s, u=u, r=r, f=f: e.tensor_tensor(h[:r, f, :], s[:r, :], u[:r, :], ALU.mult),
                         ta, tu, hf)
                u_r.done(ui, td)
                tmp.done(ti, td)
            return tt, hi, h, td

        def down(tt, hi, h, th):
            t = self.project_add(X, tt * 4, 4, d_r, lambda i, k: h[:rows(k), k, i * 128:i * 128 + 128],
                                 lambda k: wd(k)[:rows(k), :], nf, th, tw)
            H.done(hi, t)

        prev = None
        for tt in range(4):
            cur = up(tt)
            if prev:
                down(*prev)
            prev = cur
        down(*prev)

    def attend(self, units, nh, work, score, scale, pscale, pv, rings, npt=4, after=None):
        pe, act, dve, pool = self.pe, self.act, self.dve, self.pool
        s_r, t_r = rings
        PB = [self.sb(work + nh * 1024 * i, nh, 1024) for i in range(2)]
        PTr = Ring([self.sb(work + nh * 2048 + 128 * nh * i, nh * 128) for i in range(npt)])
        small = self.misc
        pfree = [[], []]
        evac = [0]

        def scores(n, u, h):
            qt = u[-1]
            nk = 128 * (qt + 1)
            q, k, tk = score(u, h)
            si, s, sf = s_r.take(nk > 512)
            for c in range(0, nk, 512):
                w = min(512, nk - c)
                t = pe(lambda e, c=c, w=w: e.matmul(s[:, c:c + w], q, k(c, c + w), start=True, stop=True), sf, tk,
                       mark=(c + 512 >= nk))
            if after:
                after(u, h, t)
            t = dve(lambda e: e.tensor_tensor(s[:, nk - 128:nk], s[:, nk - 128:nk], self.mask, ALU.add), t)
            st = self.sb(small + (n % 2) * 32, 4, 8)
            t = dve(lambda e: e.tensor_reduce(st[:, 0, h:h + 1], s[:, :nk], AX.X, ALU.max, negate=True), t,
                    pfree[n % 2])
            if scale != 1.0:
                t = dve(lambda e: e.tensor_scalar(st[:, 0, h:h + 1], st[:, 0, h:h + 1], scale, None, ALU.mult), t)
            P = PB[n % 2]
            t = act(lambda e: e.activation(P[:, h, :nk], s[:, :nk], ACT.Exp, bias=st[:, 0, h:h + 1], scale=scale,
                                           accum_out=st[:, 1, h:h + 1]), t, pfree[n % 2])
            s_r.done(si, t)
            if pscale is None:
                return lambda: t

            def finish(t=t):
                t = dve(lambda e: e.reciprocal(st[:, 2, h:h + 1], st[:, 1, h:h + 1]), t)
                r = 2
                if g is not None:
                    t = dve(lambda e: e.tensor_tensor(st[:, 3, h:h + 1], g, st[:, 2, h:h + 1], ALU.mult), t)
                    r = 3
                return (dve if h == nh - 1 else pool)(lambda e: e.tensor_scalar(
                    P[:, h, :nk], P[:, h, :nk], st[:, r, h:h + 1], 1.0, ALU.mult, ALU.mult), t)

            g = pscale(u, h)
            return finish

        def blocks(n, u, tp):
            qt = u[-1]
            P = PB[n % 2]
            pts = {}

            def tr(j):
                ti, tp_, tf = t_r.take()
                for h in range(nh):
                    t = pe(lambda e, h=h: e.transpose(tp_[:, h * 128:h * 128 + 128], P[:, h, j * 128:j * 128 + 128],
                                                      self.ident), tp[h], tf, mark=(h == nh - 1))
                pi, PT, pf = PTr.take()
                evac[0] += 1
                w = nh * 128
                if evac[0] % 2:
                    t2 = act(lambda e: e.activation(PT, tp_[:, :w], ACT.Copy), t, pf)
                else:
                    t2 = dve(lambda e: e.tensor_copy(PT, tp_[:, :w]), t, pf)
                t_r.done(ti, t2)
                pts[j] = (pi, PT, t2)
                if j == qt:
                    pfree[n % 2] = [t]

            def mul(j):
                pi, PT, t2 = pts[j]
                t = pv(u, j, PT, t2)
                PTr.done(pi, t)

            steps = [lambda j=j: tr(j) for j in range(qt + 1)]
            out = steps[:2]
            for j in range(qt + 1):
                out += steps[j + 2:j + 3]
                out.append(lambda j=j: mul(j))
            return out

        rest, ready, fin = [], [], lambda: None
        for n, u in enumerate(units):
            tp = []
            for h in range(nh):
                nxt = scores(n, u, h)
                fin()
                self.flush()
                fin = lambda nxt=nxt, tp=tp: tp.append(nxt())
                if h == 0:
                    for f in rest:
                        f()
                    k = min(2, len(ready) // 2) if nh > 1 else 0
                    now, rest = ready[:len(ready) - k], ready[len(ready) - k:]
                if h > 0 or nh == 1:
                    for _ in range(-(-len(now) // max(nh - h, 1))):
                        now.pop(0)()
            ready = blocks(n, u, tp)
        fin()
        for f in rest:
            f()
        self.flush()
        for f in ready:
            f()
        self.flush()

    def layer0(self, X, XNT):
        pe, act, dve, pool = self.pe, self.act, self.dve, self.pool
        I = self.ins
        Wq, Wa, Wb = (self.sb(WA0 + 1024 * i, 2, 512) for i in range(3))
        Wv = self.sb(WA0 + 3072, 2, 256)
        Wo = self.sb(WA0 + 4096, 4, 256)
        Tq, Tc, Ts = (self.sb(WA0 + 5120 + 1024 * i, 1024) for i in range(3))
        tmp = Ring([self.sb(WA0 + 8192 + 512 * i, 512) for i in range(2)])
        Wgu = self.sb(WF0, 2, 2048)
        Wd = self.sb(WF0 + 4096, 8, 256)
        tw = [self.dma("w_a", Wq, I["l0_wq"]), self.dma("w_a", Wa, I["l0_wa"]), self.dma("w_a", Wb, I["l0_wb"]),
              self.dma("w_a", Wv, I["l0_wv"]), self.dma("w_a", Wo, I["l0_wo"]), self.dma("w_a", Tq, I["l0_tq"]),
              self.dma("w_a", Tc, I["l0_tc"]), self.dma("w_a", Ts, I["l0_ts"])][-1:]
        tf = [self.dma("w_f", Wgu, I["l0_wgu"]), self.dma("w_f", Wd, I["l0_wd"])][-1:]
        self.norm(X, XNT)
        self.barrier()
        Q = self.sb(WK0, 4, 1024)
        Kt = self.sb(WK0 + 4096, 1024)
        V = self.sb(WK0 + 5120, 8, 16, 32)
        aT = self.sb(WK0 + 9216, 4, 1024)
        work = WK0 + 13312
        s_r = Banks(self.PS[:, 0:4, :].rearrange("p a b -> p (a b)"), 4)
        t_r = Ring([self.PS[:, i, :] for i in (4, 5, 6)])
        o_r = Ring([self.PS[:, 7, :]])
        t_one = pool(lambda e: e.memset(V[:, :, :, 16:32], 0.0))
        t_zero = pool(lambda e: e.memset(Q, 0.0))
        state = {}

        def make_qk(b, ht):
            free = state.get("qfree")
            done = []
            for tt in range(2):
                tok = slice(b * 1024 + tt * 512, b * 1024 + tt * 512 + 512)
                o = slice(tt * 512, tt * 512 + 512)
                W = slice(ht * 128, ht * 128 + 128)
                si, s, sf = s_r.take()
                ta = self.proj(s[:, 0:512], lambda k: Wa[:, k, W], lambda k: XNT[:, k, tok], 512, 2, sf, tw)
                tb = self.proj(s[:, 512:1024], lambda k: Wb[:, k, W], lambda k: XNT[:, k, tok], 512, 2, sf, tw)
                ti, tm, tf_ = tmp.take()
                t1 = dve(lambda e, s=s, o=o: e.tensor_tensor(Kt[:, o], s[:, 0:512], Tc[:, o], ALU.mult), ta, free)
                t2 = dve(lambda e, s=s, o=o, tm=tm: e.tensor_tensor(tm, s[:, 512:1024], Ts[:, o], ALU.mult), tb, tf_)
                t3 = pool(lambda e, o=o, tm=tm: e.tensor_tensor(Kt[:, o], Kt[:, o], tm, ALU.add), t1, t2)
                s_r.done(si, t2)
                tmp.done(ti, t3)
                si, s, sf = s_r.take(False)
                t = self.proj(s[:, 0:512], lambda k: Wq[:, k, W], lambda k: XNT[:, k, tok], 512, 2, sf, tw)
                for h in range(4):
                    r = slice(32 * h, 32 * h + 32)
                    t4 = dve(lambda e, s=s, o=o, r=r, h=h: e.tensor_tensor(Q[r, h, o], s[r, 0:512], Tq[r, o],
                                                                          ALU.mult), t, t_zero, free)
                s_r.done(si, t4)
                done += [t3, t4]
            state[(b, ht)] = done

        def make_v(b):
            for i in range(8):
                oi, o, of = t_r.take()
                tok = slice(b * 1024 + i * 128, b * 1024 + i * 128 + 128)
                t = self.proj(o[:, 0:256], lambda k: XNT[:, k, tok], lambda k: Wv[:, k, :], 256, 2, of, tw)
                t = act(lambda e, o=o, i=i: e.activation(V[:, i, :, 0:16],
                        o[:, 0:256].rearrange("p (h d) -> p h d", h=16), ACT.Copy), t, state.get("vfree"))
                t_r.done(oi, t)
            state["v"] = t

        cur = {}

        def score(u, h):
            b, ht, qt = u
            if (b, ht) not in state:
                make_qk(b, ht)
            return Q[:, h, qt * 128:qt * 128 + 128], lambda c0, c1: Kt[:, c0:c1], state[(b, ht)]

        def after_score(u, h, t):
            if u[-1] == 7 and h == 3:
                state["qfree"] = t

        def pv(u, j, PT, t2):
            b, ht, qt = u
            if j == 0:
                cur["o"] = o_r.take()
            oi, o, of = cur["o"]
            for h in range(4):
                t = pe(lambda e, h=h: e.matmul(o[32 * h:32 * h + 32, 0:128], V[:, j, ht * 4 + h, :],
                                               PT[:, h * 128:h * 128 + 128], start=(j == 0), stop=(j == qt)),
                       t2, of, state["v"], t_one, mark=(h == 3))
            if j == qt:
                tc = act(lambda e: e.activation(aT[:, ht, qt * 128:qt * 128 + 128], o[:, 0:128], ACT.Copy), t,
                         state.get("afree"))
                o_r.done(oi, tc)
                state["a"] = tc
                if qt == 7 and ht == 3:
                    state["vfree"] = t
                    out_proj(b)
            return t

        def out_proj(b):
            t = self.project_add(X, b * 8, 8, t_r, lambda i, k: aT[:, k, i * 128:i * 128 + 128],
                                 lambda k: Wo[:, k, :], 4, state["a"])
            state["afree"] = t
            if b == 0:
                make_v(1)

        make_v(0)
        units = [(b, ht, qt) for b in range(2) for ht in range(4) for qt in range(8)]
        self.attend(units, 4, work, score, 1.0, lambda u, h: None, pv, (s_r, t_r), 3, after_score)
        self.barrier()
        self.ffn(X, XNT, 8, lambda k, f: Wgu[:, k, f * 128:f * 128 + 128],
                 lambda k, f: Wgu[:, k, 1024 + f * 128:1024 + f * 128 + 128], lambda k: Wd[:, k, :],
                 lambda f: 128, ACT.Silu, WK0, tf)
        self.barrier()

    def layer1(self, X, XNT):
        pe, act, dve, pool = self.pe, self.act, self.dve, self.pool
        I = self.ins
        Wq = self.sb(WA0, 2, 2048)
        Wk, Wv = self.sb(WA0 + 4096, 2, 512), self.sb(WA0 + 5120, 2, 512)
        Wo = self.sb(WA0 + 6144, 16, 256)
        Tc, Ts = self.sb(WA0 + 10240, 1024), self.sb(WA0 + 11264, 1024)
        Wg = self.sb(WA0 + 12288, 2, 32)
        tmp = Ring([self.sb(EX0 + 512 * i, 512) for i in range(2)])
        Wgu = self.sb(WF0, 2, 2048)
        Wd = self.sb(WF0 + 4096, 8, 256)
        for dst, src in ((Wq, "l1_wq"), (Wk, "l1_wk"), (Wv, "l1_wv"), (Wo, "l1_wo"), (Tc, "l1_tc"), (Ts, "l1_ts"),
                         (Wg, "l1_wg")):
            tw = self.dma("w_a", dst, I[src])
        self.dma("w_f", Wgu, I["l1_wgu"])
        tf = self.dma("w_f", Wd, I["l1_wd"])
        self.norm(X, XNT)
        self.barrier()
        Q = self.sb(WK0, 4, 1024)
        Kt = self.sb(WK0 + 4096, 1024)
        V = self.sb(WK0 + 5120, 8, 512)
        aT = self.sb(WK0 + 9216, 4, 1024)
        G = self.sb(WK0 + 13312, 16, 16)
        work = WK0 + 13568
        s_r = Banks(self.PS[:, 0:4, :].rearrange("p a b -> p (a b)"), 4)
        t_r = Ring([self.PS[:, i, :] for i in (4, 5, 6)])
        o_r = Ring([self.PS[:, 7, :]])
        state, cur = {}, {}
        sg = self.sb(work, 16, 32)
        for i in range(NT):
            oi, o, of = t_r.take()
            t = self.proj(o[:, 0:32], lambda k: XNT[:, k, i * 128:i * 128 + 128], lambda k: Wg[:, k, :], 32, 2, of, tw)
            t = act(lambda e, o=o, i=i: e.activation(sg[:, i, :], o[:, 0:32], ACT.Sigmoid), t)
            t_r.done(oi, t)
        tg = dve(lambda e: e.tensor_tensor(G, sg[:, :, 0:16], sg[:, :, 16:32], ALU.add), t)
        state["sg"] = tg
        act.wait([tg])

        scale = float(np.float32(1.0) / np.sqrt(np.float32(128.0)))

        def rotate(W, dst, b, tt, *free):
            tok = slice(b * 1024 + tt * 512, b * 1024 + tt * 512 + 512)
            o = slice(tt * 512, tt * 512 + 512)
            si, s, sf = s_r.take(False)
            t = self.proj(s[:, 0:512], W, lambda k: XNT[:, k, tok], 512, 2, sf, tw)
            ti, tm, tf_ = tmp.take()
            t1 = dve(lambda e: e.tensor_tensor(dst[:, o], s[:, 0:512], Tc[:, o], ALU.mult), t, *free)
            dve(lambda e: e.tensor_tensor(tm[0:64, :], s[64:128, 0:512], Ts[64:128, o], ALU.mult), t, tf_)
            t2 = dve(lambda e: e.tensor_tensor(tm[64:128, :], s[0:64, 0:512], Ts[0:64, o], ALU.mult), t, tf_)
            t3 = pool(lambda e: e.tensor_tensor(dst[:, o], dst[:, o], tm, ALU.add), t1, t2)
            s_r.done(si, t2)
            tmp.done(ti, t3)
            return t3

        def make_qk(b, g):
            free = state.get("qfree")
            done = []
            for tt in range(2):
                done.append(rotate(lambda k: Wk[:, k, g * 128:g * 128 + 128], Kt, b, tt, free))
                o = slice(tt * 512, tt * 512 + 512)
                done.append(pool(lambda e, o=o: e.tensor_scalar(Kt[:, o], Kt[:, o], scale, 1.0, ALU.mult, ALU.mult),
                                 done[-1]))
                for h in range(4):
                    c = (g * 4 + h) * 128
                    done.append(rotate(lambda k: Wq[:, k, c:c + 128], Q[:, h, :], b, tt, free))
            state[(b, g)] = done

        def make_v(b):
            for i in range(8):
                oi, o, of = t_r.take()
                tok = slice(b * 1024 + i * 128, b * 1024 + i * 128 + 128)
                t = self.proj(o, lambda k: XNT[:, k, tok], lambda k: Wv[:, k, :], 512, 2, of, tw)
                t = act(lambda e, o=o, i=i: e.activation(V[:, i, :], o, ACT.Copy), t, state.get("vfree"))
                t_r.done(oi, t)
            state["v"] = t

        def score(u, h):
            b, g, qt = u
            if (b, g) not in state:
                make_qk(b, g)
            return Q[:, h, qt * 128:qt * 128 + 128], lambda c0, c1: Kt[:, c0:c1], state[(b, g)]

        def after_score(u, h, t):
            if u[-1] == 7 and h == 3:
                state["qfree"] = t

        def pv(u, j, PT, t2):
            b, g, qt = u
            if j == 0:
                cur["o"] = o_r.take()
            oi, o, of = cur["o"]
            t = pe(lambda e: e.matmul(o, V[:, j, g * 128:g * 128 + 128], PT, start=(j == 0), stop=(j == qt)),
                   t2, of, state["v"])
            if j == qt:
                dst = aT[:, :, qt * 128:qt * 128 + 128]
                ta = act(lambda e: e.activation(dst, o.rearrange("p (h q) -> p h q", h=4), ACT.Copy), t,
                         state.get("afree"))
                o_r.done(oi, ta)
                state["a"] = ta
                if qt == 7:
                    if g == 3:
                        state["vfree"] = t
                    out_proj(b, g)
            return t

        def out_proj(b, g):
            t = self.project_add(X, b * 8, 8, t_r, lambda i, k: aT[:, k, i * 128:i * 128 + 128],
                                 lambda k: Wo[:, g * 4 + k, :], 4, state["a"])
            state["afree"] = t
            if (b, g) == (0, 3):
                make_v(1)

        make_v(0)
        units = [(b, g, qt) for b in range(2) for g in range(4) for qt in range(8)]
        self.attend(units, 4, work, score, 1.0,
                    lambda u, h: G[:, u[0] * 8 + u[2], u[1] * 4 + h:u[1] * 4 + h + 1], pv, (s_r, t_r), 3, after_score)
        self.barrier()
        self.ffn(X, XNT, 8, lambda k, f: Wgu[:, k, f * 128:f * 128 + 128],
                 lambda k, f: Wgu[:, k, 1024 + f * 128:1024 + f * 128 + 128], lambda k: Wd[:, k, :],
                 lambda f: 128, ACT.Silu, WK0, tf)
        self.barrier()

    def layer2(self, X, XNT):
        pe, act, dve, pool = self.pe, self.act, self.dve, self.pool
        I = self.ins
        Win = self.sb(WA0, 2, 4640)
        Wout = self.sb(WA0 + 9280, 16, 256)
        W12 = self.sb(WA0 + 13376, 2, 1408)
        W3 = self.sb(WA0 + 16192, 6, 256)
        Crep = self.sb(WA0 + 17728, 1024)
        sel = Ring([self.sb(WA0 + 18752 + 128 * i, 128) for i in range(2)])
        ident4 = self.sb(EX0, 512)
        dt = self.sb(EX0 + 512, 16, 32)
        vec = self.sb(self.misc, 204)
        mup, bin_, cw, cb, Dv, nw = (vec[:, 0:36], vec[:, 36:72], vec[:, 72:152], vec[:, 152:172], vec[:, 172:188],
                                     vec[:, 188:204])
        bm = self.sb(self.misc + 204, 36)
        dv = self.sb(self.misc + 240, 4, 32)
        bout = self.sb(WK0 + 20000, 256)
        for dst, src in ((Win, "l2_win"), (Wout, "l2_wout"), (vec, "l2_vec"), (dv, "l2_dt"), (bout, "l2_bout")):
            tw = self.dma("w_a", dst, I[src])
        self.norm(X, XNT)
        for i in range(4):
            pool(lambda e, i=i: e.tensor_copy(ident4[:, i * 128:i * 128 + 128], self.ident))
        for i in range(NT):
            tx = pool(lambda e, i=i: e.tensor_tensor(X[:, i, :], X[:, i, :], bout, ALU.add), tw, dve.last())
        tbm = dve(lambda e: e.tensor_tensor(bm, bin_, mup, ALU.mult), tw)
        self.barrier()
        BC = self.sb(WK0, 4, 1024)
        BT = self.sb(WK0 + 4096, 8, 256)
        RAW = self.sb(WK0 + 6144, 2, 1032)
        XCs = [self.sb(WA0 + 13376, 2, 1024), self.sb(WK0 + 8208, 2, 1024)]
        sqR = Ring([self.sb(WA0 + 16192 + 512 * i, 512) for i in range(2)])
        rsR = Ring([self.sb(EX0 + 1024 + 8 * i, 8) for i in range(2)])
        self.mhalf = self.sb(EX0 + 1048, 8)
        pool(lambda e: e.memset(self.mhalf, -0.5))
        XD = self.sb(WK0 + 10256, 8, 256)
        LT = self.sb(WK0 + 12304, 4, 8, 128)
        Y = self.sb(WK0 + 16400, 2, 1024)
        CP = self.sb(WK0 + 18448, 1024)
        R = self.sb(WK0 + 19472, 2048)
        Zr = Ring([self.sb(WK0 + 21520 + 512 * i, 512) for i in range(2)])
        Bd = Ring([self.sb(WK0 + 22544 + 128 * i, 4, 32) for i in range(2)])
        Hb = Ring([self.sb(WK0 + 22800 + 256 * i, 256) for i in range(2)])
        ach = self.sb(self.misc + 368, 8)
        aR = Ring([self.PS[:, i, :] for i in (0, 1)])
        bR = Ring([self.PS[:, i, :] for i in (2, 3)])
        sR = Ring([self.PS[:, i, 0:64] for i in (4, 7)])
        yR = Ring([self.PS[:, i, :] for i in (5, 6)])

        ai, ap_, af = aR.take()
        for i in range(NT):
            t = self.proj(ap_[:, i * 32:i * 32 + 32], lambda k: XNT[:, k, i * 128:i * 128 + 128],
                          lambda k: Win[:, k, 4608:4640], 32, 2, tw)
        W = [self.sb(WK0 + 512 * i, 16, 32) for i in range(6)]
        wide = lambda r: dv[:, r:r + 1, :].broadcast_to([128, 16, 32])
        pv3 = ap_.rearrange("p (a b) -> p a b", a=16)
        t = dve(lambda e: e.tensor_tensor(W[0], pv3, wide(0), ALU.add), t)
        aR.done(ai, t)
        t = dve(lambda e: e.tensor_tensor(W[0], W[0], wide(1), ALU.mult), t)
        tv = dve(lambda e: e.tensor_tensor(W[0], W[0], wide(2), ALU.add), t)
        t = dve(lambda e: e.tensor_scalar(W[1], W[0], -1.0, None, ALU.mult), tv)
        t = dve(lambda e: e.tensor_tensor(W[1], W[0], W[1], ALU.min), t)
        te = act(lambda e: e.activation(W[2], W[1], ACT.Exp), t)
        tA = act(lambda e: e.activation(dv[:, 3, :], dv[:, 3, :], ACT.Exp), tw)
        t = dve(lambda e: e.tensor_scalar(W[3], W[2], 2.0, None, ALU.add), te)
        t = dve(lambda e: e.reciprocal(W[3], W[3]), t)
        ts = dve(lambda e: e.tensor_tensor(W[3], W[2], W[3], ALU.mult), t)
        tz = dve(lambda e: e.tensor_tensor(W[4], W[3], W[3], ALU.mult), ts)
        t = dve(lambda e: e.tensor_scalar(W[5], W[4], 2.0 / 17.0, 2.0 / 15.0, ALU.mult, ALU.add), tz)
        for n in (13, 11, 9, 7, 5, 3, 1):
            t = dve(lambda e: e.tensor_tensor(W[5], W[5], W[4], ALU.mult), t)
            t = dve(lambda e, n=n: e.tensor_scalar(W[5], W[5], 2.0 / n, None, ALU.add), t)
        t = dve(lambda e: e.tensor_tensor(W[5], W[5], W[3], ALU.mult), t)
        t2 = dve(lambda e: e.tensor_scalar(W[0], W[0], 0.0, None, ALU.max), tv)
        tdt = dve(lambda e: e.tensor_tensor(dt, W[0], W[5], ALU.add), t, t2)
        t = dve(lambda e: e.tensor_tensor(W[1], dt, wide(3), ALU.mult), tdt, tA)
        t = act(lambda e: e.activation(W[1], W[1], ACT.Exp, scale=-1.0), t)
        for j in range(4):
            bi, bp, bf = bR.take()
            for i in range(4):
                t2 = pe(lambda e, i=i, bp=bp, j=j: e.transpose(bp[0:32, i * 128:i * 128 + 128], W[1][:, j * 4 + i, :],
                                                              self.ident), t, bf)
            t3 = dve(lambda e, bp=bp, j=j: e.tensor_copy(R[0:32, j * 512:j * 512 + 512], bp[0:32, :]), t2)
            bR.done(bi, t3)
        for c in range(16):
            o = slice(c * 128, c * 128 + 128)
            t = dve(lambda e, o=o: e.tensor_tensor_scan(R[32:64, o], R[0:32, o], self.ones[0:32, :], 1.0, ALU.mult,
                                                        ALU.mult), t3)
        tR = dve(lambda e: e.memset(R[0:32, 0:2048:128], 0.0), t)
        dve(lambda e: e.memset(R[64:128, :], 0.0))
        for k in range(16):
            dve(lambda e, k=k: e.tensor_scalar(Wout[:, k, :], Wout[:, k, :], nw[:, k:k + 1], None, ALU.mult), tw)
        for h in Hb.bufs:
            pool(lambda e, h=h: e.memset(h, 0.0))
        tpad = pool(lambda e: e.memset(RAW[:, :, 0:3], 0.0))
        self.barrier()

        def raw(col, tile, slot, b, *free):
            for tt in range(2):
                tok = slice(b * 1024 + tt * 512, b * 1024 + tt * 512 + 512)
                ai, p, af = aR.take()
                t = self.proj(p, lambda k: Win[:, k, col:col + 128], lambda k: XNT[:, k, tok], 512, 2, af)
                t = act(lambda e, p=p, tt=tt: e.activation(RAW[:, slot, 3 + tt * 512:3 + tt * 512 + 512], p,
                        ACT.Identity, scale=mup[:, tile:tile + 1], bias=bm[:, tile:tile + 1]), t, *free)
                aR.done(ai, t)
            return t

        def conv(slot, ct, dst, t, *free):
            t = pool(lambda e: e.tensor_scalar(dst, RAW[:, slot, 0:1024], cw[:, ct * 4:ct * 4 + 1], 1.0, ALU.mult,
                                               ALU.mult), t, *free)
            for k in range(1, 4):
                t = dve(lambda e, k=k: e.scalar_tensor_tensor(dst, RAW[:, slot, k:k + 1024],
                        cw[:, ct * 4 + k:ct * 4 + k + 1], dst, ALU.mult, ALU.add), t)
            return t, act(lambda e: e.activation(dst, dst, ACT.Silu, bias=cb[:, ct:ct + 1]), t)

        def merge(*lists):
            steps = [((i + 0.5) / len(l), n, f) for n, l in enumerate(lists) for i, f in enumerate(l)]
            for _, _, f in sorted(steps, key=lambda s: (s[0], s[1])):
                f()

        rfree = [None, None]
        last, S_ = {}, {}
        sg_t = {}

        def conv_bc(b):
            tbc = []
            for n in range(4):
                s = n % 2
                t = raw(4096 + n * 128, 32 + n, s, b, rfree[s])
                rfree[s], t = conv(s, 16 + n, BC[:, n, :], t, last.get("bc"))
                tbc.append(t)
            for c in range(8):
                bi, bp, bf = bR.take()
                for n in range(2):
                    t = pe(lambda e, n=n, bp=bp, c=c: e.transpose(bp[:, n * 128:n * 128 + 128],
                           BC[:, n, c * 128:c * 128 + 128], self.ident), tbc[n], bf)
                tbt = act(lambda e, bp=bp, c=c: e.activation(BT[:, c, :], bp[:, 0:256], ACT.Copy), t, last.get("bc"))
                bR.done(bi, tbt)
            S_["bc"], S_["bt"] = tbc, tbt

        def conv_x(b, g):
            XC = XCs[g % 2]
            out = []
            S_["xc", b, g] = tcx = []

            def one(s):
                tile = 2 * g + s
                t = raw(2048 + tile * 128, 16 + tile, s, b, rfree[s])
                S_["raw", s] = t

            def two(s):
                rfree[s], t = conv(s, 2 * g + s, XC[:, s, :], S_["raw", s], last.get(("xc", g % 2)))
                tcx.append(t)

            return [lambda: one(0), lambda: one(1), lambda: two(0), lambda: two(1)]

        def prep(b, g, c4):
            XC, tcx = XCs[g % 2], S_["xc", b, g]
            gg, ct = g % 4, 2 + g // 4
            o = slice(b * 1024 + c4 * 512, b * 1024 + c4 * 512 + 512)
            w5 = slice(c4 * 512, c4 * 512 + 512)
            out = []

            def load():
                q = slice(32 * gg, 32 * gg + 32)
                for r in range(4):
                    S_["crep"] = self.dma("crep%d" % c4, Crep[32 * r:32 * r + 32, w5], BC[q, ct, w5], S_["bc"],
                                          last.get(("crep", c4)))
                if c4 == 0:
                    gi, sg, gf = sel.take()
                    S_["sg"] = (gi, sg, pool(lambda e: e.tensor_copy(sg.rearrange("p (a b) -> p a b", a=4),
                        self.ident[:, 32 + 4 * g:36 + 4 * g].unsqueeze(2).broadcast_to([128, 4, 32])), gf))

            def scan(h):
                bi, bp, bf = bR.take()
                hh = 4 * g + h
                t = pe(lambda e: e.matmul(bp, self.ident[:, hh:hh + 1].broadcast_to([128, 128]), R[:, o], start=True,
                                          stop=True), bf)
                tl = dve(lambda e: e.tensor_tensor_scan(LT[:, h, c4 * 4:c4 * 4 + 4, :].rearrange("p a b -> p (a b)"),
                         bp, ident4, 0.0, ALU.mult, ALU.add), t, last.get(("main", c4)))
                bR.done(bi, tl)
                S_["tl", c4] = tl

            def cp():
                gi, sg, tsg = S_["sg"]
                tc = S_["crep"]
                bi, bp, bf = bR.take()
                t = pe(lambda e: e.matmul(bp, sg, R[:, o], start=True, stop=True), tsg, bf)
                sel.done(gi, t)
                dve(lambda e: e.tensor_copy(ach[:, c4 * 4:c4 * 4 + 4], bp[:, 127:512:128]), t, last.get(("main", c4)))
                tcp = dve(lambda e: e.tensor_tensor(CP[:, w5], Crep[:, w5], bp, ALU.mult), t, tc,
                          last.get(("main", c4)))
                bR.done(bi, tcp)
                last["crep", c4] = tcp
                S_["tcp", c4] = tcp

            def xd(c):
                bi, bp, bf = bR.take()
                for s in range(2):
                    t = pe(lambda e, s=s: e.transpose(bp[:, s * 128:s * 128 + 128], XC[:, s, c * 128:c * 128 + 128],
                                                      self.ident), tcx[s], bf)
                t = dve(lambda e: e.tensor_tensor(
                    XD[:, c, :].rearrange("p (h d) -> p h d", h=4), bp[:, 0:256].rearrange("p (h d) -> p h d", h=4),
                    dt[:, b * 8 + c, 4 * g:4 * g + 4].unsqueeze(2).broadcast_to([128, 4, 64]), ALU.mult), t,
                    last.get(("main", c4)))
                bR.done(bi, t)
                S_["txd", c] = t

            out = [load]
            for k in range(4):
                out += [lambda k=k: scan(k), lambda k=k: xd(4 * c4 + k)]
            return out + [cp]

        def main(b, g, c4):
            XC = XCs[g % 2]
            bt, ct = g // 4, 2 + g // 4
            q = slice(32 * (g % 4), 32 * (g % 4) + 32)
            L = {}

            def begin():
                L["y"] = [yR.take(), yR.take()]
                if c4 == 0:
                    S_["h"] = None

            def one(c):
                o = slice(c * 128, c * 128 + 128)
                di, bd, df = Bd.take()
                tl, tbt = S_["tl", c4], S_["bt"]
                tbd = dve(lambda e: e.tensor_tensor(bd, BT[:, c, 32 * g:32 * g + 32].unsqueeze(1).broadcast_to(
                    [128, 4, 32]), LT[:, :, c, 127:128].broadcast_to([128, 4, 32]), ALU.mult), tl, tbt, df)
                bi, bp, bf = bR.take()
                t = pe(lambda e: e.matmul(bp[:, 0:128], BC[q, bt, o], BC[q, ct, o], start=True, stop=True), bf,
                       S_["bc"])
                tm = dve(lambda e: e.tensor_tensor(LT[:, :, c, :], LT[:, :, c, :],
                         bp[:, 0:128].unsqueeze(1).broadcast_to([128, 4, 128]), ALU.mult), t, tbd)
                bR.done(bi, tm)
                L["tm", c] = tm
                if c < 7:
                    si, sp_, sf = sR.take()
                    for h in range(4):
                        tS = pe(lambda e, h=h: e.matmul(sp_[32 * h:32 * h + 32, :], bd[:, h, :],
                                XD[:, c, h * 64:h * 64 + 64], start=True, stop=True), tbd, S_["txd", c], sf,
                                mark=(h == 3))
                    Bd.done(di, tS)
                    L["s", c] = (si, sp_, tS)
                else:
                    Bd.done(di, tbd)

            def two(c):
                o = slice(c * 128, c * 128 + 128)
                w = slice((c % 4) * 128, (c % 4) * 128 + 128)
                hcur, tm, tcp = S_["h"], L["tm", c], S_["tcp", c4]
                for s in range(2):
                    y, yf = L["y"][s][1], L["y"][s][2]
                    if c > 0:
                        pe(lambda e, s=s, y=y: e.matmul(y[:, w], hcur[0][:, s * 128:s * 128 + 128], CP[:, o],
                           start=True, stop=True, skip_group_check=True), hcur[1], tcp, yf, mark=False)
                    for k in range(2):
                        h = 2 * s + k
                        t = pe(lambda e, h=h, k=k, y=y: e.matmul(y[64 * k:64 * k + 64, w],
                               XD[:, c, h * 64:h * 64 + 64], LT[:, h, c, :], start=(c == 0), stop=True,
                               skip_group_check=True), tm, S_["txd", c], yf, mark=(h == 3))
                if hcur:
                    Hb.done(hcur[2], t)
                if c < 7:
                    si, sp_, tS = L["s", c]
                    hi, hn, hf = Hb.take()
                    for h in range(4):
                        qq, cc = slice(32 * h, 32 * h + 32), slice(64 * h, 64 * h + 64)
                        if c == 0:
                            th = dve(lambda e, qq=qq, cc=cc: e.tensor_copy(hn[qq, cc], sp_[qq, :]), tS, hf)
                        else:
                            th = dve(lambda e, qq=qq, cc=cc: e.scalar_tensor_tensor(hn[qq, cc], hcur[0][qq, cc],
                                     ach[qq, c:c + 1], sp_[qq, :], ALU.mult, ALU.add), tS, hf, hcur[1])
                    sR.done(si, th)
                    S_["h"] = (hn, th, hi)
                L["t"] = last["main", c4] = t

            def gate(s):
                tile = 2 * g + s
                tok = slice(b * 1024 + c4 * 512, b * 1024 + c4 * 512 + 512)
                ai, p, af = aR.take()
                tz = self.proj(p, lambda k: Win[:, k, tile * 128:tile * 128 + 128], lambda k: XNT[:, k, tok], 512, 2,
                               af)
                zi, z, zf = Zr.take()
                tz = act(lambda e: e.activation(z, p, ACT.Silu, scale=mup[:, tile:tile + 1], bias=bm[:, tile:tile + 1]),
                         tz, zf)
                aR.done(ai, tz)
                L["z", s] = (zi, z, tz)

            def end(s):
                w5 = slice(c4 * 512, c4 * 512 + 512)
                tile = 2 * g + s
                zi, z, tz = L["z", s]
                yi, y, _ = L["y"][s]
                t1 = dve(lambda e: e.scalar_tensor_tensor(Y[:, s, w5], XC[:, s, w5], Dv[:, tile:tile + 1], y, ALU.mult,
                                                          ALU.add), L["t"], last.get(("y", c4)))
                yR.done(yi, t1)
                t2 = dve(lambda e: e.tensor_tensor(Y[:, s, w5], Y[:, s, w5], z, ALU.mult), t1, tz)
                Zr.done(zi, t2)
                S_["fin", c4, s] = t2
                last["xc", g % 2] = t1
                if (b, g, c4, s) == (1, 6, 1, 1):
                    self.dma("w_f", W12, I["l2_w12"], t1)

            k = 4 * c4
            return [begin, lambda: one(k), lambda: gate(0), lambda: one(k + 1), lambda: two(k), lambda: gate(1),
                    lambda: one(k + 2), lambda: two(k + 1), lambda: one(k + 3), lambda: two(k + 2), lambda: two(k + 3),
                    lambda: end(0), lambda: end(1)]

        def final(b, g, c4):
            w5 = slice(c4 * 512, c4 * 512 + 512)
            L = {}

            def square(s):
                qi, sq, qf = sqR.take()
                L["q", s] = (qi, sq, act(lambda e: e.activation(sq, Y[:, s, w5], ACT.Square), S_["fin", c4, s], qf))

            def var():
                ai, p, af = aR.take()
                for i in range(4):
                    for s in range(2):
                        qi, sq, tq = L["q", s]
                        t = pe(lambda e, i=i, s=s, sq=sq: e.matmul(p[:, 2 * i:2 * i + 2],
                               sq[:, i * 128:i * 128 + 128], self.ones[:, 0:2], start=(s == 0), stop=(s == 1)), tq, af)
                for s in range(2):
                    sqR.done(L["q", s][0], t)
                ri, r, rf = rsR.take()
                t = dve(lambda e: e.tensor_scalar(r, p[:, 0:8], 1.0 / 256.0, 1e-5, ALU.mult, ALU.add), t, rf)
                aR.done(ai, t)
                t = pool(lambda e: e.tensor_tensor(r, r, self.mhalf, ALU.pow), t)
                L["r"] = (ri, r, t)

            def out(i):
                ri, r, tr = L["r"]
                ai, p, af = aR.take()
                ty = [S_["fin", c4, 0], S_["fin", c4, 1]]
                for j in range(2):
                    c = c4 * 512 + (i + j) * 128
                    t = self.proj(p[:, j * 256:j * 256 + 256], lambda k: Y[:, k, c:c + 128],
                                  lambda k: Wout[:, 2 * g + k, :], 256, 2, af, ty)
                for j in range(2):
                    x = X[:, b * 8 + c4 * 4 + i + j, :]
                    t2 = dve(lambda e, x=x, j=j: e.scalar_tensor_tensor(x, p[:, j * 256:j * 256 + 256],
                             r[:, 2 * (i + j):2 * (i + j) + 1], x, ALU.mult, ALU.add), t, tr)
                aR.done(ai, t2)
                last["y", c4] = t
                if i == 2:
                    rsR.done(ri, t2)

            return [lambda: square(0), lambda: square(1), var, lambda: out(0), lambda: out(2)]

        halves = [(b, g, c4) for b in range(2) for g in range(8) for c4 in range(2)]
        for n, (b, g, c4) in enumerate(halves):
            if (g, c4) == (0, 0):
                last["bc"] = [last.get(k) for k in (("main", 1), ("crep", 0), ("crep", 1))]
                conv_bc(b)
                if b == 0:
                    merge(conv_x(b, g))
                merge(prep(b, g, 0))
            nxt = halves[n + 1] if n + 1 < len(halves) else None
            lists = [main(b, g, c4)]
            if nxt and nxt != (1, 0, 0):
                lists.append(prep(*nxt))
            if c4 == 0 and n + 2 < len(halves):
                lists.append(conv_x(*halves[n + 2][:2]))
            if n:
                lists.append(final(*halves[n - 1]))
            merge(*lists)
        merge(final(*halves[-1]))
        self.barrier()
        st = self.sb(WK0, 8)
        tmp = self.sb(WK0 + 512, 1408)
        ps = Ring([self.PS[:, i, :] for i in (0, 1)])
        tf = self.dma("w_f", W3, I["l2_w3"])
        dve.wait([tf])
        for n, w in enumerate((W12[:, :, 0:704], W12[:, :, 704:1408], W3)):
            cols = 768 if n == 2 else 704
            axis = AX.XY
            t = dve(lambda e, n=n, w=w: e.tensor_reduce(st[:, n:n + 1], w, AX.XY, ALU.add, apply_absolute_value=True))
            pi, p, pf = ps.take()
            t = pe(lambda e, n=n, p=p: e.matmul(p[:, 0:1], self.ones, st[:, n:n + 1], start=True, stop=True), t, pf)
            t = dve(lambda e, p=p: e.tensor_scalar(st[:, 3:4], p[:, 0:1], 1.0 / 180224.0, 1e-8, ALU.mult, ALU.add), t)
            ps.done(pi, t)
            t1 = dve(lambda e: e.tensor_scalar(st[:, 4:5], st[:, 3:4], 0.5, None, ALU.mult), t)
            t2 = dve(lambda e: e.tensor_scalar(st[:, 5:6], st[:, 3:4], -0.5, None, ALU.mult), t)
            a, k = (6, 256) if n == 2 else (2, 704)
            tm = tmp[:, 0:1408] if n < 2 else self.sb(WK0 + 512, 1536)
            tm = tm.rearrange("p (a b) -> p a b", a=a)
            t = dve(lambda e, w=w, tm=tm: e.tensor_scalar(tm, w, st[:, 5:6], None, ALU.is_lt), t1, t2)
            t = dve(lambda e, w=w, tm=tm: e.scalar_tensor_tensor(w, w, st[:, 4:5], tm, ALU.is_gt, ALU.subtract), t)
        self.barrier()
        r = lambda f: 64 if f == 5 else 128
        self.ffn(X, XNT, 6, lambda k, f: W12[:, k, f * 128:f * 128 + r(f)],
                 lambda k, f: W12[:, k, 704 + f * 128:704 + f * 128 + r(f)], lambda k: W3[:, k, :],
                 r, ACT.Sigmoid, WK0, tf)
        self.barrier()

    def layer3(self, X, XNT):
        pe, act, dve, pool = self.pe, self.act, self.dve, self.pool
        I = self.ins
        Wsa = self.sb(WA0, 2, 64)
        Wo = self.sb(WA0 + 128, 2, 256)
        bo = self.sb(WA0 + 640, 256)
        Wr = self.sb(WA0 + 896, 2, 16)
        XN = self.sb(WA0 + 1024, 16, 256)
        QT, KT = self.sb(WA0 + 5120, 2048), self.sb(WA0 + 7168, 2048)
        for dst, src in ((Wsa, "l3_wsa"), (Wo, "l3_wo"), (bo, "l3_bo"), (Wr, "l3_wr")):
            tw = self.dma("w_a", dst, I[src])
        E1 = Ring([self.sb(WF0 + 2048 * i, 2, 512) for i in range(3)])
        E2 = [self.sb(WF0 + 2048 * i + 1024, 4, 256) for i in range(3)]
        te = {}

        def load(e):
            i, w1, free = E1.take()
            self.dma(f"e{i}", w1, I["l3_w1"][:, e], free)
            te[e] = (i, w1, E2[i], self.dma(f"e{i}", E2[i], I["l3_w2"][:, e], free))

        for e in range(3):
            load(e)
        self.norm(X, XNT, XN)
        for i in range(NT):
            pool(lambda e, i=i: e.tensor_tensor(X[:, i, :], X[:, i, :], bo, ALU.add), tw, dve.last())
        self.barrier()
        s_r = Banks(self.PS[:, 0:4, :].rearrange("p a b -> p (a b)"), 4)
        t_r = Ring([self.PS[:, i, :] for i in (4, 5, 6)])
        o_r = Ring([self.PS[:, 7, :]])
        LG = self.sb(WK0, 16, 16)
        M8 = self.sb(WK0 + 256, 16, 8)
        I8 = self.sb(WK0 + 384, 16, 8)
        IF = self.sb(WK0 + 512, 16, 2)
        PR = self.sb(WK0 + 544, 16, 2)
        io = self.sb(WK0 + 576, 16)
        C = self.sb(WK0 + 1024, 16, 16)
        C2 = self.sb(WK0 + 1280, 16, 16)
        oi, o, of = o_r.take()
        for i in range(NT):
            t = self.proj(o[:, i * 16:i * 16 + 16], lambda k: XNT[:, k, i * 128:i * 128 + 128], lambda k: Wr[:, k, :],
                          16, 2, of, tw)
        t = dve(lambda e: e.tensor_copy(LG, o[:, 0:256].rearrange("p (a b) -> p a b", a=16)), t)
        o_r.done(oi, t)
        tio = pool(lambda e: e.iota(io, pattern=[[1, 16]], base=0, channel_multiplier=0,
                                    allow_small_or_imprecise_dtypes=True))
        for i in range(NT):
            t1 = dve(lambda e, i=i: e.max(M8[:, i, :], LG[:, i, :]), t)
            t2 = dve(lambda e, i=i: e.max_index(I8[:, i, :].bitcast(U32), M8[:, i, :], LG[:, i, :]), t1)
        ti = dve(lambda e: e.tensor_copy(IF, I8[:, :, 0:2].bitcast(U32)), t2)
        t = dve(lambda e: e.tensor_tensor(PR[:, :, 1], M8[:, :, 1], M8[:, :, 0], ALU.subtract), t1)
        tx = act(lambda e: e.activation(PR[:, :, 1], PR[:, :, 1], ACT.Exp), t)
        t = dve(lambda e: e.tensor_scalar(PR[:, :, 0], PR[:, :, 1], 1.0, None, ALU.add), tx)
        t = dve(lambda e: e.reciprocal(PR[:, :, 0], PR[:, :, 0]), t)
        tp = dve(lambda e: e.tensor_tensor(PR[:, :, 1], PR[:, :, 1], PR[:, :, 0], ALU.mult), t)
        w3 = [128, 16, 16]
        iob = io.unsqueeze(1).broadcast_to(w3)
        tt_ = []
        for n, c in enumerate((C, C2)):
            t = dve(lambda e, n=n, c=c: e.tensor_tensor(c, iob, IF[:, :, n:n + 1].broadcast_to(w3), ALU.is_equal),
                    ti, tio)
            t = dve(lambda e, n=n, c=c: e.tensor_tensor(c, c, PR[:, :, n:n + 1].broadcast_to(w3), ALU.mult), t, tp)
            tt_.append(t)
        tC = dve(lambda e: e.tensor_tensor(C, C, C2, ALU.add), tt_)
        tq = []
        for tt in range(4):
            si, s, sf = s_r.take()
            k5 = slice(tt * 512, tt * 512 + 512)
            t = self.proj(s[0:64, 0:512], lambda k: Wsa[:, k, :], lambda k: XNT[:, k, k5], 512, 2, sf)
            t1 = act(lambda e, s=s, k5=k5: e.activation(QT[0:32, k5], s[0:32, 0:512], ACT.Copy), t)
            t2 = act(lambda e, s=s, k5=k5: e.activation(KT[0:32, k5], s[32:64, 0:512], ACT.Copy,
                                                        scale=float(np.float32(1.0 / np.sqrt(32)))), t)
            s_r.done(si, t2)
            tq.append(t2)
        work = WK0 + 2048
        nb = Ring([self.sb(WK0 + 8192 + 512 * i, 512) for i in range(2)])
        cur = {}

        def score(u, h):
            b, qt = u
            o = b * 1024
            return (QT[0:32, o + qt * 128:o + qt * 128 + 128], lambda c0, c1: KT[0:32, o + c0:o + c1], tq)

        def pv(u, j, PT, t2):
            b, qt = u
            if j == 0:
                cur["o"] = o_r.take()
            oi, o, of = cur["o"]
            t = pe(lambda e: e.matmul(o[:, 0:256], PT, XN[:, b * 8 + j, :], start=(j == 0), stop=(j == qt)), t2, of)
            if j == qt:
                st = self.sb(self.misc + (qt % 2) * 32, 4, 8)
                ni, n, nf = nb.take()
                tr = dve(lambda e: e.reciprocal(st[:, 2, 0:1], st[:, 1, 0:1]), t)
                ta = dve(lambda e: e.tensor_scalar(n[:, 0:256], o[:, 0:256], st[:, 2, 0:1], None, ALU.mult), tr, nf)
                o_r.done(oi, ta)
                oi, o, of = o_r.take()
                for c in range(2):
                    tb = pe(lambda e, c=c, o=o: e.transpose(o[:, c * 128:c * 128 + 128], n[:, c * 128:c * 128 + 128],
                                                            self.ident), ta, of)
                tc = act(lambda e, o=o: e.activation(n[:, 256:512], o[:, 0:256], ACT.Copy), tb)
                o_r.done(oi, tc)
                oi, o, of = o_r.take()
                td = self.proj(o[:, 0:256], lambda k: n[:, 256 + k * 128:384 + k * 128], lambda k: Wo[:, k, :], 256, 2,
                               of, tc)
                nb.done(ni, td)
                x = X[:, b * 8 + qt, :]
                tf = dve(lambda e, o=o: e.tensor_tensor(x, x, o[:, 0:256], ALU.add), td)
                o_r.done(oi, tf)
            return t

        units = [(b, qt) for b in range(2) for qt in range(8)]
        self.attend(units, 1, work, score, 1.0, None, pv, (s_r, t_r), 4)
        self.barrier()
        self.experts(X, XNT, C, te, load, E1)

    def experts(self, X, XNT, C, te, load, E1):
        pe, act, dve = self.pe, self.act, self.dve
        g_r = Ring([self.PS[:, i, :] for i in range(4)])
        d_r = Ring([self.PS[:, i, :] for i in range(4, 8)])
        H = Ring([self.sb(WK0 + 2048 + 2048 * i, 4, 512) for i in range(3)])

        def up(e_, tt):
            i, w1, w2, tw = te[e_]
            hi, h, hf = H.take()
            tok = slice(tt * 512, tt * 512 + 512)
            ta = []
            for f in range(4):
                gi, g, gf = g_r.take()
                t = self.proj(g, lambda k: w1[:, k, f * 128:f * 128 + 128], lambda k: XNT[:, k, tok], 512, 2, gf, tw)
                t = act(lambda e, g=g, f=f: e.activation(h[:, f, :], g, ACT.Silu), t, hf)
                g_r.done(gi, t)
                ta.append(t)
            return e_, tt, hi, h, ta

        def down(e_, tt, hi, h, ta):
            i, w1, w2, tw = te[e_]
            for j in range(0, 4, 2):
                di, d, df = d_r.take()
                for m in range(2):
                    t = self.proj(d[:, m * 256:m * 256 + 256],
                                  lambda k: h[:, k, (j + m) * 128:(j + m) * 128 + 128], lambda k: w2[:, k, :], 256, 4,
                                  df, ta)
                for m in range(2):
                    x = tt * 4 + j + m
                    t2 = dve(lambda e, d=d, m=m, x=x: e.scalar_tensor_tensor(X[:, x, :], d[:, m * 256:m * 256 + 256],
                             C[:, x, e_:e_ + 1], X[:, x, :], ALU.mult, ALU.add), t)
                d_r.done(di, t2)
            H.done(hi, t)
            if tt == 3 and e_ + 3 < 16:
                E1.done(i, t)
                load(e_ + 3)

        prev = None
        for e_ in range(16):
            for tt in range(4):
                cur = up(e_, tt)
                if prev:
                    down(*prev)
                prev = cur
        down(*prev)


def build(nc, ins, outs, first=0, layers=4):
    with ExitStack() as ctx:
        k = K(nc, ctx, ins, outs)
        block = ctx.enter_context(nc.Block())
        X = k.sb(X0, 16, 256)
        XNT = k.sb(XNT0, 2, 2048)
        tx = k.dma("x", X, ins["x"])
        k.consts()
        k.dve.wait([tx])
        for n in range(first, layers):
            (k.layer0, k.layer1, k.layer2, k.layer3)[n](X, XNT)
        k.barrier()
        to = k.dma("out", outs["out"], X)
        k.sp.wait([to])

        @block.sync
        def _(e):
            for f in k.sp.queue:
                f(e)

        @block.tensor
        def _(e):
            for f in k.pe.queue:
                f(e)

        @block.scalar
        def _(e):
            for f in k.act.queue:
                f(e)

        @block.vector
        def _(e):
            for f in k.dve.queue:
                f(e)

        @block.gpsimd
        def _(e):
            for f in k.pool.queue:
                f(e)


def kmajor(w):
    k, n = w.shape
    return np.ascontiguousarray(w.reshape(k // 128, 128, n).transpose(1, 0, 2))


def rope(n, d):
    inv = (np.float32(1.0) / np.power(np.float32(10000.0), np.arange(d // 2, dtype=np.float32) / np.float32(d // 2)))
    ang = np.arange(n, dtype=np.float32)[:, None] * inv.astype(np.float32)[None, :]
    return np.cos(ang).T.astype(np.float32), np.sin(ang).T.astype(np.float32)


def layout(i):
    a = {}
    a["x"] = np.ascontiguousarray(i["L0_attn_x"].reshape(16, 128, 256).transpose(1, 0, 2))
    h = np.arange(16)[:, None] * 16
    lo, hi = np.arange(8), np.arange(8, 16)
    iq = (h + np.concatenate([lo, hi, hi, lo])[None]).ravel()
    ia = (h + np.concatenate([lo, hi, lo, hi])[None]).ravel()
    ib = (h + np.concatenate([hi, lo, hi, lo])[None]).ravel()
    a["l0_wq"] = kmajor(i["L0_attn_Wq"].T[:, iq])
    a["l0_wa"] = kmajor(i["L0_attn_Wk"].T[:, ia])
    a["l0_wb"] = kmajor(i["L0_attn_Wk"].T[:, ib])
    a["l0_wv"] = kmajor(i["L0_attn_Wv"].T)
    wo = np.zeros((16, 32, 256), np.float32)
    wo[:, :16, :] = i["L0_attn_Wo"].T.reshape(16, 16, 256)
    a["l0_wo"] = kmajor(wo.reshape(512, 256))
    c, s = rope(1024, 16)
    q = np.float32(0.25)
    a["l0_tq"] = np.tile(np.concatenate([c, c, -s, s]) * q, (4, 1))
    a["l0_tc"] = np.tile(np.concatenate([c, c, c, c]), (4, 1))
    a["l0_ts"] = np.tile(np.concatenate([-s, s, -s, s]), (4, 1))
    a["l0_wgu"] = kmajor(i["L0_ffn_w_gate_up"].T)
    a["l0_wd"] = kmajor(i["L0_ffn_w_down"].T)
    a["l1_wq"] = kmajor(i["L1_attn_Wq"].T)
    a["l1_wk"] = kmajor(i["L1_attn_Wk"].T)
    a["l1_wv"] = kmajor(i["L1_attn_Wv"].T)
    a["l1_wo"] = kmajor(i["L1_attn_Wo"].T)
    a["l1_wg"] = kmajor(np.concatenate([i["L1_attn_Wgslc"].T, i["L1_attn_Wgswa"].T], axis=1))
    c, s = rope(1024, 128)
    a["l1_tc"] = np.concatenate([c, c])
    a["l1_ts"] = np.concatenate([s, -s])
    a["l1_wgu"] = kmajor(np.concatenate([i["L1_ffn_w_gate"].T, i["L1_ffn_w_up"].T], axis=1))
    a["l1_wd"] = kmajor(i["L1_ffn_w_down"].T)
    a["l2_win"] = kmajor(i["L2_attn_W_in"])
    a["l2_wout"] = kmajor(i["L2_attn_W_out"])
    col = lambda v, n: v.reshape(n, 128).T
    cw = i["L2_attn_conv_w"].reshape(20, 128, 4).transpose(1, 0, 2).reshape(128, 80)
    a["l2_vec"] = np.concatenate([col(i["L2_attn_mup_vector"][:4608], 36), col(i["L2_attn_b_in"][:4608], 36), cw,
                                  col(i["L2_attn_conv_b"], 20), col(np.repeat(i["L2_attn_D_param"], 64), 16),
                                  col(i["L2_attn_norm_w"], 16)], axis=1)
    a["l2_dt"] = np.broadcast_to(np.stack([i["L2_attn_b_in"][4608:], i["L2_attn_mup_vector"][4608:],
                                           i["L2_attn_dt_bias"], i["L2_attn_A_log"]])[None], (128, 4, 32))
    a["l2_bout"] = np.broadcast_to(i["L2_attn_b_out"][None], (128, 256))
    a["l2_w12"] = kmajor(np.concatenate([i["L2_ffn_w1"].T, i["L2_ffn_w2"].T], axis=1))
    w3 = np.zeros((768, 256), np.float32)
    w3[:704] = i["L2_ffn_w3"].T
    a["l2_w3"] = kmajor(w3)
    a["l3_wsa"] = kmajor(np.concatenate([i["L3_attn_Ws"], i["L3_attn_Wa"]], axis=1))
    a["l3_wo"] = kmajor(i["L3_attn_Wo"].T)
    a["l3_bo"] = np.broadcast_to(i["L3_attn_bo"][None], (128, 256))
    a["l3_wr"] = kmajor(i["L3_ffn_router_w"])
    a["l3_w1"] = i["L3_ffn_W1"].reshape(16, 2, 128, 512).transpose(2, 0, 1, 3)
    a["l3_w2"] = i["L3_ffn_W2"].reshape(16, 4, 128, 256).transpose(2, 0, 1, 3)
    return a


def kernel(**inputs):
    import concourse.bacc as bacc
    from concourse.bass_utils import run_bass_kernel_spmd as run

    arrays = layout({k: np.asarray(v) for k, v in inputs.items()})
    arrays = {k: np.ascontiguousarray(v) for k, v in arrays.items()}
    nc = bacc.Bacc("TRN2", target_bir_lowering=False, num_devices=1)
    ins = {k: nc.dram_tensor(k, v.shape, mybir.dt.from_np(v.dtype), kind="ExternalInput").ap()
           for k, v in arrays.items()}
    outs = {"out": nc.dram_tensor("out", (128, 16, 256), F32, kind="ExternalOutput").ap()}
    build(nc, ins, outs)
    r = run(nc, [arrays], core_ids=[0]).results[0]["out"]
    return np.ascontiguousarray(r.reshape(128, 16, 256).transpose(1, 0, 2)).reshape(2, 1024, 256)
```

```python
import numpy as np
from contextlib import ExitStack
import concourse.bass as bass
from concourse import mybir

F32 = mybir.dt.float32
U32 = mybir.dt.uint32
I32 = mybir.dt.int32
F32R = mybir.dt.float32r
ALU = mybir.AluOpType
ACT = mybir.ActivationFunctionType
AX = mybir.AxisListType

T = 2048
NT = 16
D = 256
NEG = -1.0e30

X0, XNT0, CONST0, WA0, WF0, WK0, EX0, END = 0, 4096, 8192, 9216, 22224, 28672, 52000, 53200
EW0 = END - 14 * 2048
R0 = END - 24832
SLOTS = (2 * T + 16 * 127) // 128


class Lane:

    def __init__(self, name, sem):
        self.name, self.sem, self.count, self.seen, self.queue = name, sem, 0, {}, []

    def wait(self, tokens):
        for sem, value in tokens:
            if value > self.seen.get(id(sem), 0):
                self.seen[id(sem)] = value
                self.queue.append(lambda e, s=sem, v=value: e.wait_ge(s, v))

    def __call__(self, f, *tokens, mark=True):
        self.wait(flat(tokens))
        if not mark:
            self.queue.append(f)
            return None
        self.count += 1
        self.queue.append(lambda e, s=self.sem: f(e).then_inc(s, 1))
        return (self.sem, self.count)

    def last(self):
        return (self.sem, self.count)


def flat(tokens):
    for t in tokens:
        if t is None:
            continue
        if isinstance(t, list):
            yield from flat(t)
        else:
            yield t


class Ring:

    def __init__(self, bufs):
        self.bufs, self.free, self.at = bufs, [[] for _ in bufs], -1

    def take(self):
        self.at = (self.at + 1) % len(self.bufs)
        return self.at, self.bufs[self.at], self.free[self.at]

    def done(self, i, *tokens):
        self.free[i] = list(flat(tokens))


class Banks:

    def __init__(self, view, n):
        self.view, self.n, self.free, self.at = view, n, [[] for _ in range(n)], 0

    def take(self, two=True):
        w = 2 if two else 1
        self.at += self.at % w
        i = self.at % self.n
        self.at = i + w
        at = slice(i, i + w)
        return at, self.view[:, i * 512:(i + w) * 512], [self.free[j] for j in range(i, i + w)]

    def done(self, at, *tokens):
        for j in range(at.start, at.stop):
            self.free[j] = list(flat(tokens))


class Net:

    def __init__(self, nc, ctx, ins, outs):
        self.nc, self.ins, self.outs = nc, ins, outs
        with nc.sbuf_tensor("whole", [128, END], F32) as self.whole:
            pass
        self.front = ctx.enter_context(nc.sbuf_tensor("front", [128, R0], F32))
        with nc.sbuf_tensor("back", [128, END - R0], F32) as self.back:
            pass
        self.rounded = ctx.enter_context(nc.sbuf_tensor("rounded", [128, END - R0], F32R))
        self.PS = ctx.enter_context(nc.psum_tensor("ps", [128, 8, 512], F32))
        mk = lambda n: ctx.enter_context(nc.semaphore(n))
        self.pe = Lane("pe", mk("s_pe"))
        self.act = Lane("act", mk("s_act"))
        self.dve = Lane("dve", mk("s_dve"))
        self.pool = Lane("pool", mk("s_pool"))
        self.sp = Lane("sp", mk("s_sp"))
        self.mk = mk
        self.dsem = {}
        self.later = []
        self.xg = nc.dram_tensor("xg", (SLOTS * 128, 256), F32, kind="Internal").ap()
        self.yg = nc.dram_tensor("yg", (SLOTS * 128, 256), F32, kind="Internal").ap()

    def sbr(self, at, *shape):
        return self.view(self.rounded, at - R0, shape)

    def sbw(self, at, *shape):
        return self.view(self.whole, at, shape)

    def sb(self, at, *shape):
        if at >= R0:
            return self.view(self.back, at - R0, shape)
        return self.view(self.front, at, shape)

    def view(self, tensor, at, shape):
        n = int(np.prod(shape))
        assert 0 <= at and at + n <= tensor.shape[1]
        v = tensor[:, at:at + n]
        if len(shape) == 2:
            v = v.rearrange("p (a b) -> p a b", a=shape[0])
        elif len(shape) == 3:
            v = v.rearrange("p (a b c) -> p a b c", a=shape[0], b=shape[1])
        return v

    def dma(self, name, out, in_, *tokens, lane=None):
        if name not in self.dsem:
            self.dsem[name] = [self.mk("d_" + name), 0]
        s = self.dsem[name]
        s[1] += 16
        (lane or self.sp)(lambda e, sem=s[0]: e.dma_start(out, in_).then_inc(sem, 16), *tokens, mark=False)
        return (s[0], s[1])

    def barrier(self):
        lanes = [self.pe, self.act, self.dve, self.pool]
        marks = [l.last() for l in lanes]
        for l in lanes + [self.sp]:
            l.wait(marks)

    def consts(self):
        pool, dve = self.pool, self.dve
        self.ident = self.sb(CONST0, 128)
        self.mask = self.sb(CONST0 + 128, 128)
        self.ones = self.sb(CONST0 + 256, 128)
        self.eps = self.sb(CONST0 + 384, 1)
        self.eps8 = self.sb(CONST0 + 385, 1)
        self.zero1 = self.sb(CONST0 + 386, 1)
        self.misc = CONST0 + 400
        t0 = pool(lambda e: e.memset(self.ident, 0.0))
        t1 = pool(lambda e: e.memset(self.mask, 0.0))
        pool(lambda e: e.memset(self.ones, 1.0))
        pool(lambda e: e.memset(self.eps, 1e-5))
        pool(lambda e: e.memset(self.zero1, 0.0))
        pool(lambda e: e.affine_select(out=self.ident, in_=self.ident, compare_op=ALU.not_equal, fill=1.0,
                                       base=0, pattern=[[-1, 128]], channel_multiplier=1), t0)
        t = pool(lambda e: e.affine_select(out=self.mask, in_=self.mask, compare_op=ALU.is_ge, fill=NEG,
                                           base=0, pattern=[[-1, 128]], channel_multiplier=1), t1)
        for l in (self.pe, self.act, self.dve, self.pool):
            l.wait([t])

    def norm(self, X, XNT, XN=None, work=WK0):
        pe, act, dve = self.pe, self.act, self.dve
        st = self.sb(work, 16, 6)
        mv = self.sb(work + 96, 16, 2)
        sd = self.sb(work + 128, 16)
        tmp = Ring([self.sb(work + 256 + 256 * i, 256) for i in range(4)])
        ps = Ring([self.PS[:, i, :] for i in range(8)])
        for i in range(NT):
            t = dve(lambda e, i=i: e.bn_stats(st[:, i, :], X[:, i, :]))
            t = dve(lambda e, i=i: e.bn_aggr(mv[:, i, :], st[:, i, :]), t)
        t = act(lambda e: e.activation(sd, mv[:, :, 1], ACT.Sqrt, bias=self.eps), t)
        trs = dve(lambda e: e.reciprocal(sd, sd), t)
        tl = []
        tm = self.dve.last()
        for i0 in range(0, NT, 4):
            pend = []
            (b0, p0, f0), (b1, p1, f1) = ps.take(), ps.take()
            for i in range(i0, i0 + 4):
                if XN is None:
                    k, xn, fr = tmp.take()
                else:
                    xn, fr = XN[:, i, :], []
                t = dve(lambda e, i=i, xn=xn: e.tensor_scalar(xn, X[:, i, :], mv[:, i, 0:1], sd[:, i:i + 1],
                                                              ALU.subtract, ALU.mult), trs, tm, fr)
                for c, (p, f) in enumerate(((p0, f0), (p1, f1))):
                    t2 = pe(lambda e, p=p, xn=xn, c=c, j=i - i0: e.transpose(
                        p[:, j * 128:j * 128 + 128], xn[:, c * 128:c * 128 + 128], self.ident), t, f)
                if XN is None:
                    tmp.done(k, t2)
            a = act(lambda e, p=p0, i0=i0: e.activation(XNT[:, 0, i0 * 128:i0 * 128 + 512], p, ACT.Copy), t2)
            b = dve(lambda e, p=p1, i0=i0: e.tensor_copy(XNT[:, 1, i0 * 128:i0 * 128 + 512], p), t2)
            ps.done(b0, a)
            ps.done(b1, b)
            tl += [a, b]
        return tl

    def flush(self):
        for f in self.later:
            f()
        self.later = []

    def proj(self, ps, lhsT, rhs, n, nk, *tokens):
        for k in range(nk):
            t = self.pe(lambda e, k=k, a=lhsT(k), b=rhs(k): e.matmul(ps, a, b, start=(k == 0), stop=(k == nk - 1)),
                        *tokens, mark=(k == nk - 1))
        return t

    def project_add(self, X, first, n, ring, lhsT, rhs, nk, *tokens):
        for i in range(0, n, 2):
            pi, p, pf = ring.take()
            for j in range(2):
                t = self.proj(p[:, j * 256:j * 256 + 256], lambda k: lhsT(i + j, k), rhs, 256, nk, pf, *tokens)
            x = X[:, first + i:first + i + 2, :]
            t2 = self.dve(lambda e, p=p, x=x: e.tensor_tensor(x, x, p.rearrange("p (a b) -> p a b", a=2), ALU.add), t)
            ring.done(pi, t2)
        return t

    def ffn(self, X, XNT, nf, wg, wu, wd, rows, gate, work, tw, out_scale=None):
        pe, act, dve = self.pe, self.act, self.dve
        g_r = Ring([self.PS[:, i, :] for i in (0, 1)])
        u_r = Ring([self.PS[:, i, :] for i in (2, 3)])
        d_r = Ring([self.PS[:, i, :] for i in (4, 5, 6, 7)])
        tmp = Ring([self.sb(work + 512 * i, 512) for i in range(3)])
        H = Ring([self.sb(work + 1536 + 512 * nf * i, nf, 512) for i in range(2)])

        def up(tt):
            hi, h, hf = H.take()
            done = []
            tok = slice(tt * 512, tt * 512 + 512)
            for f in range(nf):
                r = rows(f)
                gi, g, gf = g_r.take()
                ui, u, uf = u_r.take()
                tg = self.proj(g[:r, :], lambda k: wg(k, f), lambda k: XNT[:, k, tok], 512, 2, gf, tw)
                tu = self.proj(u[:r, :], lambda k: wu(k, f), lambda k: XNT[:, k, tok], 512, 2, uf, tw)
                ti, s, sf = tmp.take()
                ta = act(lambda e, s=s, g=g, r=r: e.activation(s[:r, :], g[:r, :], gate), tg, sf)
                g_r.done(gi, ta)
                td = dve(lambda e, s=s, u=u, r=r, f=f: e.tensor_tensor(h[:r, f, :], s[:r, :], u[:r, :], ALU.mult),
                         ta, tu, hf)
                u_r.done(ui, td)
                tmp.done(ti, td)
            return tt, hi, h, td

        def down(tt, hi, h, th):
            t = self.project_add(X, tt * 4, 4, d_r, lambda i, k: h[:rows(k), k, i * 128:i * 128 + 128],
                                 lambda k: wd(k)[:rows(k), :], nf, th, tw)
            H.done(hi, t)

        prev = None
        for tt in range(4):
            cur = up(tt)
            if prev:
                down(*prev)
            prev = cur
        down(*prev)

    def attend(self, units, nh, work, score, scale, pscale, pv, rings, npt=4, after=None):
        pe, act, dve, pool = self.pe, self.act, self.dve, self.pool
        s_r, t_r = rings
        PB = [self.sb(work + nh * 1024 * i, nh, 1024) for i in range(2)]
        PTr = Ring([self.sb(work + nh * 2048 + 128 * nh * i, nh * 128) for i in range(npt)])
        small = self.misc
        pfree = [[], []]
        evac = [0]

        def scores(n, u, h):
            qt = u[-1]
            nk = 128 * (qt + 1)
            q, k, tk = score(u, h)
            si, s, sf = s_r.take(nk > 512)
            for c in range(0, nk, 512):
                w = min(512, nk - c)
                t = pe(lambda e, c=c, w=w: e.matmul(s[:, c:c + w], q, k(c, c + w), start=True, stop=True), sf, tk,
                       mark=(c + 512 >= nk))
            if after:
                after(u, h, t)
            t = dve(lambda e: e.tensor_tensor(s[:, nk - 128:nk], s[:, nk - 128:nk], self.mask, ALU.add), t)
            st = self.sb(small + (n % 2) * 32, 4, 8)
            t = dve(lambda e: e.tensor_reduce(st[:, 0, h:h + 1], s[:, :nk], AX.X, ALU.max, negate=True), t,
                    pfree[n % 2])
            if scale != 1.0:
                t = dve(lambda e: e.tensor_scalar(st[:, 0, h:h + 1], st[:, 0, h:h + 1], scale, None, ALU.mult), t)
            P = PB[n % 2]
            t = act(lambda e: e.activation(P[:, h, :nk], s[:, :nk], ACT.Exp, bias=st[:, 0, h:h + 1], scale=scale,
                                           accum_out=st[:, 1, h:h + 1]), t, pfree[n % 2])
            s_r.done(si, t)
            if pscale is None:
                return lambda: t

            def finish(t=t):
                t = dve(lambda e: e.reciprocal(st[:, 2, h:h + 1], st[:, 1, h:h + 1]), t)
                r = 2
                if g is not None:
                    t = dve(lambda e: e.tensor_tensor(st[:, 3, h:h + 1], g, st[:, 2, h:h + 1], ALU.mult), t)
                    r = 3
                return (dve if h == nh - 1 else pool)(lambda e: e.tensor_scalar(
                    P[:, h, :nk], P[:, h, :nk], st[:, r, h:h + 1], 1.0, ALU.mult, ALU.mult), t)

            g = pscale(u, h)
            return finish

        def blocks(n, u, tp):
            qt = u[-1]
            P = PB[n % 2]
            pts = {}

            def tr(j):
                ti, tp_, tf = t_r.take()
                for h in range(nh):
                    t = pe(lambda e, h=h: e.transpose(tp_[:, h * 128:h * 128 + 128], P[:, h, j * 128:j * 128 + 128],
                                                      self.ident), tp[h], tf, mark=(h == nh - 1))
                pi, PT, pf = PTr.take()
                evac[0] += 1
                w = nh * 128
                if evac[0] % 2:
                    t2 = act(lambda e: e.activation(PT, tp_[:, :w], ACT.Copy), t, pf)
                else:
                    t2 = dve(lambda e: e.tensor_copy(PT, tp_[:, :w]), t, pf)
                t_r.done(ti, t2)
                pts[j] = (pi, PT, t2)
                if j == qt:
                    pfree[n % 2] = [t]

            def mul(j):
                pi, PT, t2 = pts[j]
                t = pv(u, j, PT, t2)
                PTr.done(pi, t)

            steps = [lambda j=j: tr(j) for j in range(qt + 1)]
            out = steps[:2]
            for j in range(qt + 1):
                out += steps[j + 2:j + 3]
                out.append(lambda j=j: mul(j))
            return out

        rest, ready, fin = [], [], lambda: None
        for n, u in enumerate(units):
            tp = []
            for h in range(nh):
                nxt = scores(n, u, h)
                fin()
                self.flush()
                fin = lambda nxt=nxt, tp=tp: tp.append(nxt())
                if h == 0:
                    for f in rest:
                        f()
                    k = min(2, len(ready) // 2) if nh > 1 else 0
                    now, rest = ready[:len(ready) - k], ready[len(ready) - k:]
                if h > 0 or nh == 1:
                    for _ in range(-(-len(now) // max(nh - h, 1))):
                        now.pop(0)()
            ready = blocks(n, u, tp)
        fin()
        for f in rest:
            f()
        self.flush()
        for f in ready:
            f()
        self.flush()

    def layer0(self, X, XNT):
        pe, act, dve, pool = self.pe, self.act, self.dve, self.pool
        I = self.ins
        Wq, Wa, Wb = (self.sb(WA0 + 1024 * i, 2, 512) for i in range(3))
        Wv = self.sb(WA0 + 3072, 2, 256)
        Wo = self.sb(WA0 + 4096, 4, 256)
        Tq, Tc, Ts = (self.sb(WA0 + 5120 + 1024 * i, 1024) for i in range(3))
        tmp = Ring([self.sb(WA0 + 8192 + 512 * i, 512) for i in range(2)])
        Wgu = self.sb(WF0, 2, 2048)
        Wd = self.sb(WF0 + 4096, 8, 256)
        tw = [self.dma("w_a", Wq, I["l0_wq"]), self.dma("w_a", Wa, I["l0_wa"]), self.dma("w_a", Wb, I["l0_wb"]),
              self.dma("w_a", Wv, I["l0_wv"]), self.dma("w_a", Wo, I["l0_wo"]), self.dma("w_a", Tq, I["l0_tq"]),
              self.dma("w_a", Tc, I["l0_tc"]), self.dma("w_a", Ts, I["l0_ts"])][-1:]
        tf = [self.dma("w_f", Wgu, I["l0_wgu"]), self.dma("w_f", Wd, I["l0_wd"])][-1:]
        self.norm(X, XNT)
        self.barrier()
        Q = self.sb(WK0, 4, 1024)
        Kt = self.sb(WK0 + 4096, 1024)
        V = self.sb(WK0 + 5120, 8, 16, 32)
        aT = self.sb(WK0 + 9216, 4, 1024)
        work = WK0 + 13312
        s_r = Banks(self.PS[:, 0:4, :].rearrange("p a b -> p (a b)"), 4)
        t_r = Ring([self.PS[:, i, :] for i in (4, 5, 6)])
        o_r = Ring([self.PS[:, 7, :]])
        t_one = pool(lambda e: e.memset(V[:, :, :, 16:32], 0.0))
        t_zero = pool(lambda e: e.memset(Q, 0.0))
        state = {}

        def make_qk(b, ht):
            free = state.get("qfree")
            done = []
            for tt in range(2):
                tok = slice(b * 1024 + tt * 512, b * 1024 + tt * 512 + 512)
                o = slice(tt * 512, tt * 512 + 512)
                W = slice(ht * 128, ht * 128 + 128)
                si, s, sf = s_r.take()
                ta = self.proj(s[:, 0:512], lambda k: Wa[:, k, W], lambda k: XNT[:, k, tok], 512, 2, sf, tw)
                tb = self.proj(s[:, 512:1024], lambda k: Wb[:, k, W], lambda k: XNT[:, k, tok], 512, 2, sf, tw)
                ti, tm, tf_ = tmp.take()
                t1 = dve(lambda e, s=s, o=o: e.tensor_tensor(Kt[:, o], s[:, 0:512], Tc[:, o], ALU.mult), ta, free)
                t2 = dve(lambda e, s=s, o=o, tm=tm: e.tensor_tensor(tm, s[:, 512:1024], Ts[:, o], ALU.mult), tb, tf_)
                t3 = pool(lambda e, o=o, tm=tm: e.tensor_tensor(Kt[:, o], Kt[:, o], tm, ALU.add), t1, t2)
                s_r.done(si, t2)
                tmp.done(ti, t3)
                si, s, sf = s_r.take(False)
                t = self.proj(s[:, 0:512], lambda k: Wq[:, k, W], lambda k: XNT[:, k, tok], 512, 2, sf, tw)
                for h in range(4):
                    r = slice(32 * h, 32 * h + 32)
                    t4 = dve(lambda e, s=s, o=o, r=r, h=h: e.tensor_tensor(Q[r, h, o], s[r, 0:512], Tq[r, o],
                                                                          ALU.mult), t, t_zero, free)
                s_r.done(si, t4)
                done += [t3, t4]
            state[(b, ht)] = done

        def make_v(b):
            for i in range(8):
                oi, o, of = t_r.take()
                tok = slice(b * 1024 + i * 128, b * 1024 + i * 128 + 128)
                t = self.proj(o[:, 0:256], lambda k: XNT[:, k, tok], lambda k: Wv[:, k, :], 256, 2, of, tw)
                t = act(lambda e, o=o, i=i: e.activation(V[:, i, :, 0:16],
                        o[:, 0:256].rearrange("p (h d) -> p h d", h=16), ACT.Copy), t, state.get("vfree"))
                t_r.done(oi, t)
            state["v"] = t

        cur = {}

        def score(u, h):
            b, ht, qt = u
            if (b, ht) not in state:
                make_qk(b, ht)
            return Q[:, h, qt * 128:qt * 128 + 128], lambda c0, c1: Kt[:, c0:c1], state[(b, ht)]

        def after_score(u, h, t):
            if u[-1] == 7 and h == 3:
                state["qfree"] = t

        def pv(u, j, PT, t2):
            b, ht, qt = u
            if j == 0:
                cur["o"] = o_r.take()
            oi, o, of = cur["o"]
            for h in range(4):
                t = pe(lambda e, h=h: e.matmul(o[32 * h:32 * h + 32, 0:128], V[:, j, ht * 4 + h, :],
                                               PT[:, h * 128:h * 128 + 128], start=(j == 0), stop=(j == qt)),
                       t2, of, state["v"], t_one, mark=(h == 3))
            if j == qt:
                tc = act(lambda e: e.activation(aT[:, ht, qt * 128:qt * 128 + 128], o[:, 0:128], ACT.Copy), t,
                         state.get("afree"))
                o_r.done(oi, tc)
                state["a"] = tc
                if qt == 7 and ht == 3:
                    state["vfree"] = t
                    out_proj(b)
            return t

        def out_proj(b):
            t = self.project_add(X, b * 8, 8, t_r, lambda i, k: aT[:, k, i * 128:i * 128 + 128],
                                 lambda k: Wo[:, k, :], 4, state["a"])
            state["afree"] = t
            if b == 0:
                make_v(1)

        make_v(0)
        units = [(b, ht, qt) for b in range(2) for ht in range(4) for qt in range(8)]
        self.attend(units, 4, work, score, 1.0, lambda u, h: None, pv, (s_r, t_r), 3, after_score)
        self.barrier()
        self.ffn(X, XNT, 8, lambda k, f: Wgu[:, k, f * 128:f * 128 + 128],
                 lambda k, f: Wgu[:, k, 1024 + f * 128:1024 + f * 128 + 128], lambda k: Wd[:, k, :],
                 lambda f: 128, ACT.Silu, WK0, tf)
        self.barrier()

    def layer1(self, X, XNT):
        pe, act, dve, pool = self.pe, self.act, self.dve, self.pool
        I = self.ins
        Wq = self.sb(WA0, 2, 2048)
        Wk, Wv = self.sb(WA0 + 4096, 2, 512), self.sb(WA0 + 5120, 2, 512)
        Wo = self.sb(WA0 + 6144, 16, 256)
        Tc, Ts = self.sb(WA0 + 10240, 1024), self.sb(WA0 + 11264, 1024)
        Wg = self.sb(WA0 + 12288, 2, 32)
        tmp = Ring([self.sb(EX0 + 512 * i, 512) for i in range(2)])
        Wgu = self.sb(WF0, 2, 2048)
        Wd = self.sb(WF0 + 4096, 8, 256)
        for dst, src in ((Wq, "l1_wq"), (Wk, "l1_wk"), (Wv, "l1_wv"), (Wo, "l1_wo"), (Tc, "l1_tc"), (Ts, "l1_ts"),
                         (Wg, "l1_wg")):
            tw = self.dma("w_a", dst, I[src])
        self.dma("w_f", Wgu, I["l1_wgu"])
        tf = self.dma("w_f", Wd, I["l1_wd"])
        self.norm(X, XNT)
        self.barrier()
        Q = self.sb(WK0, 4, 1024)
        Kt = self.sb(WK0 + 4096, 1024)
        V = self.sb(WK0 + 5120, 8, 512)
        aT = self.sb(WK0 + 9216, 4, 1024)
        G = self.sb(WK0 + 13312, 16, 16)
        work = WK0 + 13568
        s_r = Banks(self.PS[:, 0:4, :].rearrange("p a b -> p (a b)"), 4)
        t_r = Ring([self.PS[:, i, :] for i in (4, 5, 6)])
        o_r = Ring([self.PS[:, 7, :]])
        state, cur = {}, {}
        sg = self.sb(work, 16, 32)
        for i in range(NT):
            oi, o, of = t_r.take()
            t = self.proj(o[:, 0:32], lambda k: XNT[:, k, i * 128:i * 128 + 128], lambda k: Wg[:, k, :], 32, 2, of, tw)
            t = act(lambda e, o=o, i=i: e.activation(sg[:, i, :], o[:, 0:32], ACT.Sigmoid), t)
            t_r.done(oi, t)
        tg = dve(lambda e: e.tensor_tensor(G, sg[:, :, 0:16], sg[:, :, 16:32], ALU.add), t)
        state["sg"] = tg
        act.wait([tg])

        scale = float(np.float32(1.0) / np.sqrt(np.float32(128.0)))

        def rotate(W, dst, b, tt, *free):
            tok = slice(b * 1024 + tt * 512, b * 1024 + tt * 512 + 512)
            o = slice(tt * 512, tt * 512 + 512)
            si, s, sf = s_r.take(False)
            t = self.proj(s[:, 0:512], W, lambda k: XNT[:, k, tok], 512, 2, sf, tw)
            ti, tm, tf_ = tmp.take()
            t1 = dve(lambda e: e.tensor_tensor(dst[:, o], s[:, 0:512], Tc[:, o], ALU.mult), t, *free)
            dve(lambda e: e.tensor_tensor(tm[0:64, :], s[64:128, 0:512], Ts[64:128, o], ALU.mult), t, tf_)
            t2 = dve(lambda e: e.tensor_tensor(tm[64:128, :], s[0:64, 0:512], Ts[0:64, o], ALU.mult), t, tf_)
            t3 = pool(lambda e: e.tensor_tensor(dst[:, o], dst[:, o], tm, ALU.add), t1, t2)
            s_r.done(si, t2)
            tmp.done(ti, t3)
            return t3

        def make_qk(b, g):
            free = state.get("qfree")
            done = []
            for tt in range(2):
                done.append(rotate(lambda k: Wk[:, k, g * 128:g * 128 + 128], Kt, b, tt, free))
                o = slice(tt * 512, tt * 512 + 512)
                done.append(pool(lambda e, o=o: e.tensor_scalar(Kt[:, o], Kt[:, o], scale, 1.0, ALU.mult, ALU.mult),
                                 done[-1]))
                for h in range(4):
                    c = (g * 4 + h) * 128
                    done.append(rotate(lambda k: Wq[:, k, c:c + 128], Q[:, h, :], b, tt, free))
            state[(b, g)] = done

        def make_v(b):
            for i in range(8):
                oi, o, of = t_r.take()
                tok = slice(b * 1024 + i * 128, b * 1024 + i * 128 + 128)
                t = self.proj(o, lambda k: XNT[:, k, tok], lambda k: Wv[:, k, :], 512, 2, of, tw)
                t = act(lambda e, o=o, i=i: e.activation(V[:, i, :], o, ACT.Copy), t, state.get("vfree"))
                t_r.done(oi, t)
            state["v"] = t

        def score(u, h):
            b, g, qt = u
            if (b, g) not in state:
                make_qk(b, g)
            return Q[:, h, qt * 128:qt * 128 + 128], lambda c0, c1: Kt[:, c0:c1], state[(b, g)]

        def after_score(u, h, t):
            if u[-1] == 7 and h == 3:
                state["qfree"] = t

        def pv(u, j, PT, t2):
            b, g, qt = u
            if j == 0:
                cur["o"] = o_r.take()
            oi, o, of = cur["o"]
            t = pe(lambda e: e.matmul(o, V[:, j, g * 128:g * 128 + 128], PT, start=(j == 0), stop=(j == qt)),
                   t2, of, state["v"])
            if j == qt:
                dst = aT[:, :, qt * 128:qt * 128 + 128]
                ta = act(lambda e: e.activation(dst, o.rearrange("p (h q) -> p h q", h=4), ACT.Copy), t,
                         state.get("afree"))
                o_r.done(oi, ta)
                state["a"] = ta
                if qt == 7:
                    if g == 3:
                        state["vfree"] = t
                    out_proj(b, g)
            return t

        def out_proj(b, g):
            t = self.project_add(X, b * 8, 8, t_r, lambda i, k: aT[:, k, i * 128:i * 128 + 128],
                                 lambda k: Wo[:, g * 4 + k, :], 4, state["a"])
            state["afree"] = t
            if (b, g) == (0, 3):
                make_v(1)

        make_v(0)
        units = [(b, g, qt) for b in range(2) for g in range(4) for qt in range(8)]
        self.attend(units, 4, work, score, 1.0,
                    lambda u, h: G[:, u[0] * 8 + u[2], u[1] * 4 + h:u[1] * 4 + h + 1], pv, (s_r, t_r), 3, after_score)
        self.barrier()
        self.ffn(X, XNT, 8, lambda k, f: Wgu[:, k, f * 128:f * 128 + 128],
                 lambda k, f: Wgu[:, k, 1024 + f * 128:1024 + f * 128 + 128], lambda k: Wd[:, k, :],
                 lambda f: 128, ACT.Silu, WK0, tf)
        self.barrier()

    def layer2(self, X, XNT):
        pe, act, dve, pool = self.pe, self.act, self.dve, self.pool
        I = self.ins
        Win = self.sb(WA0, 2, 4640)
        Wout = self.sb(WA0 + 9280, 16, 256)
        W12 = self.sb(WA0 + 13376, 2, 1408)
        W3 = self.sb(WA0 + 16192, 6, 256)
        Crep = self.sb(WA0 + 17728, 1024)
        sel = Ring([self.sb(WA0 + 18752 + 128 * i, 128) for i in range(2)])
        ident4 = self.sb(EX0, 512)
        dt = self.sb(EX0 + 512, 16, 32)
        vec = self.sb(self.misc, 204)
        mup, bin_, cw, cb, Dv, nw = (vec[:, 0:36], vec[:, 36:72], vec[:, 72:152], vec[:, 152:172], vec[:, 172:188],
                                     vec[:, 188:204])
        bm = self.sb(self.misc + 204, 36)
        dv = self.sb(self.misc + 240, 4, 32)
        bout = self.sb(WK0 + 20000, 256)
        for dst, src in ((Win, "l2_win"), (Wout, "l2_wout"), (vec, "l2_vec"), (dv, "l2_dt"), (bout, "l2_bout")):
            tw = self.dma("w_a", dst, I[src])
        self.norm(X, XNT)
        for i in range(4):
            pool(lambda e, i=i: e.tensor_copy(ident4[:, i * 128:i * 128 + 128], self.ident))
        for i in range(NT):
            tx = pool(lambda e, i=i: e.tensor_tensor(X[:, i, :], X[:, i, :], bout, ALU.add), tw, dve.last())
        tbm = dve(lambda e: e.tensor_tensor(bm, bin_, mup, ALU.mult), tw)
        self.barrier()
        BC = self.sb(WK0, 4, 1024)
        BT = self.sb(WK0 + 4096, 8, 256)
        RAW = self.sb(WK0 + 6144, 2, 1032)
        XCs = [self.sb(WA0 + 13376, 2, 1024), self.sb(WK0 + 8208, 2, 1024)]
        sqR = Ring([self.sb(WA0 + 16192 + 512 * i, 512) for i in range(2)])
        rsR = Ring([self.sb(EX0 + 1024 + 8 * i, 8) for i in range(2)])
        self.mhalf = self.sb(EX0 + 1048, 8)
        pool(lambda e: e.memset(self.mhalf, -0.5))
        XD = self.sb(WK0 + 10256, 8, 256)
        LT = self.sb(WK0 + 12304, 4, 8, 128)
        Y = self.sb(WK0 + 16400, 2, 1024)
        CP = self.sb(WK0 + 18448, 1024)
        R = self.sb(WK0 + 19472, 2048)
        Zr = Ring([self.sb(WK0 + 21520 + 512 * i, 512) for i in range(2)])
        Bd = Ring([self.sb(WK0 + 22544 + 128 * i, 4, 32) for i in range(2)])
        Hb = Ring([self.sb(WK0 + 22800 + 256 * i, 256) for i in range(2)])
        ach = self.sb(self.misc + 368, 8)
        aR = Ring([self.PS[:, i, :] for i in (0, 1)])
        bR = Ring([self.PS[:, i, :] for i in (2, 3)])
        sR = Ring([self.PS[:, i, 0:64] for i in (4, 7)])
        yR = Ring([self.PS[:, i, :] for i in (5, 6)])

        ai, ap_, af = aR.take()
        for i in range(NT):
            t = self.proj(ap_[:, i * 32:i * 32 + 32], lambda k: XNT[:, k, i * 128:i * 128 + 128],
                          lambda k: Win[:, k, 4608:4640], 32, 2, tw)
        W = [self.sb(WK0 + 512 * i, 16, 32) for i in range(6)]
        wide = lambda r: dv[:, r:r + 1, :].broadcast_to([128, 16, 32])
        pv3 = ap_.rearrange("p (a b) -> p a b", a=16)
        t = dve(lambda e: e.tensor_tensor(W[0], pv3, wide(0), ALU.add), t)
        aR.done(ai, t)
        t = dve(lambda e: e.tensor_tensor(W[0], W[0], wide(1), ALU.mult), t)
        tv = dve(lambda e: e.tensor_tensor(W[0], W[0], wide(2), ALU.add), t)
        t = dve(lambda e: e.tensor_scalar(W[1], W[0], -1.0, None, ALU.mult), tv)
        t = dve(lambda e: e.tensor_tensor(W[1], W[0], W[1], ALU.min), t)
        te = act(lambda e: e.activation(W[2], W[1], ACT.Exp), t)
        tA = act(lambda e: e.activation(dv[:, 3, :], dv[:, 3, :], ACT.Exp), tw)
        t = dve(lambda e: e.tensor_scalar(W[3], W[2], 2.0, None, ALU.add), te)
        t = dve(lambda e: e.reciprocal(W[3], W[3]), t)
        ts = dve(lambda e: e.tensor_tensor(W[3], W[2], W[3], ALU.mult), t)
        tz = dve(lambda e: e.tensor_tensor(W[4], W[3], W[3], ALU.mult), ts)
        t = dve(lambda e: e.tensor_scalar(W[5], W[4], 2.0 / 17.0, 2.0 / 15.0, ALU.mult, ALU.add), tz)
        for n in (13, 11, 9, 7, 5, 3, 1):
            t = dve(lambda e: e.tensor_tensor(W[5], W[5], W[4], ALU.mult), t)
            t = dve(lambda e, n=n: e.tensor_scalar(W[5], W[5], 2.0 / n, None, ALU.add), t)
        t = dve(lambda e: e.tensor_tensor(W[5], W[5], W[3], ALU.mult), t)
        t2 = dve(lambda e: e.tensor_scalar(W[0], W[0], 0.0, None, ALU.max), tv)
        tdt = dve(lambda e: e.tensor_tensor(dt, W[0], W[5], ALU.add), t, t2)
        t = dve(lambda e: e.tensor_tensor(W[1], dt, wide(3), ALU.mult), tdt, tA)
        t = act(lambda e: e.activation(W[1], W[1], ACT.Exp, scale=-1.0), t)
        for j in range(4):
            bi, bp, bf = bR.take()
            for i in range(4):
                t2 = pe(lambda e, i=i, bp=bp, j=j: e.transpose(bp[0:32, i * 128:i * 128 + 128], W[1][:, j * 4 + i, :],
                                                              self.ident), t, bf)
            t3 = dve(lambda e, bp=bp, j=j: e.tensor_copy(R[0:32, j * 512:j * 512 + 512], bp[0:32, :]), t2)
            bR.done(bi, t3)
        for c in range(16):
            o = slice(c * 128, c * 128 + 128)
            t = dve(lambda e, o=o: e.tensor_tensor_scan(R[32:64, o], R[0:32, o], self.ones[0:32, :], 1.0, ALU.mult,
                                                        ALU.mult), t3)
        tR = dve(lambda e: e.memset(R[0:32, 0:2048:128], 0.0), t)
        dve(lambda e: e.memset(R[64:128, :], 0.0))
        for k in range(16):
            dve(lambda e, k=k: e.tensor_scalar(Wout[:, k, :], Wout[:, k, :], nw[:, k:k + 1], None, ALU.mult), tw)
        for h in Hb.bufs:
            pool(lambda e, h=h: e.memset(h, 0.0))
        tpad = pool(lambda e: e.memset(RAW[:, :, 0:3], 0.0))
        self.barrier()

        def raw(col, tile, slot, b, *free):
            for tt in range(2):
                tok = slice(b * 1024 + tt * 512, b * 1024 + tt * 512 + 512)
                ai, p, af = aR.take()
                t = self.proj(p, lambda k: Win[:, k, col:col + 128], lambda k: XNT[:, k, tok], 512, 2, af)
                t = act(lambda e, p=p, tt=tt: e.activation(RAW[:, slot, 3 + tt * 512:3 + tt * 512 + 512], p,
                        ACT.Identity, scale=mup[:, tile:tile + 1], bias=bm[:, tile:tile + 1]), t, *free)
                aR.done(ai, t)
            return t

        def conv(slot, ct, dst, t, *free):
            t = pool(lambda e: e.tensor_scalar(dst, RAW[:, slot, 0:1024], cw[:, ct * 4:ct * 4 + 1], 1.0, ALU.mult,
                                               ALU.mult), t, *free)
            for k in range(1, 4):
                t = dve(lambda e, k=k: e.scalar_tensor_tensor(dst, RAW[:, slot, k:k + 1024],
                        cw[:, ct * 4 + k:ct * 4 + k + 1], dst, ALU.mult, ALU.add), t)
            return t, act(lambda e: e.activation(dst, dst, ACT.Silu, bias=cb[:, ct:ct + 1]), t)

        def merge(*lists):
            steps = [((i + 0.5) / len(l) * w, n, f) for n, (l, w) in enumerate(lists) for i, f in enumerate(l)]
            for _, _, f in sorted(steps, key=lambda s: (s[0], s[1])):
                f()

        rfree = [None, None]
        last, S_ = {}, {}
        sg_t = {}

        def conv_bc(b):
            tbc = []
            for n in range(4):
                s = n % 2
                t = raw(4096 + n * 128, 32 + n, s, b, rfree[s])
                rfree[s], t = conv(s, 16 + n, BC[:, n, :], t, last.get("bc"))
                tbc.append(t)
            for c in range(8):
                bi, bp, bf = bR.take()
                for n in range(2):
                    t = pe(lambda e, n=n, bp=bp, c=c: e.transpose(bp[:, n * 128:n * 128 + 128],
                           BC[:, n, c * 128:c * 128 + 128], self.ident), tbc[n], bf)
                tbt = act(lambda e, bp=bp, c=c: e.activation(BT[:, c, :], bp[:, 0:256], ACT.Copy), t, last.get("bc"))
                bR.done(bi, tbt)
            S_["bc"], S_["bt"] = tbc, tbt

        def conv_x(b, g):
            XC = XCs[g % 2]
            out = []
            S_["xc", b, g] = tcx = []

            def one(s):
                tile = 2 * g + s
                t = raw(2048 + tile * 128, 16 + tile, s, b, rfree[s])
                S_["raw", s] = t

            def first(s):
                ct = 2 * g + s
                S_["cv", s] = pool(lambda e: e.tensor_scalar(XC[:, s, :], RAW[:, s, 0:1024], cw[:, ct * 4:ct * 4 + 1],
                                                             1.0, ALU.mult, ALU.mult), S_["raw", s],
                                   last.get(("xc", g % 2)))

            def tap(s, k):
                ct = 2 * g + s
                S_["cv", s] = dve(lambda e: e.scalar_tensor_tensor(XC[:, s, :], RAW[:, s, k:k + 1024],
                                  cw[:, ct * 4 + k:ct * 4 + k + 1], XC[:, s, :], ALU.mult, ALU.add), S_["cv", s])
                if k == 3:
                    rfree[s] = S_["cv", s]
                    tcx.append(act(lambda e: e.activation(XC[:, s, :], XC[:, s, :], ACT.Silu, bias=cb[:, ct:ct + 1]),
                                   S_["cv", s]))

            return [lambda: one(0), lambda: one(1), lambda: first(0), lambda: first(1)] + [
                lambda s=s, k=k: tap(s, k) for s in range(2) for k in (1, 2, 3)]

        def prep(b, g, c4):
            XC, tcx = XCs[g % 2], S_["xc", b, g]
            gg, ct = g % 4, 2 + g // 4
            o = slice(b * 1024 + c4 * 512, b * 1024 + c4 * 512 + 512)
            w5 = slice(c4 * 512, c4 * 512 + 512)
            out = []

            def load():
                q = slice(32 * gg, 32 * gg + 32)
                for r in range(4):
                    S_["crep"] = self.dma("crep%d" % c4, Crep[32 * r:32 * r + 32, w5], BC[q, ct, w5], S_["bc"],
                                          last.get(("crep", c4)))
                if c4 == 0:
                    gi, sg, gf = sel.take()
                    S_["sg"] = (gi, sg, pool(lambda e: e.tensor_copy(sg.rearrange("p (a b) -> p a b", a=4),
                        self.ident[:, 32 + 4 * g:36 + 4 * g].unsqueeze(2).broadcast_to([128, 4, 32])), gf))

            def scan(h):
                bi, bp, bf = bR.take()
                hh = 4 * g + h
                t = pe(lambda e: e.matmul(bp, self.ident[:, hh:hh + 1].broadcast_to([128, 128]), R[:, o], start=True,
                                          stop=True), bf)
                tl = dve(lambda e: e.tensor_tensor_scan(LT[:, h, c4 * 4:c4 * 4 + 4, :].rearrange("p a b -> p (a b)"),
                         bp, ident4, 0.0, ALU.mult, ALU.add), t, last.get(("main", c4)))
                bR.done(bi, tl)
                S_["tl", c4] = tl

            def cp():
                gi, sg, tsg = S_["sg"]
                tc = S_["crep"]
                bi, bp, bf = bR.take()
                t = pe(lambda e: e.matmul(bp, sg, R[:, o], start=True, stop=True), tsg, bf)
                sel.done(gi, t)
                dve(lambda e: e.tensor_copy(ach[:, c4 * 4:c4 * 4 + 4], bp[:, 127:512:128]), t, last.get(("main", c4)))
                tcp = dve(lambda e: e.tensor_tensor(CP[:, w5], Crep[:, w5], bp, ALU.mult), t, tc,
                          last.get(("main", c4)))
                bR.done(bi, tcp)
                last["crep", c4] = tcp
                S_["tcp", c4] = tcp

            def xd(c):
                bi, bp, bf = bR.take()
                for s in range(2):
                    t = pe(lambda e, s=s: e.transpose(bp[:, s * 128:s * 128 + 128], XC[:, s, c * 128:c * 128 + 128],
                                                      self.ident), tcx[s], bf)
                t = dve(lambda e: e.tensor_tensor(
                    XD[:, c, :].rearrange("p (h d) -> p h d", h=4), bp[:, 0:256].rearrange("p (h d) -> p h d", h=4),
                    dt[:, b * 8 + c, 4 * g:4 * g + 4].unsqueeze(2).broadcast_to([128, 4, 64]), ALU.mult), t,
                    last.get(("main", c4)))
                bR.done(bi, t)
                S_["txd", c] = t

            out = [load]
            for k in range(4):
                out += [lambda k=k: scan(k), lambda k=k: xd(4 * c4 + k)]
            return out + [cp]

        def main(b, g, c4):
            XC = XCs[g % 2]
            bt, ct = g // 4, 2 + g // 4
            q = slice(32 * (g % 4), 32 * (g % 4) + 32)
            L = {}

            def begin():
                L["y"] = [yR.take(), yR.take()]
                if c4 == 0:
                    S_["h"] = None

            def one(c):
                o = slice(c * 128, c * 128 + 128)
                di, bd, df = Bd.take()
                tl, tbt = S_["tl", c4], S_["bt"]
                tbd = dve(lambda e: e.tensor_tensor(bd, BT[:, c, 32 * g:32 * g + 32].unsqueeze(1).broadcast_to(
                    [128, 4, 32]), LT[:, :, c, 127:128].broadcast_to([128, 4, 32]), ALU.mult), tl, tbt, df)
                bi, bp, bf = bR.take()
                t = pe(lambda e: e.matmul(bp[:, 0:128], BC[q, bt, o], BC[q, ct, o], start=True, stop=True), bf,
                       S_["bc"])
                tm = dve(lambda e: e.tensor_tensor(LT[:, :, c, :], LT[:, :, c, :],
                         bp[:, 0:128].unsqueeze(1).broadcast_to([128, 4, 128]), ALU.mult), t, tbd)
                bR.done(bi, tm)
                L["tm", c] = tm
                if c < 7:
                    si, sp_, sf = sR.take()
                    for h in range(4):
                        tS = pe(lambda e, h=h: e.matmul(sp_[32 * h:32 * h + 32, :], bd[:, h, :],
                                XD[:, c, h * 64:h * 64 + 64], start=True, stop=True), tbd, S_["txd", c], sf,
                                mark=(h == 3))
                    Bd.done(di, tS)
                    L["s", c] = (si, sp_, tS)
                else:
                    Bd.done(di, tbd)

            def two(c):
                o = slice(c * 128, c * 128 + 128)
                w = slice((c % 4) * 128, (c % 4) * 128 + 128)
                hcur, tm, tcp = S_["h"], L["tm", c], S_["tcp", c4]
                for s in range(2):
                    y, yf = L["y"][s][1], L["y"][s][2]
                    if c > 0:
                        pe(lambda e, s=s, y=y: e.matmul(y[:, w], hcur[0][:, s * 128:s * 128 + 128], CP[:, o],
                           start=True, stop=True, skip_group_check=True), hcur[1], tcp, yf, mark=False)
                    for k in range(2):
                        h = 2 * s + k
                        t = pe(lambda e, h=h, k=k, y=y: e.matmul(y[64 * k:64 * k + 64, w],
                               XD[:, c, h * 64:h * 64 + 64], LT[:, h, c, :], start=(c == 0), stop=True,
                               skip_group_check=True), tm, S_["txd", c], yf, mark=(h == 3))
                if hcur:
                    Hb.done(hcur[2], t)
                if c < 7:
                    si, sp_, tS = L["s", c]
                    hi, hn, hf = Hb.take()
                    for h in range(4):
                        qq, cc = slice(32 * h, 32 * h + 32), slice(64 * h, 64 * h + 64)
                        if c == 0:
                            th = dve(lambda e, qq=qq, cc=cc: e.tensor_copy(hn[qq, cc], sp_[qq, :]), tS, hf)
                        else:
                            th = dve(lambda e, qq=qq, cc=cc: e.scalar_tensor_tensor(hn[qq, cc], hcur[0][qq, cc],
                                     ach[qq, c:c + 1], sp_[qq, :], ALU.mult, ALU.add), tS, hf, hcur[1])
                    sR.done(si, th)
                    S_["h"] = (hn, th, hi)
                L["t"] = last["main", c4] = t

            def gate(s):
                tile = 2 * g + s
                tok = slice(b * 1024 + c4 * 512, b * 1024 + c4 * 512 + 512)
                ai, p, af = aR.take()
                tz = self.proj(p, lambda k: Win[:, k, tile * 128:tile * 128 + 128], lambda k: XNT[:, k, tok], 512, 2,
                               af)
                zi, z, zf = Zr.take()
                tz = act(lambda e: e.activation(z, p, ACT.Silu, scale=mup[:, tile:tile + 1], bias=bm[:, tile:tile + 1]),
                         tz, zf)
                aR.done(ai, tz)
                L["z", s] = (zi, z, tz)

            def end(s):
                w5 = slice(c4 * 512, c4 * 512 + 512)
                tile = 2 * g + s
                zi, z, tz = L["z", s]
                yi, y, _ = L["y"][s]
                t1 = dve(lambda e: e.scalar_tensor_tensor(Y[:, s, w5], XC[:, s, w5], Dv[:, tile:tile + 1], y, ALU.mult,
                                                          ALU.add), L["t"], last.get(("y", c4)))
                yR.done(yi, t1)
                t2 = dve(lambda e: e.tensor_tensor(Y[:, s, w5], Y[:, s, w5], z, ALU.mult), t1, tz)
                Zr.done(zi, t2)
                S_["fin", c4, s] = t2
                last["xc", g % 2] = t1
                if (b, g, c4, s) == (1, 6, 1, 1):
                    self.dma("w_f", W12, I["l2_w12"], t1)

            k = 4 * c4
            return [begin, lambda: one(k), lambda: gate(0), lambda: one(k + 1), lambda: two(k), lambda: gate(1),
                    lambda: one(k + 2), lambda: two(k + 1), lambda: one(k + 3), lambda: two(k + 2), lambda: two(k + 3),
                    lambda: end(0), lambda: end(1)]

        def final(b, g, c4):
            w5 = slice(c4 * 512, c4 * 512 + 512)
            L = {}

            def square(s):
                qi, sq, qf = sqR.take()
                L["q", s] = (qi, sq, act(lambda e: e.activation(sq, Y[:, s, w5], ACT.Square), S_["fin", c4, s], qf))

            def var():
                ai, p, af = aR.take()
                for i in range(4):
                    for s in range(2):
                        qi, sq, tq = L["q", s]
                        t = pe(lambda e, i=i, s=s, sq=sq: e.matmul(p[:, 2 * i:2 * i + 2],
                               sq[:, i * 128:i * 128 + 128], self.ones[:, 0:2], start=(s == 0), stop=(s == 1)), tq, af)
                for s in range(2):
                    sqR.done(L["q", s][0], t)
                ri, r, rf = rsR.take()
                t = dve(lambda e: e.tensor_scalar(r, p[:, 0:8], 1.0 / 256.0, 1e-5, ALU.mult, ALU.add), t, rf)
                aR.done(ai, t)
                t = pool(lambda e: e.tensor_tensor(r, r, self.mhalf, ALU.pow), t)
                L["r"] = (ri, r, t)

            def out(i):
                ri, r, tr = L["r"]
                ai, p, af = aR.take()
                ty = [S_["fin", c4, 0], S_["fin", c4, 1]]
                for j in range(2):
                    c = c4 * 512 + (i + j) * 128
                    t = self.proj(p[:, j * 256:j * 256 + 256], lambda k: Y[:, k, c:c + 128],
                                  lambda k: Wout[:, 2 * g + k, :], 256, 2, af, ty)
                for j in range(2):
                    x = X[:, b * 8 + c4 * 4 + i + j, :]
                    t2 = dve(lambda e, x=x, j=j: e.scalar_tensor_tensor(x, p[:, j * 256:j * 256 + 256],
                             r[:, 2 * (i + j):2 * (i + j) + 1], x, ALU.mult, ALU.add), t, tr)
                aR.done(ai, t2)
                last["y", c4] = t
                if i == 2:
                    rsR.done(ri, t2)

            return [lambda: square(0), lambda: square(1), var, lambda: out(0), lambda: out(2)]

        halves = [(b, g, c4) for b in range(2) for g in range(8) for c4 in range(2)]
        for n, (b, g, c4) in enumerate(halves):
            if (g, c4) == (0, 0):
                last["bc"] = [last.get(k) for k in (("main", 1), ("crep", 0), ("crep", 1))]
                conv_bc(b)
                if b == 0:
                    merge((conv_x(b, g), 1))
                merge((prep(b, g, 0), 1))
            nxt = halves[n + 1] if n + 1 < len(halves) else None
            lists = [(main(b, g, c4), 1)]
            if nxt and nxt != (1, 0, 0):
                lists.append((prep(*nxt), 1))
            if c4 == 0 and n + 2 < len(halves):
                lists.append((conv_x(*halves[n + 2][:2]), 0.7))
            if n:
                lists.append((final(*halves[n - 1]), 1))
            merge(*lists[::-1])
        merge((final(*halves[-1]), 1))
        self.barrier()
        XH, XL = self.sbr(R0, 2, 2048), self.sbr(R0 + 4096, 2, 2048)
        Q12 = self.sbr(R0 + 8192, 2, 1408)
        Q3 = self.sbr(R0 + 11008, 6, 256)
        st = self.sb(WA0, 8)
        tmp = self.sb(WA0 + 512, 1408)
        ps = Ring([self.PS[:, i, :] for i in (0, 1)])
        tf = self.dma("w_f", W3, I["l2_w3"])
        for tt in range(4):
            for k in range(2):
                tok = slice(tt * 512, tt * 512 + 512)
                t = act(lambda e, k=k, tok=tok: e.activation(XH[:, k, tok], XNT[:, k, tok], ACT.Copy))
                pool(lambda e, k=k, tok=tok: e.tensor_tensor(XL[:, k, tok], XNT[:, k, tok], XH[:, k, tok],
                                                             ALU.subtract), t)
        dve.wait([tf])
        for n, (w, q) in enumerate(((W12[:, :, 0:704], Q12[:, :, 0:704]), (W12[:, :, 704:1408], Q12[:, :, 704:1408]),
                                    (W3, Q3))):
            t = dve(lambda e, n=n, w=w: e.tensor_reduce(st[:, n:n + 1], w, AX.XY, ALU.add, apply_absolute_value=True))
            pi, p, pf = ps.take()
            t = pe(lambda e, n=n, p=p: e.matmul(p[:, 0:1], self.ones, st[:, n:n + 1], start=True, stop=True), t, pf)
            t = dve(lambda e, p=p: e.tensor_scalar(st[:, 3:4], p[:, 0:1], 1.0 / 180224.0, 1e-8, ALU.mult, ALU.add), t)
            ps.done(pi, t)
            t1 = dve(lambda e: e.tensor_scalar(st[:, 4:5], st[:, 3:4], 0.5, None, ALU.mult), t)
            t2 = dve(lambda e: e.tensor_scalar(st[:, 5:6], st[:, 3:4], -0.5, None, ALU.mult), t)
            tm = tmp[:, 0:1408] if n < 2 else self.sb(WA0 + 512, 1536)
            tm = tm.rearrange("p (a b) -> p a b", a=6 if n == 2 else 2)
            t = dve(lambda e, w=w, tm=tm: e.tensor_scalar(tm, w, st[:, 5:6], None, ALU.is_lt), t1, t2)
            t = dve(lambda e, w=w, q=q, tm=tm: e.scalar_tensor_tensor(q, w, st[:, 4:5], tm, ALU.is_gt, ALU.subtract),
                    t)
        self.barrier()
        r = lambda f: 64 if f == 5 else 128
        self.ffn_ternary(X, (XH, XL), 6, Q12, Q3, r, WA0)
        self.barrier()

    def ffn_ternary(self, X, XP, nf, Q12, Q3, rows, work):
        act, dve, pool = self.act, self.dve, self.pool
        g_r = Ring([self.PS[:, i, :] for i in (0, 1)])
        u_r = Ring([self.PS[:, i, :] for i in (2, 3)])
        d_r = Ring([self.PS[:, i, :] for i in (4, 5, 6, 7)])
        tmp = Ring([self.sb(work + 512 * i, 512) for i in range(3)])
        prod = Ring([self.sb(work + 1536 + 512 * i, 512) for i in range(3)])
        H = Ring([self.sbr(R0 + 12544 + 1024 * nf * i, 2, nf, 512) for i in range(2)])
        half = Q12.shape[2] // 2

        def up(tt):
            hi, h, hf = H.take()
            tok = slice(tt * 512, tt * 512 + 512)
            td = []
            for f in range(nf):
                r = rows(f)
                gi, g, gf = g_r.take()
                ui, u, uf = u_r.take()
                x = lambda k: XP[k % 2][:, k // 2, tok]
                tg = self.proj(g[:r, :], lambda k: Q12[:, k // 2, f * 128:f * 128 + r], x, 512, 4, gf)
                tu = self.proj(u[:r, :], lambda k: Q12[:, k // 2, half + f * 128:half + f * 128 + r], x, 512, 4, uf)
                ti, s, sf = tmp.take()
                pi, p, pf = prod.take()
                ta = act(lambda e, s=s, g=g, r=r: e.activation(s[:r, :], g[:r, :], ACT.Sigmoid), tg, sf)
                g_r.done(gi, ta)
                t = dve(lambda e, s=s, u=u, r=r, p=p: e.tensor_tensor(p[:r, :], s[:r, :], u[:r, :], ALU.mult),
                        ta, tu, pf)
                u_r.done(ui, t)
                tmp.done(ti, t)
                t1 = act(lambda e, p=p, r=r, f=f: e.activation(h[:r, 0, f, :], p[:r, :], ACT.Copy), t, hf)
                t2 = pool(lambda e, p=p, r=r, f=f: e.tensor_tensor(h[:r, 1, f, :], p[:r, :], h[:r, 0, f, :],
                                                                   ALU.subtract), t1, hf)
                prod.done(pi, t2)
                td = [t1, t2]
            return tt, hi, h, td

        def down(tt, hi, h, th):
            t = self.project_add(X, tt * 4, 4, d_r, lambda i, k: h[:rows(k // 2), k % 2, k // 2, i * 128:i * 128 + 128],
                                 lambda k: Q3[:rows(k // 2), k // 2, :], 2 * nf, th)
            H.done(hi, t)

        prev = None
        for tt in range(4):
            cur = up(tt)
            if prev:
                down(*prev)
            prev = cur
        down(*prev)

    def layer3(self, X, XNT):
        pe, act, dve, pool = self.pe, self.act, self.dve, self.pool
        I = self.ins
        P0 = WA0
        Wsa = self.sb(P0, 2, 64)
        Wo = self.sb(P0 + 128, 2, 256)
        bo = self.sb(P0 + 640, 256)
        Wr = self.sb(P0 + 896, 2, 16)
        XN = self.sb(P0 + 1024, 16, 256)
        QT, KT = self.sb(P0 + 5120, 1024), self.sb(P0 + 6144, 1024)
        AW = P0 + 7168
        MW = AW + 3584
        PR = self.sb(MW + 4352, 16, 2)
        idx = self.sb(MW + 4384, 2, 16)
        tcol = self.sb(MW + 4416, SLOTS)
        assert MW + 4352 + 208 == EW0
        for dst, src in ((Wsa, "l3_wsa"), (Wo, "l3_wo"), (bo, "l3_bo"), (Wr, "l3_wr")):
            tw = self.dma("w_a", dst, I[src])
        te = []

        def load(e, *tokens):
            at = EW0 + 2048 * e if e < 14 else XNT0 + 2048 * (e - 14)
            self.dma("exp", self.sbw(at, 2, 512), I["l3_w1"][:, e], *tokens)
            te[:] = [self.dma("exp", self.sbw(at + 1024, 4, 256), I["l3_w2"][:, e], *tokens)]

        self.barrier()
        for e in range(14):
            load(e)
        self.norm(X, XNT, XN, AW)
        for i in range(NT):
            pool(lambda e, i=i: e.tensor_tensor(X[:, i, :], X[:, i, :], bo, ALU.add), tw, dve.last())
        self.barrier()
        s_r = Banks(self.PS[:, 0:4, :].rearrange("p a b -> p (a b)"), 4)
        t_r = Ring([self.PS[:, i, :] for i in (4, 5, 6)])
        o_r = Ring([self.PS[:, 7, :]])
        w3 = [128, 16, 16]
        LG, O1, O2, pre, cnt, cmp_ = (self.sb(MW + 256 * i, 16, 16) for i in range(6))
        base = self.sb(MW + 1536, 17, 16)
        M8 = self.sb(MW + 1808, 16, 8)
        I8 = self.sb(MW + 1936, 16, 8)
        IF = self.sb(MW + 2064, 16, 2)
        io = self.sb(MW + 2096, 16)
        io128 = self.sb(MW + 2112, 16)
        io47 = self.sb(MW + 2128, SLOTS)
        upper = self.sb(MW + 2176, 128)
        ne, inc, st0 = (self.sb(MW + 2304 + 16 * i, 16) for i in range(3))
        fidx = self.sb(MW + 2352, 2, 16)
        ft, ft2 = self.sb(MW + 2384, SLOTS), self.sb(MW + 2432, SLOTS)
        big = self.sb(MW + 2480, SLOTS, 16)
        for dst, m, n in ((io, 1, 16), (io128, 128, 16), (io47, 1, SLOTS)):
            pool(lambda e, dst=dst, m=m, n=n: e.iota(dst, pattern=[[m, n]], base=0, channel_multiplier=0,
                                                     allow_small_or_imprecise_dtypes=True))
        t = pool(lambda e: e.memset(upper, 1.0))
        tio = pool(lambda e: e.affine_select(out=upper, in_=upper, compare_op=ALU.is_ge, fill=0.0, base=-1,
                                             pattern=[[1, 128]], channel_multiplier=-1), t)
        oi, o, of = o_r.take()
        for i in range(NT):
            t = self.proj(o[:, i * 16:i * 16 + 16], lambda k: XNT[:, k, i * 128:i * 128 + 128], lambda k: Wr[:, k, :],
                          16, 2, of, tw)
        t = dve(lambda e, o=o: e.tensor_copy(LG, o[:, 0:256].rearrange("p (a b) -> p a b", a=16)), t)
        o_r.done(oi, t)
        for i in range(NT):
            t1 = dve(lambda e, i=i: e.max(M8[:, i, :], LG[:, i, :]), t)
            t2 = dve(lambda e, i=i: e.max_index(I8[:, i, :].bitcast(U32), M8[:, i, :], LG[:, i, :]), t1)
        ti = dve(lambda e: e.tensor_copy(IF, I8[:, :, 0:2].bitcast(U32)), t2)
        iob = io.unsqueeze(1).broadcast_to(w3)
        for n, c in enumerate((O1, O2)):
            t = dve(lambda e, n=n, c=c: e.tensor_tensor(c, iob, IF[:, :, n:n + 1].broadcast_to(w3), ALU.is_equal),
                    ti, tio)
        tO = dve(lambda e: e.tensor_tensor(LG, O1, O2, ALU.add), t)
        both = LG.rearrange("p a b -> p (a b)")
        oi, o, of = o_r.take()
        t = pe(lambda e, o=o: e.matmul(o[:, 0:256], upper, both, start=True, stop=True), tO, tio, of)
        t = pe(lambda e, o=o: e.matmul(o[:, 256:512], self.ones, both, start=True, stop=True))
        t = dve(lambda e, o=o: e.tensor_copy(pre, o[:, 0:256].rearrange("p (a b) -> p a b", a=16)), t)
        t = dve(lambda e, o=o: e.tensor_copy(cnt, o[:, 256:512].rearrange("p (a b) -> p a b", a=16)), t)
        o_r.done(oi, t)
        t = dve(lambda e: e.memset(base[:, 0, :], 0.0), t)
        for i in range(NT):
            t = dve(lambda e, i=i: e.tensor_tensor(base[:, i + 1, :], base[:, i, :], cnt[:, i, :], ALU.add), t)
        t = dve(lambda e: e.tensor_tensor(cmp_, base[:, 16, :].unsqueeze(2).broadcast_to(w3),
                                          io128.unsqueeze(1).broadcast_to(w3), ALU.is_gt), t)
        t = dve(lambda e: e.tensor_reduce(ne, cmp_, AX.X, ALU.add), t)
        t = dve(lambda e: e.tensor_tensor_scan(inc, self.ones[:, 0:16], ne, 0.0, ALU.mult, ALU.add), t)
        tn = t
        t = dve(lambda e: e.tensor_tensor(st0, inc, ne, ALU.subtract), t)
        t = dve(lambda e: e.tensor_scalar(st0, st0, 128.0, None, ALU.mult), t)
        t = dve(lambda e: e.tensor_tensor(pre, pre, base[:, 0:16, :], ALU.add), t)
        t = dve(lambda e: e.tensor_tensor(pre, pre, st0.unsqueeze(1).broadcast_to(w3), ALU.add), t)
        for n, c in enumerate((O1, O2)):
            t2 = dve(lambda e, c=c: e.tensor_tensor(c, c, pre, ALU.mult), t)
            t2 = dve(lambda e, n=n, c=c: e.tensor_reduce(fidx[:, n, :], c, AX.X, ALU.add), t2)
        tidx = dve(lambda e: e.tensor_copy(idx.bitcast(U32), fidx), t2)
        w47 = [128, SLOTS, 16]
        t = dve(lambda e: e.tensor_tensor(big, io47.unsqueeze(2).broadcast_to(w47),
                                          inc.unsqueeze(1).broadcast_to(w47), ALU.is_ge), tn)
        t = dve(lambda e: e.tensor_reduce(ft, big, AX.X, ALU.add), t)
        t = dve(lambda e: e.tensor_scalar(ft, ft, 15.0, None, ALU.min), t)
        t = dve(lambda e: e.tensor_scalar(ft2, ft, 13.5, float(XNT0 - EW0 - 28672), ALU.is_ge, ALU.mult), t)
        t = dve(lambda e: e.tensor_scalar(ft, ft, 2048.0, float(EW0), ALU.mult, ALU.add), t)
        t = dve(lambda e: e.tensor_tensor(ft, ft, ft2, ALU.add), t)
        tcl = dve(lambda e: e.tensor_copy(tcol.bitcast(I32), ft), t)
        t = dve(lambda e: e.tensor_tensor(PR[:, :, 1], M8[:, :, 1], M8[:, :, 0], ALU.subtract), t1)
        tx = act(lambda e: e.activation(PR[:, :, 1], PR[:, :, 1], ACT.Exp), t)
        t = dve(lambda e: e.tensor_scalar(PR[:, :, 0], PR[:, :, 1], 1.0, None, ALU.add), tx)
        t = dve(lambda e: e.reciprocal(PR[:, :, 0], PR[:, :, 0]), t)
        tp = dve(lambda e: e.tensor_tensor(PR[:, :, 1], PR[:, :, 1], PR[:, :, 0], ALU.mult), t)
        row = lambda n, i: bass.IndirectOffsetOnAxis(ap=idx[:, n, i:i + 1].bitcast(U32), axis=0)
        for i in range(NT):
            for n in range(2):
                tsc = self.indirect("scatter", self.xg, row(n, i), XN[:, i, :], None, tidx, self.tclear)
        tq = []
        for tt in range(4):
            si, s, sf = s_r.take()
            k5 = slice(tt * 512, tt * 512 + 512)
            t = self.proj(s[0:64, 0:512], lambda k: Wsa[:, k, :], lambda k: XNT[:, k, k5], 512, 2, sf)
            r = slice(32 * (tt // 2), 32 * (tt // 2) + 32)
            kb = slice((tt % 2) * 512, (tt % 2) * 512 + 512)
            t1 = act(lambda e, s=s, r=r, kb=kb: e.activation(QT[r, kb], s[0:32, 0:512], ACT.Copy), t)
            t2 = act(lambda e, s=s, r=r, kb=kb: e.activation(KT[r, kb], s[32:64, 0:512], ACT.Copy,
                                                             scale=float(np.float32(1.0 / np.sqrt(32)))), t)
            s_r.done(si, t2)
            tq.append(t2)
        load(14, t)
        load(15, t)
        nb = Ring([self.sb(AW + 2560 + 512 * i, 512) for i in range(2)])
        YT = self.sb(R0, 2, 16, 256)
        cur = {}
        tg = {}

        def combine(i):
            t = None
            for n in range(2):
                t = dve(lambda e, n=n: e.scalar_tensor_tensor(X[:, i, :], YT[:, n, i, :], PR[:, i, n:n + 1],
                                                              X[:, i, :], ALU.mult, ALU.add), tg[i // 4], t, tp)

        def score(u, h):
            b, qt = u
            r = slice(32 * b, 32 * b + 32)
            return QT[r, qt * 128:qt * 128 + 128], lambda c0, c1: KT[r, c0:c1], tq

        def pv(u, j, PT, t2):
            b, qt = u
            if j == 0:
                cur["o"] = o_r.take()
            oi, o, of = cur["o"]
            t = pe(lambda e: e.matmul(o[:, 0:256], PT, XN[:, b * 8 + j, :], start=(j == 0), stop=(j == qt)), t2, of)
            if j == qt:
                st = self.sb(self.misc + (qt % 2) * 32, 4, 8)
                ni, n, nf = nb.take()
                tr = dve(lambda e: e.reciprocal(st[:, 2, 0:1], st[:, 1, 0:1]), t)
                ta = dve(lambda e: e.tensor_scalar(n[:, 0:256], o[:, 0:256], st[:, 2, 0:1], None, ALU.mult), tr, nf)
                o_r.done(oi, ta)
                oi, o, of = o_r.take()
                for c in range(2):
                    tb = pe(lambda e, c=c, o=o: e.transpose(o[:, c * 128:c * 128 + 128], n[:, c * 128:c * 128 + 128],
                                                            self.ident), ta, of)
                tc = act(lambda e, o=o: e.activation(n[:, 256:512], o[:, 0:256], ACT.Copy), tb)
                o_r.done(oi, tc)
                oi, o, of = o_r.take()
                td = self.proj(o[:, 0:256], lambda k: n[:, 256 + k * 128:384 + k * 128], lambda k: Wo[:, k, :], 256, 2,
                               of, tc)
                nb.done(ni, td)
                x = X[:, b * 8 + qt, :]
                tf = dve(lambda e, o=o: e.tensor_tensor(x, x, o[:, 0:256], ALU.add), td)
                o_r.done(oi, tf)
                if b == 1 and qt >= 4:
                    for i in range(4 * qt - 16, 4 * qt - 12):
                        combine(i)
            return t

        self.attend([(0, qt) for qt in range(8)], 1, AW, score, 1.0, None, pv, (s_r, t_r), 4)
        self.barrier()
        ty = self.experts(MW, tcol, [tcl, te], tsc)
        self.barrier()
        for i in range(NT):
            for n in range(2):
                tg[i // 4] = self.indirect(f"gather{i // 4}", YT[:, n, i, :], None, self.yg, row(n, i), ty)
        self.attend([(1, qt) for qt in range(8)], 1, AW, score, 1.0, None, pv, (s_r, t_r), 4)

    def indirect(self, name, out, oo, in_, io, *tokens):
        if name not in self.dsem:
            self.dsem[name] = [self.mk("d_" + name), 0]
        s = self.dsem[name]
        s[1] += 16
        self.pool(lambda e, sem=s[0]: e.indirect_dma_start(out, oo, in_, io).then_inc(sem, 16), *tokens, mark=False)
        return (s[0], s[1])

    def clear(self):
        zero = self.sb(CONST0 + 784, 128)
        t = self.pool(lambda e: e.memset(zero, 0.0))
        n = SLOTS * 2
        return self.dma("clear", self.xg.rearrange("(p a) (b c) -> p (a b) c", p=128, c=128),
                        zero.unsqueeze(1).broadcast_to([128, n, 128]), t)

    def experts(self, at, tcol, tw, tsc):
        pe, act, dve = self.pe, self.act, self.dve
        G = Ring([self.sb(at + 256 * i, 256) for i in range(3)])
        XT = Ring([self.sbw(at + 768 + 256 * i, 256) for i in range(3)])
        H = Ring([self.sb(at + 1536 + 512 * i, 512) for i in range(2)])
        HT = Ring([self.sbw(at + 2560 + 512 * i, 512) for i in range(2)])
        Y = Ring([self.sb(at + 3584 + 256 * i, 256) for i in range(3)])
        x_r, g_r, h_r, y_r = (Ring([self.PS[:, i, :] for i in (j, j + 1)]) for j in (0, 2, 4, 6))
        tiles = [{} for _ in range(SLOTS)]
        col = {}
        out = [None] * 3

        def fetch(s):
            d = tiles[s]
            d["gi"], d["g"], free = G.take()
            d["tg"] = self.dma(f"xg{d['gi']}", d["g"], self.xg[s * 128:s * 128 + 128, :], tsc, free)

        def turn_x(s):
            d = tiles[s]
            pi, p, pf = x_r.take()
            for k in range(2):
                t = pe(lambda e, k=k: e.transpose(p[:, k * 128:k * 128 + 128], d["g"][:, k * 128:k * 128 + 128],
                                                  self.ident), d["tg"], pf, mark=(k == 1))
            G.done(d["gi"], t)
            d["xi"], d["xt"], free = XT.take()
            d["tx"] = dve(lambda e: e.tensor_copy(d["xt"], p[:, 0:256]), t, free)
            x_r.done(pi, d["tx"])
            if s + 3 < SLOTS:
                fetch(s + 3)

        def pick(e, s):
            col[s] = e.value_load(tcol[0:1, s:s + 1].bitcast(I32), min_val=XNT0, max_val=EW0 + 13 * 2048)

        def up(s):
            d = tiles[s]
            pi, p, pf = g_r.take()
            pe(lambda e: pick(e, s), tw, mark=False)
            for k in range(2):
                t = pe(lambda e, k=k: e.matmul(p, d["xt"][:, k * 128:k * 128 + 128],
                                               self.whole[:, bass.ds(col[s] + k * 512, 512)], start=(k == 0),
                                               stop=(k == 1)), d["tx"], pf, mark=(k == 1))
            XT.done(d["xi"], t)
            d["hi"], d["h"], free = H.take()
            d["th"] = act(lambda e: e.activation(d["h"], p, ACT.Silu), t, free)
            g_r.done(pi, d["th"])

        def turn_h(s):
            d = tiles[s]
            pi, p, pf = h_r.take()
            for k in range(4):
                t = pe(lambda e, k=k: e.transpose(p[:, k * 128:k * 128 + 128], d["h"][:, k * 128:k * 128 + 128],
                                                  self.ident), d["th"], pf, mark=(k == 3))
            H.done(d["hi"], t)
            d["ti"], d["ht"], free = HT.take()
            d["tt"] = dve(lambda e: e.tensor_copy(d["ht"], p), t, free)
            h_r.done(pi, d["tt"])

        def down(s):
            d = tiles[s]
            pi, p, pf = y_r.take()
            for k in range(4):
                t = pe(lambda e, k=k: e.matmul(p[:, 0:256], d["ht"][:, k * 128:k * 128 + 128],
                                               self.whole[:, bass.ds(col[s] + 1024 + k * 256, 256)], start=(k == 0),
                                               stop=(k == 3)), d["tt"], pf, mark=(k == 3))
            HT.done(d["ti"], t)
            yi, y, free = Y.take()
            t = act(lambda e: e.activation(y, p[:, 0:256], ACT.Copy), t, free)
            y_r.done(pi, t)
            out[yi] = self.dma(f"yg{yi}", self.yg[s * 128:s * 128 + 128, :], y, t)
            Y.done(yi, out[yi])

        for s in range(3):
            fetch(s)
        for n in range(-2, SLOTS + 1):
            if n + 2 < SLOTS:
                turn_x(n + 2)
            if 0 <= n + 1 < SLOTS:
                up(n + 1)
            if 0 <= n < SLOTS:
                turn_h(n)
            if n >= 1:
                down(n - 1)
        return out


def build(nc, ins, outs, first=0, layers=4):
    with ExitStack() as ctx:
        k = Net(nc, ctx, ins, outs)
        block = ctx.enter_context(nc.Block())
        X = k.sb(X0, 16, 256)
        XNT = k.sb(XNT0, 2, 2048)
        tx = k.dma("x", X, ins["x"])
        k.consts()
        k.dve.wait([tx])
        for n in range(first, layers):
            if n == max(first, 1):
                k.tclear = k.clear()
            (k.layer0, k.layer1, k.layer2, k.layer3)[n](X, XNT)
        k.barrier()
        to = k.dma("out", outs["out"], X)
        k.sp.wait([to])

        @block.sync
        def _(e):
            for f in k.sp.queue:
                f(e)

        @block.tensor
        def _(e):
            for f in k.pe.queue:
                f(e)

        @block.scalar
        def _(e):
            for f in k.act.queue:
                f(e)

        @block.vector
        def _(e):
            for f in k.dve.queue:
                f(e)

        @block.gpsimd
        def _(e):
            for f in k.pool.queue:
                f(e)


def kmajor(w):
    k, n = w.shape
    return np.ascontiguousarray(w.reshape(k // 128, 128, n).transpose(1, 0, 2))


def rope(n, d):
    inv = (np.float32(1.0) / np.power(np.float32(10000.0), np.arange(d // 2, dtype=np.float32) / np.float32(d // 2)))
    ang = np.arange(n, dtype=np.float32)[:, None] * inv.astype(np.float32)[None, :]
    return np.cos(ang).T.astype(np.float32), np.sin(ang).T.astype(np.float32)


def layout(i):
    a = {}
    a["x"] = np.ascontiguousarray(i["L0_attn_x"].reshape(16, 128, 256).transpose(1, 0, 2))
    h = np.arange(16)[:, None] * 16
    lo, hi = np.arange(8), np.arange(8, 16)
    iq = (h + np.concatenate([lo, hi, hi, lo])[None]).ravel()
    ia = (h + np.concatenate([lo, hi, lo, hi])[None]).ravel()
    ib = (h + np.concatenate([hi, lo, hi, lo])[None]).ravel()
    a["l0_wq"] = kmajor(i["L0_attn_Wq"].T[:, iq])
    a["l0_wa"] = kmajor(i["L0_attn_Wk"].T[:, ia])
    a["l0_wb"] = kmajor(i["L0_attn_Wk"].T[:, ib])
    a["l0_wv"] = kmajor(i["L0_attn_Wv"].T)
    wo = np.zeros((16, 32, 256), np.float32)
    wo[:, :16, :] = i["L0_attn_Wo"].T.reshape(16, 16, 256)
    a["l0_wo"] = kmajor(wo.reshape(512, 256))
    c, s = rope(1024, 16)
    q = np.float32(0.25)
    a["l0_tq"] = np.tile(np.concatenate([c, c, -s, s]) * q, (4, 1))
    a["l0_tc"] = np.tile(np.concatenate([c, c, c, c]), (4, 1))
    a["l0_ts"] = np.tile(np.concatenate([-s, s, -s, s]), (4, 1))
    a["l0_wgu"] = kmajor(i["L0_ffn_w_gate_up"].T)
    a["l0_wd"] = kmajor(i["L0_ffn_w_down"].T)
    a["l1_wq"] = kmajor(i["L1_attn_Wq"].T)
    a["l1_wk"] = kmajor(i["L1_attn_Wk"].T)
    a["l1_wv"] = kmajor(i["L1_attn_Wv"].T)
    a["l1_wo"] = kmajor(i["L1_attn_Wo"].T)
    a["l1_wg"] = kmajor(np.concatenate([i["L1_attn_Wgslc"].T, i["L1_attn_Wgswa"].T], axis=1))
    c, s = rope(1024, 128)
    a["l1_tc"] = np.concatenate([c, c])
    a["l1_ts"] = np.concatenate([s, -s])
    a["l1_wgu"] = kmajor(np.concatenate([i["L1_ffn_w_gate"].T, i["L1_ffn_w_up"].T], axis=1))
    a["l1_wd"] = kmajor(i["L1_ffn_w_down"].T)
    a["l2_win"] = kmajor(i["L2_attn_W_in"])
    a["l2_wout"] = kmajor(i["L2_attn_W_out"])
    col = lambda v, n: v.reshape(n, 128).T
    cw = i["L2_attn_conv_w"].reshape(20, 128, 4).transpose(1, 0, 2).reshape(128, 80)
    a["l2_vec"] = np.concatenate([col(i["L2_attn_mup_vector"][:4608], 36), col(i["L2_attn_b_in"][:4608], 36), cw,
                                  col(i["L2_attn_conv_b"], 20), col(np.repeat(i["L2_attn_D_param"], 64), 16),
                                  col(i["L2_attn_norm_w"], 16)], axis=1)
    a["l2_dt"] = np.broadcast_to(np.stack([i["L2_attn_b_in"][4608:], i["L2_attn_mup_vector"][4608:],
                                           i["L2_attn_dt_bias"], i["L2_attn_A_log"]])[None], (128, 4, 32))
    a["l2_bout"] = np.broadcast_to(i["L2_attn_b_out"][None], (128, 256))
    a["l2_w12"] = kmajor(np.concatenate([i["L2_ffn_w1"].T, i["L2_ffn_w2"].T], axis=1))
    w3 = np.zeros((768, 256), np.float32)
    w3[:704] = i["L2_ffn_w3"].T
    a["l2_w3"] = kmajor(w3)
    a["l3_wsa"] = kmajor(np.concatenate([i["L3_attn_Ws"], i["L3_attn_Wa"]], axis=1))
    a["l3_wo"] = kmajor(i["L3_attn_Wo"].T)
    a["l3_bo"] = np.broadcast_to(i["L3_attn_bo"][None], (128, 256))
    a["l3_wr"] = kmajor(i["L3_ffn_router_w"])
    a["l3_w1"] = i["L3_ffn_W1"].reshape(16, 2, 128, 512).transpose(2, 0, 1, 3)
    a["l3_w2"] = i["L3_ffn_W2"].reshape(16, 4, 128, 256).transpose(2, 0, 1, 3)
    return a


def kernel(**inputs):
    import concourse.bacc as bacc
    from concourse.bass_utils import run_bass_kernel_spmd as run

    arrays = layout({k: np.asarray(v) for k, v in inputs.items()})
    arrays = {k: np.ascontiguousarray(v) for k, v in arrays.items()}
    nc = bacc.Bacc("TRN2", target_bir_lowering=False, num_devices=1)
    ins = {k: nc.dram_tensor(k, v.shape, mybir.dt.from_np(v.dtype), kind="ExternalInput").ap()
           for k, v in arrays.items()}
    outs = {"out": nc.dram_tensor("out", (128, 16, 256), F32, kind="ExternalOutput").ap()}
    build(nc, ins, outs)
    r = run(nc, [arrays], core_ids=[0]).results[0]["out"]
    return np.ascontiguousarray(r.reshape(128, 16, 256).transpose(1, 0, 2)).reshape(2, 1024, 256)
```
